# Optimizing a Trainium2 kernel written in Bass

```python
import numpy as np
import jax
import jax.numpy as jnp

def _softmax(x, axis=-1):
    return jax.nn.softmax(x, axis=axis)

def _gelu(x):
    return jax.nn.gelu(x, approximate=True)

def _silu(x):
    return jax.nn.silu(x)

def _sigmoid(x):
    return jax.nn.sigmoid(x)

def _layernorm(x, axis=-1, eps=1e-05):
    m = jnp.mean(x, axis=axis, keepdims=True)
    v = jnp.var(x, axis=axis, keepdims=True)
    return (x - m) / jnp.sqrt(v + eps)

def _scatter_add(tgt, idx, src, axis=0):
    return tgt.at[idx].add(src)

def _segment_sum(src, seg, n):
    return jax.ops.segment_sum(src, seg, n)
kernel_name = 'mk_recurrent_d4_jaxref_r8_b471c2'

def setup_inputs(seed: int=0):
    np.random.seed(seed)
    _w = jnp.asarray

    def _L0_attn_setup():
        import jax, jax.numpy as jnp
        import numpy as np
        DIM = 512
        N_HEADS = 32
        HEAD_DIM = DIM // N_HEADS
        key = jax.random.key(seed)
        k0, k1, k2, k3, k4 = jax.random.split(key, 5)
        B, T = (2, 256)
        x = jax.random.normal(k0, (B, T, DIM), dtype=jnp.float32)
        s = 1.0 / np.sqrt(DIM)
        wq = jax.random.normal(k1, (DIM, DIM), dtype=jnp.float32) * s
        wk = jax.random.normal(k2, (DIM, HEAD_DIM), dtype=jnp.float32) * s
        wv = jax.random.normal(k3, (DIM, HEAD_DIM), dtype=jnp.float32) * s
        wo = jax.random.normal(k4, (DIM, DIM), dtype=jnp.float32) * s
        return {'x': x, 'wq': wq, 'wk': wk, 'wv': wv, 'wo': wo}
    _L0_attn_in = _L0_attn_setup()

    def _L0_ffn_setup():
        import jax, jax.numpy as jnp
        import numpy as np
        TOP_K = 2
        key = jax.random.key(seed)
        k0, k1, k2 = jax.random.split(key, 3)
        B, S, D, H, E = (4, 256, 512, 512, 8)
        sc = 1.0 / np.sqrt(D).astype(np.float32)
        x = jax.random.normal(k0, (B, S, D), dtype=jnp.float32)
        W_gate = jax.random.normal(k1, (D, E), dtype=jnp.float32) * sc
        b_gate = jnp.zeros((E,), dtype=jnp.float32)
        W_e = jax.random.normal(k2, (E, D, H), dtype=jnp.float32) * sc
        b_e = jnp.zeros((E, H), dtype=jnp.float32)
        return {'x': x, 'W_gate': W_gate, 'b_gate': b_gate, 'W_e': W_e, 'b_e': b_e}
    _L0_ffn_in = _L0_ffn_setup()

    def _L1_attn_setup():
        import jax, jax.numpy as jnp
        import numpy as np
        from jax import lax
        H, KVH, D, CHUNK = (32, 8, 128, 128)
        ROPE_THETA = 10000.0
        RMS_EPS = 1e-05

        def _rope_tables(L):
            inv_freq = 1.0 / ROPE_THETA ** (jnp.arange(0, D, 2, dtype=jnp.float32) / D)
            ang = jnp.arange(L, dtype=jnp.float32)[:, None] * inv_freq
            cos = jnp.concatenate([jnp.cos(ang), jnp.cos(ang)], axis=-1)[:, None, :]
            sin = jnp.concatenate([jnp.sin(ang), jnp.sin(ang)], axis=-1)[:, None, :]
            return (cos, sin)

        def _apply_rope(x, cos, sin):
            half = D // 2
            rot = jnp.concatenate([-x[..., half:], x[..., :half]], axis=-1)
            return x * cos + rot * sin
        key = jax.random.key(seed)
        ks = jax.random.split(key, 10)
        B, L, HID = (1, 512, 512)
        s = lambda fan: 1.0 / np.sqrt(fan)
        return {'hidden_states': jax.random.normal(ks[0], (B, L, HID), jnp.float32), 'Wq': jax.random.normal(ks[1], (H * D, HID), jnp.float32) * s(HID), 'Wk': jax.random.normal(ks[2], (KVH * D, HID), jnp.float32) * s(HID), 'Wv': jax.random.normal(ks[3], (KVH * D, HID), jnp.float32) * s(HID), 'Wo': jax.random.normal(ks[4], (HID, H * D), jnp.float32) * s(H * D), 'Wg': jax.random.normal(ks[5], (H * D, HID), jnp.float32) * (s(HID) * 2 ** (-2.5)), 'Win': jax.random.normal(ks[6], (H, HID), jnp.float32) * s(HID), 'dt_bias': jnp.zeros((H,), jnp.float32), 'A_log_bias': jnp.log(jax.random.uniform(ks[7], (H,), jnp.float32, 1.0, 16.0)), 'gnorm_w': jnp.ones((D,), jnp.float32)}
    _L1_attn_in = _L1_attn_setup()

    def _L1_ffn_setup():
        import jax, jax.numpy as jnp
        import numpy as np
        NUM_EXPERTS = 4
        HIDDEN = 512
        RANK = 8
        ALPHA = 8.0
        SCALE = ALPHA / RANK
        key = jax.random.key(seed)
        ks = jax.random.split(key, 6)
        B, T, H, E, R = (4, 512, HIDDEN, NUM_EXPERTS, RANK)
        x = jax.random.normal(ks[0], (B, T, H), dtype=jnp.float32)
        W_up = jax.random.normal(ks[1], (H, H), dtype=jnp.float32) / np.sqrt(H)
        gate_w = jax.random.normal(ks[2], (E, H), dtype=jnp.float32) / np.sqrt(H)
        expert_bias = jnp.zeros((E,), dtype=jnp.float32)
        lora_A = jax.random.normal(ks[3], (E, R, H), dtype=jnp.float32) / np.sqrt(H)
        lora_B = jax.random.normal(ks[4], (E, H, R), dtype=jnp.float32) * 0.01
        return {'x': x, 'W_up': W_up, 'gate_w': gate_w, 'expert_bias': expert_bias, 'lora_A': lora_A, 'lora_B': lora_B}
    _L1_ffn_in = _L1_ffn_setup()

    def _L2_attn_setup():
        import jax, jax.numpy as jnp
        import numpy as np
        import math
        B, L, D, H = (32, 64, 512, 32)
        HD = D // H
        key = jax.random.key(seed)
        ks = jax.random.split(key, 9)
        s = 1.0 / math.sqrt(D)
        return {'x': jax.random.normal(ks[0], (B, L, D), jnp.float32), 'Wq': jax.random.normal(ks[1], (D, D), jnp.float32) * s, 'bq': jax.random.normal(ks[2], (D,), jnp.float32) * s, 'Wk': jax.random.normal(ks[3], (D, D), jnp.float32) * s, 'bk': jax.random.normal(ks[4], (D,), jnp.float32) * s, 'Wv': jax.random.normal(ks[5], (D, D), jnp.float32) * s, 'bv': jax.random.normal(ks[6], (D,), jnp.float32) * s, 'Wo': jax.random.normal(ks[7], (D, D), jnp.float32) * s, 'bo': jax.random.normal(ks[8], (D,), jnp.float32) * s}
    _L2_attn_in = _L2_attn_setup()

    def _L2_ffn_setup():
        import jax, jax.numpy as jnp
        import numpy as np
        LORA_RANK = 16
        LORA_ALPHA = 16
        LORA_SCALE = LORA_ALPHA / LORA_RANK
        key = jax.random.key(seed)
        k1, k2, k3, k4, k5 = jax.random.split(key, 5)
        B, S, D_IN, D_OUT, N_LORA, R = (8, 256, 512, 512, 3, LORA_RANK)
        std = 1.0 / np.sqrt(D_IN)
        x = jax.random.normal(k1, (B, S, D_IN), dtype=jnp.float32)
        weight = jax.random.truncated_normal(k2, -3.0, 3.0, (D_OUT, D_IN), dtype=jnp.float32) * std
        bias = jax.random.normal(k3, (D_OUT,), dtype=jnp.float32) * 0.01
        lora_A = jax.random.normal(k4, (N_LORA, R, D_IN), dtype=jnp.float32) * std
        lora_B = jax.random.normal(k5, (N_LORA, D_OUT, R), dtype=jnp.float32) * 0.02
        lora_start_indices = jnp.arange(4, dtype=jnp.int64) * 2
        return {'x': x, 'weight': weight, 'bias': bias, 'lora_A': lora_A, 'lora_B': lora_B, 'lora_start_indices': lora_start_indices}
    _L2_ffn_in = _L2_ffn_setup()

    def _L3_attn_setup():
        import jax, jax.numpy as jnp
        import numpy as np
        B, N, D = (8, 128, 512)
        H = 8
        HEAD_DIM = D // H
        E = HEAD_DIM // H
        key = jax.random.key(seed)
        ks = jax.random.split(key, 7)
        s = 0.02
        return {'x': jax.random.normal(ks[0], (B, N, D), dtype=jnp.float32), 'Wqk_w': jax.random.normal(ks[1], (2 * HEAD_DIM, D), dtype=jnp.float32) * s, 'Wqk_b': jnp.zeros((2 * HEAD_DIM,), dtype=jnp.float32), 'Wv_w': jax.random.normal(ks[2], (HEAD_DIM, D), dtype=jnp.float32) * s, 'Wv_b': jnp.zeros((HEAD_DIM,), dtype=jnp.float32), 'Wo_w': jax.random.normal(ks[3], (D, HEAD_DIM), dtype=jnp.float32) * s, 'Wo_b': jnp.zeros((D,), dtype=jnp.float32)}
    _L3_attn_in = _L3_attn_setup()

    def _L3_ffn_setup():
        import jax, jax.numpy as jnp
        import numpy as np
        import math
        P = 0.8
        key = jax.random.key(seed)
        k1, k2 = jax.random.split(key)
        B, S, IN_DIM, FEATURES = (4, 256, 512, 512)
        x = jax.random.normal(k1, (B, S, IN_DIM), dtype=jnp.float32)
        kernel = jax.random.bernoulli(k2, 0.1, (IN_DIM, FEATURES))
        scale = jnp.asarray(1.0 / math.sqrt(IN_DIM), dtype=jnp.float32)
        return {'x': x, 'kernel': kernel, 'scale': scale}
    _L3_ffn_in = _L3_ffn_setup()
    _d = {'L0_attn_x': _L0_attn_in['x'], 'L0_attn_wq': _L0_attn_in['wq'], 'L0_attn_wk': _L0_attn_in['wk'], 'L0_attn_wv': _L0_attn_in['wv'], 'L0_attn_wo': _L0_attn_in['wo'], 'L0_ffn_W_gate': _L0_ffn_in['W_gate'], 'L0_ffn_b_gate': _L0_ffn_in['b_gate'], 'L0_ffn_W_e': _L0_ffn_in['W_e'], 'L0_ffn_b_e': _L0_ffn_in['b_e'], 'L1_attn_Wq': _L1_attn_in['Wq'], 'L1_attn_Wk': _L1_attn_in['Wk'], 'L1_attn_Wv': _L1_attn_in['Wv'], 'L1_attn_Wo': _L1_attn_in['Wo'], 'L1_attn_Wg': _L1_attn_in['Wg'], 'L1_attn_Win': _L1_attn_in['Win'], 'L1_attn_dt_bias': _L1_attn_in['dt_bias'], 'L1_attn_A_log_bias': _L1_attn_in['A_log_bias'], 'L1_attn_gnorm_w': _L1_attn_in['gnorm_w'], 'L1_ffn_W_up': _L1_ffn_in['W_up'], 'L1_ffn_gate_w': _L1_ffn_in['gate_w'], 'L1_ffn_expert_bias': _L1_ffn_in['expert_bias'], 'L1_ffn_lora_A': _L1_ffn_in['lora_A'], 'L1_ffn_lora_B': _L1_ffn_in['lora_B'], 'L2_attn_Wq': _L2_attn_in['Wq'], 'L2_attn_bq': _L2_attn_in['bq'], 'L2_attn_Wk': _L2_attn_in['Wk'], 'L2_attn_bk': _L2_attn_in['bk'], 'L2_attn_Wv': _L2_attn_in['Wv'], 'L2_attn_bv': _L2_attn_in['bv'], 'L2_attn_Wo': _L2_attn_in['Wo'], 'L2_attn_bo': _L2_attn_in['bo'], 'L2_ffn_weight': _L2_ffn_in['weight'], 'L2_ffn_bias': _L2_ffn_in['bias'], 'L2_ffn_lora_A': _L2_ffn_in['lora_A'], 'L2_ffn_lora_B': _L2_ffn_in['lora_B'], 'L2_ffn_lora_start_indices': _L2_ffn_in['lora_start_indices'], 'L3_attn_Wqk_w': _L3_attn_in['Wqk_w'], 'L3_attn_Wqk_b': _L3_attn_in['Wqk_b'], 'L3_attn_Wv_w': _L3_attn_in['Wv_w'], 'L3_attn_Wv_b': _L3_attn_in['Wv_b'], 'L3_attn_Wo_w': _L3_attn_in['Wo_w'], 'L3_attn_Wo_b': _L3_attn_in['Wo_b'], 'L3_ffn_kernel': _L3_ffn_in['kernel'], 'L3_ffn_scale': _L3_ffn_in['scale']}
    _x0 = _d['L0_attn_x']
    _d['L0_attn_x'] = jax.random.normal(jax.random.fold_in(jax.random.key(seed), 1), (2, 512, 512), dtype=_x0.dtype)
    del _x0
    return _d

def reference(L0_attn_x, L0_attn_wq, L0_attn_wk, L0_attn_wv, L0_attn_wo, L0_ffn_W_gate, L0_ffn_b_gate, L0_ffn_W_e, L0_ffn_b_e, L1_attn_Wq, L1_attn_Wk, L1_attn_Wv, L1_attn_Wo, L1_attn_Wg, L1_attn_Win, L1_attn_dt_bias, L1_attn_A_log_bias, L1_attn_gnorm_w, L1_ffn_W_up, L1_ffn_gate_w, L1_ffn_expert_bias, L1_ffn_lora_A, L1_ffn_lora_B, L2_attn_Wq, L2_attn_bq, L2_attn_Wk, L2_attn_bk, L2_attn_Wv, L2_attn_bv, L2_attn_Wo, L2_attn_bo, L2_ffn_weight, L2_ffn_bias, L2_ffn_lora_A, L2_ffn_lora_B, L2_ffn_lora_start_indices, L3_attn_Wqk_w, L3_attn_Wqk_b, L3_attn_Wv_w, L3_attn_Wv_b, L3_attn_Wo_w, L3_attn_Wo_b, L3_ffn_kernel, L3_ffn_scale):

    def _L0_attn_ref(x, wq, wk, wv, wo):
        import jax, jax.numpy as jnp
        import numpy as np
        DIM = 512
        N_HEADS = 32
        HEAD_DIM = DIM // N_HEADS
        B, T, C = x.shape
        q = (x @ wq).reshape(B, T, N_HEADS, HEAD_DIM)
        k = x @ wk
        v = x @ wv
        scale = 1.0 / jnp.sqrt(jnp.asarray(HEAD_DIM, dtype=x.dtype))
        scores = jnp.einsum('bqhd,bkd->bhqk', q, k) * scale
        causal = jnp.tril(jnp.ones((T, T), dtype=bool))
        scores = jnp.where(causal[None, None], scores, -jnp.inf)
        probs = jax.nn.softmax(scores.astype(jnp.float32), axis=-1).astype(x.dtype)
        out = jnp.einsum('bhqk,bkd->bqhd', probs, v).reshape(B, T, C)
        return out @ wo

    def _L0_ffn_ref(x, W_gate, b_gate, W_e, b_e):
        import jax, jax.numpy as jnp
        import numpy as np
        TOP_K = 2
        logits = x @ W_gate + b_gate
        _, top_idx = jax.lax.top_k(logits, TOP_K)
        y_all = jax.nn.relu(jnp.einsum('bsd,edh->bseh', x, W_e) + b_e)
        y = jnp.take_along_axis(y_all, top_idx[..., None], axis=2)
        return y.mean(axis=2)

    def _L1_attn_ref(hidden_states, Wq, Wk, Wv, Wo, Wg, Win, dt_bias, A_log_bias, gnorm_w):
        import jax, jax.numpy as jnp
        import numpy as np
        from jax import lax
        H, KVH, D, CHUNK = (32, 8, 128, 128)
        ROPE_THETA = 10000.0
        RMS_EPS = 1e-05

        def _rope_tables(L):
            inv_freq = 1.0 / ROPE_THETA ** (jnp.arange(0, D, 2, dtype=jnp.float32) / D)
            ang = jnp.arange(L, dtype=jnp.float32)[:, None] * inv_freq
            cos = jnp.concatenate([jnp.cos(ang), jnp.cos(ang)], axis=-1)[:, None, :]
            sin = jnp.concatenate([jnp.sin(ang), jnp.sin(ang)], axis=-1)[:, None, :]
            return (cos, sin)

        def _apply_rope(x, cos, sin):
            half = D // 2
            rot = jnp.concatenate([-x[..., half:], x[..., :half]], axis=-1)
            return x * cos + rot * sin
        B, L, HID = hidden_states.shape
        NC = L // CHUNK
        q = (hidden_states @ Wq.T).reshape(B, L, H, D)
        k = (hidden_states @ Wk.T).reshape(B, L, KVH, D)
        v = (hidden_states @ Wv.T).reshape(B, L, KVH, D)
        cos, sin = _rope_tables(L)
        q = _apply_rope(q, cos, sin)
        k = _apply_rope(k, cos, sin)
        k = jnp.repeat(k, H // KVH, axis=2)
        v = jnp.repeat(v, H // KVH, axis=2)
        dt = jax.nn.softplus(hidden_states @ Win.T + dt_bias)
        A = -jnp.exp(A_log_bias)
        g = dt * A

        def chunked(t):
            return t.transpose(0, 2, 1, 3).reshape(B, H, NC, CHUNK, D)
        qc, kc = (chunked(q), chunked(k))
        xc = chunked(v * dt[..., None])
        gc = g.transpose(0, 2, 1).reshape(B, H, NC, CHUNK)
        G = jnp.cumsum(gc, axis=-1)
        scores = jnp.einsum('bhnid,bhnjd->bhnij', qc, kc)
        idx = jnp.arange(CHUNK)
        causal = idx[:, None] >= idx[None, :]
        decay = jnp.where(causal, jnp.exp(G[..., :, None] - G[..., None, :]), 0.0)
        y_intra = jnp.einsum('bhnij,bhnjd->bhnid', scores * decay, xc)
        Glast = G[..., -1:]
        k_dec = kc * jnp.exp(Glast - G)[..., None]
        cstates = jnp.einsum('bhnjd,bhnje->bhnde', k_dec, xc)
        chunk_decay = jnp.exp(G[..., -1])

        def step(state, inp):
            dec, cs = inp
            return (state * dec + cs, state)
        init = jnp.zeros((B, H, D, D), hidden_states.dtype)
        _, prev = lax.scan(step, init, (chunk_decay.transpose(2, 0, 1)[..., None, None], cstates.transpose(2, 0, 1, 3, 4)))
        prev = prev.transpose(1, 2, 0, 3, 4)
        y_inter = jnp.einsum('bhnid,bhnde->bhnie', qc * jnp.exp(G)[..., None], prev)
        y = (y_intra + y_inter).reshape(B, H, L, D).transpose(0, 2, 1, 3)
        rms = jnp.sqrt(jnp.mean(jnp.square(y), axis=-1, keepdims=True) + RMS_EPS)
        y = y / rms * gnorm_w
        gate = (hidden_states @ Wg.T).reshape(B, L, H, D)
        y = y * (gate * jax.nn.sigmoid(gate))
        return y.reshape(B, L, H * D) @ Wo.T

    def _L1_ffn_ref(x, W_up, gate_w, expert_bias, lora_A, lora_B):
        import jax, jax.numpy as jnp
        import numpy as np
        NUM_EXPERTS = 4
        HIDDEN = 512
        RANK = 8
        ALPHA = 8.0
        SCALE = ALPHA / RANK
        B, T, H = x.shape
        E = gate_w.shape[0]
        x_flat = x.reshape(-1, H)
        logits = x_flat @ gate_w.T + expert_bias
        top1 = jnp.argmax(logits, axis=-1)
        one_hot = jax.nn.one_hot(top1, E, dtype=x_flat.dtype)
        base_out = jnp.einsum('bth,oh->bto', x, W_up)
        z = jnp.einsum('nh,erh->ner', x_flat, lora_A)
        d = jnp.einsum('ner,ehr->neh', z, lora_B) * SCALE
        delta = jnp.einsum('neh,ne->nh', d, one_hot)
        return base_out + delta.reshape(B, T, H)

    def _L2_attn_ref(x, Wq, bq, Wk, bk, Wv, bv, Wo, bo):
        import jax, jax.numpy as jnp
        import numpy as np
        import math
        B, L, D, H = (32, 64, 512, 32)
        HD = D // H
        b, l, d = x.shape
        h, hd = (H, HD)
        q = (x @ Wq.T + bq).reshape(b, l, h, hd).transpose(0, 2, 1, 3)
        k = (x @ Wk.T + bk).reshape(b, l, h, hd).transpose(0, 2, 1, 3)
        v = (x @ Wv.T + bv).reshape(b, l, h, hd).transpose(0, 2, 1, 3)
        scores = jnp.einsum('bhqd,bhkd->bhqk', q, k) / math.sqrt(hd)
        causal = jnp.tril(jnp.ones((l, l), bool))
        scores = jnp.where(causal, scores, -jnp.inf)
        att = jax.nn.softmax(scores, axis=-1)
        out = jnp.einsum('bhqk,bhkd->bhqd', att, v)
        out = out.transpose(0, 2, 1, 3).reshape(b, l, d)
        return out @ Wo.T + bo

    def _L2_ffn_ref(x, weight, bias, lora_A, lora_B, lora_start_indices):
        import jax, jax.numpy as jnp
        import numpy as np
        LORA_RANK = 16
        LORA_ALPHA = 16
        LORA_SCALE = LORA_ALPHA / LORA_RANK
        y = jnp.einsum('bsd,od->bso', x, weight) + bias
        B = x.shape[0]
        seg = jnp.searchsorted(lora_start_indices, jnp.arange(B), side='right') - 1
        adapter_idx = jnp.clip(seg - 1, 0, lora_A.shape[0] - 1)
        A = lora_A[adapter_idx]
        Bw = lora_B[adapter_idx]
        lo = jnp.einsum('bsr,bor->bso', jnp.einsum('bsd,brd->bsr', x, A), Bw) * LORA_SCALE
        use_lora = (seg > 0)[:, None, None]
        return y + jnp.where(use_lora, lo, jnp.zeros((), dtype=y.dtype))

    def _L3_attn_ref(x, Wqk_w, Wqk_b, Wv_w, Wv_b, Wo_w, Wo_b):
        import jax, jax.numpy as jnp
        import numpy as np
        B, N, D = (8, 128, 512)
        H = 8
        HEAD_DIM = D // H
        E = HEAD_DIM // H
        b, n, _ = x.shape
        qk = (x @ Wqk_w.T + Wqk_b).reshape(b, n, H, E, 2)
        q = jnp.transpose(qk[..., 0], (0, 2, 1, 3))
        k = jnp.transpose(qk[..., 1], (0, 2, 1, 3))
        v = (x @ Wv_w.T + Wv_b).reshape(b, n, H, E)
        v = jnp.transpose(v, (0, 2, 1, 3))
        scores = jnp.einsum('bhqd,bhkd->bhqk', q, k)
        attn = jax.nn.softmax(scores, axis=-1) / jnp.asarray(HEAD_DIM ** 0.5, x.dtype)
        out = jnp.einsum('bhsl,bhlv->bhsv', attn, v)
        out = jnp.transpose(out, (0, 2, 1, 3)).reshape(b, n, H * E)
        return out @ Wo_w.T + Wo_b

    def _L3_ffn_ref(x, kernel, scale):
        import jax, jax.numpy as jnp
        import numpy as np
        import math
        P = 0.8
        in_dim = x.shape[-1]
        num_excitatory = round(in_dim * P)
        x_exc = x[..., :num_excitatory]
        x_inh = x[..., num_excitatory:]
        x_ei = jnp.concatenate([x_exc, -P / (1.0 - P) * x_inh], axis=-1)
        out = jnp.einsum('bsi,if->bsf', x_ei, kernel.astype(x_ei.dtype))
        return scale * out
    x = L0_attn_x
    xn = _layernorm(x, axis=-1)
    s = _L0_attn_ref(xn, L0_attn_wq, L0_attn_wk, L0_attn_wv, L0_attn_wo)
    g = _silu(_L0_ffn_ref(xn, L0_ffn_W_gate, L0_ffn_b_gate, L0_ffn_W_e, L0_ffn_b_e))
    x = x + s * g
    xn = _layernorm(x, axis=-1)
    s = _L1_attn_ref(xn, L1_attn_Wq, L1_attn_Wk, L1_attn_Wv, L1_attn_Wo, L1_attn_Wg, L1_attn_Win, L1_attn_dt_bias, L1_attn_A_log_bias, L1_attn_gnorm_w)
    g = _silu(_L1_ffn_ref(xn, L1_ffn_W_up, L1_ffn_gate_w, L1_ffn_expert_bias, L1_ffn_lora_A, L1_ffn_lora_B))
    x = x + s * g
    xn = _layernorm(x, axis=-1)
    s = _L2_attn_ref(xn, L2_attn_Wq, L2_attn_bq, L2_attn_Wk, L2_attn_bk, L2_attn_Wv, L2_attn_bv, L2_attn_Wo, L2_attn_bo)
    g = _silu(_L2_ffn_ref(xn, L2_ffn_weight, L2_ffn_bias, L2_ffn_lora_A, L2_ffn_lora_B, L2_ffn_lora_start_indices))
    x = x + s * g
    xn = _layernorm(x, axis=-1)
    s = _L3_attn_ref(xn, L3_attn_Wqk_w, L3_attn_Wqk_b, L3_attn_Wv_w, L3_attn_Wv_b, L3_attn_Wo_w, L3_attn_Wo_b)
    g = _silu(_L3_ffn_ref(xn, L3_ffn_kernel, L3_ffn_scale))
    x = x + s * g
    return x

_drawn_inputs = setup_inputs


def setup_inputs(seed=0):
    import zlib

    import numpy as np

    out = dict(_drawn_inputs(seed))
    spreads = {'L0_ffn_b_gate': (0.0, 0.509),
     'L0_ffn_b_e': (0.0, 0.716),
     'L1_attn_dt_bias': (0.0, 0.8),
     'L1_attn_gnorm_w': (1.0, 0.6),
     'L1_ffn_expert_bias': (0.0, 0.8),
     'L3_attn_Wqk_b': (0.0, 0.8),
     'L3_attn_Wv_b': (0.0, 0.8),
     'L3_attn_Wo_b': (0.0, 0.1)}
    factors = {'L1_ffn_gate_w': 8.0,
     'L1_ffn_lora_A': 8.0,
     'L1_ffn_lora_B': 8.0,
     'L2_attn_bq': 8.0,
     'L2_attn_bk': 64.0,
     'L2_ffn_bias': 25.021,
     'L3_attn_Wqk_w': 8.0,
     'L3_attn_Wv_w': 8.0,
     'L3_attn_Wo_w': 8.0}
    for name, (base, spread) in spreads.items():
        noise = np.random.default_rng([zlib.crc32(name.encode()), seed]).standard_normal(out[name].shape)
        drawn = base * np.exp(spread * noise) if base else spread * noise
        out[name] = jnp.asarray(drawn.astype(out[name].dtype))
    for name, factor in factors.items():
        out[name] = (out[name] * factor).astype(out[name].dtype)
    return out
```

```python
from contextlib import ExitStack

import concourse.bass as bass
from concourse import mybir

F32 = mybir.dt.float32
BF16 = mybir.dt.bfloat16
I32 = mybir.dt.int32
U32 = mybir.dt.uint32
ALU = mybir.AluOpType
ACT = mybir.ActivationFunctionType
AX = mybir.AxisListType

P = 128
B = 2
T = 512
N = B * T
NT = N // P
QT = T // P
D = 512
KC = D // P
EPS = 1e-5
NEG = -1e30
U = 8


class Core:

    def __init__(self, nc, ctx, ins):
        self.nc = nc
        self.ins = ins
        self.x = ctx.enter_context(nc.sbuf_tensor("x_sb", [P, NT, D], F32))
        self.xnT = ctx.enter_context(nc.sbuf_tensor("xnT", [P, KC, N], F32))
        self.mixed = ctx.enter_context(nc.sbuf_tensor("mixed", [P, NT, D], F32))
        self.ident = ctx.enter_context(nc.sbuf_tensor("ident", [P, P], F32))
        self.identb = ctx.enter_context(nc.sbuf_tensor("identb", [P, P], BF16))
        self.ps = ctx.enter_context(nc.psum_tensor("banks", [P, 8, 512], F32))


class Stage:

    def __init__(self, core, name):
        self.core, self.nc, self.name = core, core.nc, name
        self.ctx, self.sems = ExitStack(), []

    def __enter__(self):
        return self

    def __exit__(self, *a):
        self.ctx.close()
        if self.sems:
            self.nc.clear_and_free_semaphores(self.sems)
            self.nc.all_engine_barrier()

    def sb(self, name, shape, dt=F32):
        return self.ctx.enter_context(self.nc.sbuf_tensor(f"{self.name}_{name}", shape, dt))

    def sem(self, name):
        self.sems.append(self.nc.alloc_semaphore(f"{self.name}_{name}"))
        return self.sems[-1]

    def block(self):
        return self.ctx.enter_context(self.nc.Block())


class Chain:

    def __init__(self, eng, sem):
        self.eng, self.sem, self.n = eng, sem, 0

    def __call__(self, ins):
        self.n += 1
        ins.then_inc(self.sem, 1)
        self.eng.wait_ge(self.sem, self.n)


def load_inputs(core):
    with Stage(core, "load") as st:
        loaded, made = st.sem("loaded"), st.sem("ident_made")
        block = st.block()

        @block.sync
        def _(sp):
            sp.dma_start(core.x[:, :, :], core.ins["x"].rearrange("(t p) d -> p t d", p=P)).then_inc(loaded, 16)
            sp.dma_start(core.ident[:, :], core.ins["ident"]).then_inc(loaded, 16)

        @block.vector
        def _(dve):
            dve.wait_ge(loaded, 32)
            dve.tensor_copy(core.identb[:, :], core.ident[:, :]).then_inc(made, 1)
            dve.wait_ge(made, 1)


def layernorm(core, name):
    x, xnT, ps = core.x, core.xnT, core.ps
    with Stage(core, name) as st:
        xn = st.sb("xn", [P, NT, D])
        stats = st.sb("stats", [P, NT, 6])
        mv = st.sb("mean_var", [P, NT, 2])
        var = st.sb("var", [P, NT])
        std = st.sb("std", [P, NT])
        rstd = st.sb("rstd", [P, NT])
        step, var_ready, std_ready = st.sem("step"), st.sem("var_ready"), st.sem("std_ready")
        xn_ready, turned = st.sem("xn_ready"), st.sem("turned")
        kept_v, kept_s = st.sem("kept_v"), st.sem("kept_s")
        block = st.block()

        def keep(t):
            return xnT[:, :, t * P:(t + 1) * P], ps[:, t, :].rearrange("p (c n) -> p c n", c=KC)

        @block.vector
        def _(dve):
            chain = Chain(dve, step)
            for t in range(NT):
                last = dve.bn_stats(stats[:, t, :], x[:, t, :])
            chain(last)
            for t in range(NT):
                last = dve.bn_aggr(mv[:, t, :], stats[:, t, :])
            chain(last)
            dve.tensor_scalar(var[:, :], mv[:, :, 1], EPS, None, ALU.add).then_inc(var_ready, 1)
            dve.wait_ge(std_ready, 1)
            chain(dve.reciprocal(rstd[:, :], std[:, :]))
            for t in range(NT):
                dve.tensor_scalar(xn[:, t, :], x[:, t, :], mv[:, t, 0:1], rstd[:, t:t + 1],
                                  ALU.subtract, ALU.mult).then_inc(xn_ready, 1)
            for t in range(0, NT, 2):
                dve.wait_ge(turned, t + 1)
                dve.tensor_copy(*keep(t)).then_inc(kept_v, 1)

        @block.scalar
        def _(act):
            act.wait_ge(var_ready, 1)
            act.activation(std[:, :], var[:, :], ACT.Sqrt).then_inc(std_ready, 1)
            for t in range(1, NT, 2):
                act.wait_ge(turned, t + 1)
                act.activation(*keep(t), ACT.Copy).then_inc(kept_s, 1)

        @block.tensor
        def _(pe):
            for t in range(NT):
                pe.wait_ge(xn_ready, t + 1)
                for c in range(KC):
                    last = pe.transpose(ps[:, t, c * P:(c + 1) * P], xn[:, t, c * P:(c + 1) * P], core.ident[:, :])
                last.then_inc(turned, 1)


def attention(core, name, oT, G, E, scale, denominator, causal, shared_kv, qk_bias=None, v_bias=None):
    nc, ins, ps, xnT = core.nc, core.ins, core.ps, core.xnT
    W = E + 1
    M = U * E
    parts = 1 if causal else 2
    if causal:
        qside = [[(3, 0, 512), (2, 512, 384), (0, 896, 128), (1, 1024, 256)]]
        kside = [[(0, 0, 512), (1, 512, 384), (3, 896, 128), (2, 1024, 256)]]
    else:
        qside = kside = [[(0, 0, 512), (1, 512, 512)], [(2, 0, 512), (3, 512, 512)]]
    NU = U * parts
    STEPS = 3 + 2 * NU
    with Stage(core, name) as st:
        wq = st.sb("wq", [P, KC, P])
        wk = st.sb("wk", [P, KC, P])
        wv = st.sb("wv", [P, KC, E if shared_kv else M])
        qT = st.sb("qT", [P, T])
        kT = st.sb("kT", [P, B if shared_kv else 1, T])
        kmask = st.sb("kmask", [P, U, T])
        vaug = st.sb("vaug", [P, B if shared_kv else 1, QT, 1 if shared_kv else U, W])
        mcol = st.sb("mcol", [P, QT, P])
        mT = st.sb("mT", [P, T], BF16)
        probs = st.sb("probs", [P, 2, 1280 if causal else 2048])
        rec = st.sb("rec", [P, QT, U])
        o = st.sb("o", [P, QT, M])
        headmask = st.sb("headmask", [P, U])
        minus1 = st.sb("minus1", [P, U, P])
        minus1b = st.sb("minus1b", [P, U, P], BF16)
        masks = st.sb("masks", [P, 2, P])
        masksb = st.sb("masksb", [P, 2, P], BF16)
        qkb = st.sb("qkb", [P, 2])
        vb = st.sb("vb", [P, M])

        consts_in, consts_made = st.sem("consts_in"), st.sem("consts_made")
        w_in, w_used, w_freed = st.sem("w_in"), st.sem("w_used"), st.sem("w_freed")
        projected = st.sem("projected")
        q_kept, k_kept, v_kept = st.sem("q_kept"), st.sem("k_kept"), st.sem("v_kept")
        k_masked = st.sem("k_masked")
        rows_scored, max_taken = st.sem("rows_scored"), st.sem("max_taken")
        max_turned, max_kept = st.sem("max_turned"), st.sem("max_kept")
        cols_scored, exp_done = st.sem("cols_scored"), st.sem("exp_done")
        pv_done, rec_done, normed = st.sem("pv_done"), st.sem("rec_done"), st.sem("normed")
        o_turned, o_kept = st.sem("o_turned"), st.sem("o_kept")
        kv_projected, kv_kept = st.sem("kv_projected"), st.sem("kv_kept")
        WDMAS = (1 if shared_kv else 3) + (qk_bias is not None) + (v_bias is not None)
        block = st.block()

        def flat(step):
            first = 3 * (step % 2)
            return ps[:, first:first + 3, :].rearrange("p b n -> p (b n)")

        def weights(eng, g):
            eng.dma_start(wq[:, :, :], ins[name + "_wq"][g]).then_inc(w_in, 16)
            if not shared_kv:
                eng.dma_start(wk[:, :, :], ins[name + "_wk"][g]).then_inc(w_in, 16)
                eng.dma_start(wv[:, :, :], ins[name + "_wv"][g]).then_inc(w_in, 16)
            if qk_bias is not None:
                eng.dma_start(qkb[:, :], qk_bias[g]).then_inc(w_in, 16)
            if v_bias is not None:
                eng.dma_start(vb[:, :], v_bias[g].partition_broadcast(P)).then_inc(w_in, 16)

        @block.sync
        def _(sp):
            sp.dma_start(headmask[:, :], ins[f"headmask{E}"]).then_inc(consts_in, 16)
            sp.dma_start(minus1[:, :, :], ins["minus1"]).then_inc(consts_in, 16)
            sp.dma_start(masks[:, :, :], ins["masks"]).then_inc(consts_in, 16)
            if shared_kv:
                sp.dma_start(wk[:, :, :], ins[name + "_wk"]).then_inc(consts_in, 16)
                sp.dma_start(wv[:, :, :], ins[name + "_wv"]).then_inc(consts_in, 16)
            with sp.Fori(0, G) as g:
                sp.wait_ge(w_used, g + 1)
                sp.sem_inc(w_freed, 1)
                weights(sp, g)

        @block.gpsimd
        def _(pool):
            pool.wait_ge(consts_in, 48 + 32 * shared_kv)
            with pool.Fori(0, G) as g:
                for b in range(B):
                    r = g * B + b
                    pool.wait_ge(q_kept if shared_kv else k_kept, r + 1)
                    for u in range(U):
                        pool.tensor_tensor(kmask[:, u, :], kT[:, b if shared_kv else 0, :],
                                           headmask[:, u:u + 1].broadcast_to([P, T]), ALU.mult).then_inc(k_masked, 1)

        @block.tensor
        def _(pe):
            pe.sem_inc(w_used, 1)
            pe.wait_ge(consts_made, 4 if shared_kv else 4)
            if shared_kv:
                pe.wait_ge(consts_in, 80)
                for b in range(B):
                    for c in range(KC):
                        last = pe.matmul(ps[:, b, :], wk[:, c, :], xnT[:, c, b * T:(b + 1) * T],
                                         start=(c == 0), stop=(c == KC - 1))
                for t in range(NT):
                    for c in range(KC):
                        last = pe.matmul(ps[:, 2, t * E:(t + 1) * E], xnT[:, c, t * P:(t + 1) * P], wv[:, c, :],
                                         start=(c == 0), stop=(c == KC - 1))
                last.then_inc(kv_projected, 1)
                pe.wait_ge(kv_kept, 2)

            def freed(g, b, step):
                back = step - 2
                if back < 0:
                    back += STEPS
                    r = g * B + b - 1
                else:
                    r = g * B + b
                if back == 0:
                    pe.wait_ge(q_kept, r + 1)
                    if not shared_kv:
                        pe.wait_ge(k_kept, r + 1)
                        pe.wait_ge(v_kept, r + 1)
                elif back <= NU:
                    pe.wait_ge(max_taken, r * NU + back)
                elif back == NU + 1:
                    pe.wait_ge(max_kept, r + 1)
                elif back <= 2 * NU + 1:
                    pe.wait_ge(exp_done, r * NU + back - NU - 1 + 1)
                else:
                    pe.wait_ge(o_kept, r + 1 + 1)

            with pe.Fori(0, G) as g:
                pe.wait_ge(w_in, g * (16 * WDMAS) + 16 * WDMAS)
                for b in range(B):
                    r = g * B + b
                    step = 0
                    bank = [3 * ((b * STEPS + s) % 2) for s in range(STEPS)]
                    freed(g, b, 0)
                    for c in range(KC):
                        last = pe.matmul(ps[:, bank[0], :], wq[:, c, :], xnT[:, c, b * T:(b + 1) * T],
                                         start=(c == 0), stop=(c == KC - 1))
                    if not shared_kv:
                        for c in range(KC):
                            pe.matmul(ps[:, bank[0] + 1, :], wk[:, c, :], xnT[:, c, b * T:(b + 1) * T],
                                      start=(c == 0), stop=(c == KC - 1))
                        for i in range(QT):
                            t = b * QT + i
                            for c in range(KC):
                                last = pe.matmul(ps[:, bank[0] + 2, i * M:(i + 1) * M], xnT[:, c, t * P:(t + 1) * P],
                                                 wv[:, c, :], start=(c == 0), stop=(c == KC - 1))
                    last.then_inc(projected, 1)
                    pe.wait_ge(q_kept, r + 1)
                    if not shared_kv:
                        pe.wait_ge(k_kept, r + 1)
                        pe.wait_ge(v_kept, r + 1)
                    if b == B - 1:
                        pe.sem_inc(w_used, 1)
                    for u in range(U):
                        pe.wait_ge(k_masked, r * U + u + 1)
                        for h in range(parts):
                            step += 1
                            freed(g, b, step)
                            out = flat(b * STEPS + step)
                            for i, off, n in qside[h]:
                                last = pe.matmul(out[:, off:off + n], qT[:, i * P:(i + 1) * P], kmask[:, u, 0:n],
                                                 start=True, stop=not causal)
                                if causal:
                                    last = pe.matmul(out[:, off + n - P:off + n], core.identb[:, :], masksb[:, 0, :],
                                                     start=False, stop=True)
                            last.then_inc(rows_scored, 1)

                    step += 1
                    freed(g, b, step)
                    pe.wait_ge(max_taken, r * NU + NU)
                    out = flat(b * STEPS + step)
                    for i in range(QT):
                        last = pe.transpose(out[:, i * P:(i + 1) * P], mcol[:, i, :], core.ident[:, :])
                    last.then_inc(max_turned, 1)

                    def cols(u, h, step):
                        freed(g, b, step)
                        out = flat(b * STEPS + step)
                        for k, off, n in kside[h]:
                            q0 = T - n
                            pe.matmul(out[:, off:off + n], kmask[:, u, k * P:(k + 1) * P], qT[:, q0:T],
                                      start=True, stop=False)
                            last = pe.matmul(out[:, off:off + n], minus1b[:, u, :], mT[:, q0:T],
                                             start=False, stop=not causal)
                            if causal:
                                last = pe.matmul(out[:, off:off + P], core.identb[:, :], masksb[:, 1, :],
                                                 start=False, stop=True)
                        last.then_inc(cols_scored, 1)

                    def weigh(u):
                        pe.wait_ge(exp_done, r * NU + (u + 1) * parts + 1)
                        if u == 0:
                            pe.wait_ge(normed, r + 1)
                            pe.wait_ge(kv_kept if shared_kv else v_kept, 2 if shared_kv else r + 1)
                        for i in range(QT):
                            lo = (i % 2) * U * W + u * W
                            keys = [k for k in range(QT) if k <= i or not causal]
                            for k in keys:
                                if causal:
                                    off = next(off for kk, off, n in kside[0] if kk == k) + (i - k) * P
                                else:
                                    off = k * T + i * P
                                last = pe.matmul(ps[:, 6 + i // 2, lo:lo + W], probs[:, u % 2, off:off + P],
                                                 vaug[:, b if shared_kv else 0, k, 0 if shared_kv else u, :],
                                                 start=(k == keys[0]), stop=(k == keys[-1]))
                        last.then_inc(pv_done, 1)

                    pe.wait_ge(max_kept, r + 1)
                    for u in range(U):
                        for h in range(parts):
                            step += 1
                            cols(u, h, step)
                        if u >= 1:
                            weigh(u - 1)
                    weigh(U - 1)

                    step += 1
                    freed(g, b, step)
                    pe.wait_ge(normed, r + 2)
                    out = flat(b * STEPS + step)
                    for i in range(QT):
                        last = pe.transpose(out[0:M, i * P:(i + 1) * P], o[:, i, :], core.ident[:, :])
                    last.then_inc(o_turned, 1)

        @block.scalar
        def _(act):
            act.sem_inc(exp_done, 1)
            act.sem_inc(o_kept, 1)
            if shared_kv:
                act.wait_ge(kv_projected, 1)
                act.activation(kT[:, :, :], ps[:, 0:B, :], ACT.Copy).then_inc(kv_kept, 1)
            with act.Fori(0, G) as g:
                for b in range(B):
                    r = g * B + b
                    act.wait_ge(projected, r + 1)
                    out = flat(b * STEPS)
                    if qk_bias is None:
                        act.activation(qT[:, :], out[:, 0:T], ACT.Copy).then_inc(q_kept, 1)
                    else:
                        act.activation(qT[:, :], out[:, 0:T], ACT.Identity, bias=qkb[:, 0:1]).then_inc(q_kept, 1)
                    act.wait_ge(max_turned, r + 1)
                    out = flat(b * STEPS + NU + 1)
                    act.activation(mT[:, :], out[:, 0:T], ACT.Copy).then_inc(max_kept, 1)
                    for n in range(NU):
                        act.wait_ge(cols_scored, r * NU + n + 1)
                        u, h = n // parts, n % parts
                        if u >= 2 and h == 0:
                            act.wait_ge(pv_done, r * U + u - 1)
                        size = 1280 if causal else 1024
                        out = flat(b * STEPS + NU + 2 + n)
                        act.activation(probs[:, u % 2, h * 1024:h * 1024 + size], out[:, 0:size], ACT.Exp,
                                       scale=scale).then_inc(exp_done, 1)
                    act.wait_ge(o_turned, r + 1)
                    out = flat(b * STEPS + STEPS - 1)
                    act.activation(oT[0:M, g, b * T:(b + 1) * T], out[0:M, 0:T], ACT.Copy).then_inc(o_kept, 1)

        @block.vector
        def _(dve):
            dve.sem_inc(normed, 1)
            dve.memset(mcol[:, :, :], 0.0).then_inc(consts_made, 1)
            dve.memset(vaug[:, :, :, :, :], denominator).then_inc(consts_made, 1)
            dve.wait_ge(consts_in, 48 + 32 * shared_kv)
            dve.tensor_copy(minus1b[:, :, :], minus1[:, :, :]).then_inc(consts_made, 1)
            dve.tensor_copy(masksb[:, :, :], masks[:, :, :]).then_inc(consts_made, 1)
            dve.wait_ge(consts_made, 2)
            if shared_kv:
                dve.wait_ge(kv_projected, 1)
                dve.tensor_copy(vaug[:, :, :, 0, 0:E],
                                ps[:, 2, 0:NT * E].rearrange("p (b i e) -> p b i e", b=B, i=QT)).then_inc(kv_kept, 1)
            with dve.Fori(0, G) as g:
                for b in range(B):
                    r = g * B + b
                    if not shared_kv:
                        dve.wait_ge(projected, r + 1)
                        out = flat(b * STEPS)
                        if qk_bias is None:
                            dve.tensor_copy(kT[:, 0, :], out[:, T:2 * T]).then_inc(k_kept, 1)
                        else:
                            dve.tensor_scalar(kT[:, 0, :], out[:, T:2 * T], qkb[:, 1:2], None, ALU.add).then_inc(k_kept, 1)
                        for i in range(QT):
                            src = out[:, 2 * T + i * M:2 * T + (i + 1) * M].rearrange("p (u e) -> p u e", u=U)
                            if v_bias is None:
                                last = dve.tensor_copy(vaug[:, 0, i, :, 0:E], src)
                            else:
                                last = dve.tensor_tensor(vaug[:, 0, i, :, 0:E], src,
                                                         vb[:, :].rearrange("p (u e) -> p u e", u=U), ALU.add)
                        last.then_inc(v_kept, 1)
                    for n in range(NU):
                        dve.wait_ge(rows_scored, r * NU + n + 1)
                        u, h = n // parts, n % parts
                        out = flat(b * STEPS + 1 + n)
                        for i, off, w in qside[h]:
                            last = dve.reduce_max(mcol[:, i, u:u + 1], out[:, off:off + w], AX.X)
                        last.then_inc(max_taken, 1)
                    dve.wait_ge(pv_done, r * U + U)
                    for half in range(2):
                        pv = ps[:, 6 + half, 0:2 * U * W].rearrange("p (n e) -> p n e", e=W)
                        last = dve.reciprocal(rec[:, 2 * half:2 * half + 2, :].rearrange("p i u -> p (i u)"), pv[:, :, E])
                    last.then_inc(rec_done, 1)
                    dve.wait_ge(rec_done, r + 1)
                    for half in range(2):
                        pv = ps[:, 6 + half, 0:2 * U * W].rearrange("p (n e) -> p n e", e=W)
                        rb = rec[:, 2 * half:2 * half + 2, :].rearrange("p i u -> p (i u)").unsqueeze(2)
                        last = dve.tensor_tensor(
                            o[:, 2 * half:2 * half + 2, :].rearrange("p i (u e) -> p (i u) e", u=U),
                            pv[:, :, 0:E], rb.broadcast_to([P, 2 * U, E]), ALU.mult)
                    last.then_inc(normed, 1)


def project_out(core, name, oT, G, M, w_d, bias_d=None):
    ps, mixed = core.ps, core.mixed
    with Stage(core, name) as st:
        w = st.sb("w", [M, G, D])
        bias = st.sb("bias", [P, D])
        w_in, done = st.sem("w_in"), st.sem("done")
        kept = st.sem("kept_v"), st.sem("kept_s")
        block = st.block()

        @block.sync
        def _(sp):
            sp.dma_start(w[:, :, :], w_d).then_inc(w_in, 16)
            if bias_d is not None:
                sp.dma_start(bias[:, :], bias_d.partition_broadcast(P)).then_inc(w_in, 16)

        @block.tensor
        def _(pe):
            pe.wait_ge(w_in, 16 if bias_d is None else 32)
            for t in range(NT):
                for g in range(G):
                    last = pe.matmul(ps[:, t, :], oT[0:M, g, t * P:(t + 1) * P], w[:, g, :],
                                     start=(g == 0), stop=(g == G - 1))
                last.then_inc(done, 1)

        @block.vector
        def _(dve):
            for t in range(NT) if bias_d is not None else range(0, NT, 2):
                dve.wait_ge(done, t + 1)
                if bias_d is not None:
                    dve.tensor_tensor(mixed[:, t, :], ps[:, t, :], bias[:, :], ALU.add).then_inc(kept[0], 1)
                else:
                    dve.tensor_copy(mixed[:, t, :], ps[:, t, :]).then_inc(kept[0], 1)

        @block.scalar
        def _(act):
            if bias_d is None:
                for t in range(1, NT, 2):
                    act.wait_ge(done, t + 1)
                    act.activation(mixed[:, t, :], ps[:, t, :], ACT.Copy).then_inc(kept[1], 1)


def gate_steps(core, eng_wait, dve, t, f, th, gated, chain, x_done):
    chain(dve.scalar_tensor_tensor(out=gated, in0=th, scalar=1.0, in1=f, op0=ALU.add, op1=ALU.mult))
    chain(dve.scalar_tensor_tensor(out=gated, in0=gated, scalar=0.5, in1=core.mixed[:, t, :],
                                   op0=ALU.mult, op1=ALU.mult))
    dve.tensor_tensor(core.x[:, t, :], core.x[:, t, :], gated, ALU.add).then_inc(x_done, 1)


def experts(core, name):
    nc, ins, ps, xnT = core.nc, core.ins, core.ps, core.xnT
    NE = 8
    with Stage(core, name) as st:
        wg = st.sb("wg", [P, KC, NE])
        bg = st.sb("bg", [P, NE])
        we = st.sb("we", [P, 2, KC, D])
        be = st.sb("be", [P, 2, D])
        logits = st.sb("logits", [P, NT, NE])
        best = st.sb("best", [P, NT, 8])
        where = st.sb("where", [P, NT, 8], U32)
        wheref = st.sb("wheref", [P, NT, 8])
        iota = st.sb("iota", [P, NE])
        pick = st.sb("pick", [P, 2, NT, NE])
        share = st.sb("share", [P, NT, NE])
        now = st.sb("now", [P, 2, NT])
        biased = st.sb("biased", [P, 2, D])
        acted = st.sb("acted", [P, 2, D])
        f = st.sb("f", [P, NT, D])
        th = st.sb("th", [P, 2, D])
        gated = st.sb("gated", [P, D])
        step, consts_in = st.sem("step"), st.sem("consts_in")
        w_in = st.sem("w_in"), st.sem("w_in1")
        e_done, freed = st.sem("expert_done"), st.sem("freed")
        logits_done, shared = st.sem("logits_done"), st.sem("shared")
        mm_done, biased_done, acted_done, summed = (st.sem("mm_done"), st.sem("biased_done"), st.sem("acted_done"),
                                                    st.sem("summed"))
        cleared, now_done = st.sem("cleared"), st.sem("now_done")
        tanh_done, x_done = st.sem("tanh_done"), st.sem("x_done")
        block = st.block()
        TILES = 2 * NT

        @block.sync
        def _(sp):
            sp.dma_start(wg[:, :, :], ins["l0_wgate"]).then_inc(consts_in, 16)
            sp.dma_start(bg[:, :], ins["l0_bgate"].partition_broadcast(P)).then_inc(consts_in, 16)
            sp.dma_start(iota[:, :], ins["iota8"].partition_broadcast(P)).then_inc(consts_in, 16)
            with sp.Fori(0, NE // 2) as j:
                for s in range(2):
                    sp.wait_ge(e_done, j * 2 + s + 1)
                    sp.sem_inc(freed, 1)
                    sp.dma_start(we[:, s, :, :], ins["l0_we"][j * 2 + s]).then_inc(w_in[s], 16)
                    sp.dma_start(be[:, s, :], ins["l0_be"][j * 2 + s].partition_broadcast(P)).then_inc(w_in[s], 16)

        @block.tensor
        def _(pe):
            pe.wait_ge(consts_in, 48)
            for t in range(NT):
                for c in range(KC):
                    last = pe.matmul(ps[:, 7, t * NE:(t + 1) * NE], xnT[:, c, t * P:(t + 1) * P], wg[:, c, :],
                                     start=(c == 0), stop=(c == KC - 1))
            last.then_inc(logits_done, 1)
            with pe.Fori(0, NE // 2) as j:
                for s in range(2):
                    pe.wait_ge(w_in[s], j * 32 + 32)
                    for t in range(NT):
                        n = s * NT + t
                        pe.wait_ge(biased_done, j * TILES + n + 1)
                        for c in range(KC):
                            last = pe.matmul(ps[:, n % 4, :], xnT[:, c, t * P:(t + 1) * P], we[:, s, c, :],
                                             start=(c == 0), stop=(c == KC - 1))
                        last.then_inc(mm_done, 1)

        @block.vector
        def _(dve):
            chain = Chain(dve, step)
            dve.sem_inc(biased_done, 4)
            dve.sem_inc(e_done, 2)
            dve.wait_ge(consts_in, 48)
            dve.wait_ge(logits_done, 1)
            chain(dve.tensor_tensor(logits[:, :, :], ps[:, 7, 0:NT * NE].rearrange("p (t e) -> p t e", e=NE),
                                    bg[:, :].unsqueeze(1).broadcast_to([P, NT, NE]), ALU.add))
            for t in range(NT):
                last = dve.max(best[:, t, :], logits[:, t, :])
            chain(last)
            for t in range(NT):
                last = dve.max_index(where[:, t, :], best[:, t, :], logits[:, t, :])
            chain(last)
            chain(dve.tensor_copy(wheref[:, :, :], where[:, :, :]))
            for k in range(2):
                last = dve.tensor_tensor(pick[:, k, :, :], iota[:, :].unsqueeze(1).broadcast_to([P, NT, NE]),
                                         wheref[:, :, k:k + 1].broadcast_to([P, NT, NE]), ALU.is_equal)
            chain(last)
            chain(dve.tensor_tensor(share[:, :, :], pick[:, 0, :, :], pick[:, 1, :, :], ALU.add))
            chain(dve.tensor_scalar(share[:, :, :], share[:, :, :], 0.5, None, ALU.mult))
            with dve.Fori(0, NE // 2) as j:
                for s in range(2):
                    dve.wait_ge(acted_done, j * TILES + s * NT + NT)
                    dve.tensor_copy(now[:, s, :].unsqueeze(2), share[:, :, bass.ds(j * 2 + s, 1)]).then_inc(now_done, 1)
                    dve.wait_ge(w_in[s], j * 32 + 32)
                    for t in range(NT):
                        n = s * NT + t
                        dve.wait_ge(mm_done, j * TILES + n + 1)
                        dve.wait_ge(acted_done, j * TILES + n + TILES - 1)
                        dve.tensor_tensor(biased[:, t % 2, :], ps[:, n % 4, :], be[:, s, :],
                                          ALU.add).then_inc(biased_done, 1)
                    dve.wait_ge(biased_done, j * TILES + s * NT + NT + 4)
                    dve.sem_inc(e_done, 1)
            dve.wait_ge(summed, NE * NT + 2)
            chain.n = chain.n
            for t in range(NT):
                dve.wait_ge(tanh_done, t + 1)
                gate_steps(core, None, dve, t, f[:, t, :], th[:, t % 2, :], gated[:, :], chain, x_done)
                dve.wait_ge(x_done, t + 1)

        @block.scalar
        def _(act):
            act.sem_inc(acted_done, TILES)
            with act.Fori(0, NE // 2) as j:
                for s in range(2):
                    act.wait_ge(now_done, j * 2 + s + 1)
                    for t in range(NT):
                        n = s * NT + t
                        act.wait_ge(biased_done, j * TILES + n + 1 + 4)
                        act.wait_ge(summed, j * TILES + n + 1)
                        act.activation(acted[:, t % 2, :], biased[:, t % 2, :], ACT.Relu,
                                       scale=now[:, s, t:t + 1]).then_inc(acted_done, 1)
            for t in range(NT):
                act.wait_ge(summed, NE * NT + 2)
                if t >= 2:
                    act.wait_ge(x_done, t - 1)
                act.activation(th[:, t % 2, :], f[:, t, :], ACT.Tanh, scale=0.5).then_inc(tanh_done, 1)

        @block.gpsimd
        def _(pool):
            pool.memset(f[:, :, :], 0.0).then_inc(cleared, 1)
            pool.wait_ge(cleared, 1)
            pool.sem_inc(summed, 2)
            with pool.Fori(0, NE // 2) as j:
                for s in range(2):
                    for t in range(NT):
                        n = s * NT + t
                        pool.wait_ge(acted_done, j * TILES + n + 1 + TILES)
                        if s == 1 or t >= 0:
                            pool.wait_ge(summed, j * TILES + n + 1)
                        pool.tensor_tensor(f[:, t, :], f[:, t, :], acted[:, t % 2, :], ALU.add).then_inc(summed, 1)


def dense_gate(core, name, w_d, zT=None, ZR=0, zw_d=None, half=0.5, out_d=None):
    ps, xnT = core.ps, core.xnT
    with Stage(core, name) as st:
        w = st.sb("w", [P, KC, D])
        zw = st.sb("zw", [max(ZR, 1), D])
        th = st.sb("th", [P, 2, D])
        fsb = st.sb("fsb", [P, 2, D])
        gated = st.sb("gated", [P, D])
        w_in, done, tanh_done, x_done = st.sem("w_in"), st.sem("done"), st.sem("tanh_done"), st.sem("x_done")
        step, stored = st.sem("step"), st.sem("stored")
        block = st.block()

        @block.sync
        def _(sp):
            sp.dma_start(w[:, :, :], w_d).then_inc(w_in, 16)
            if ZR:
                sp.dma_start(zw[:, :], zw_d).then_inc(w_in, 16)
            if out_d is not None:
                for t in range(NT):
                    sp.wait_ge(x_done, t + 1)
                    sp.dma_start(out_d[t * P:(t + 1) * P, :], core.x[:, t, :]).then_inc(stored, 16)
                sp.wait_ge(stored, 16 * NT)

        @block.tensor
        def _(pe):
            pe.wait_ge(w_in, 32 if ZR else 16)
            for t in range(NT):
                for c in range(KC):
                    last = pe.matmul(ps[:, t, :], xnT[:, c, t * P:(t + 1) * P], w[:, c, :],
                                     start=(c == 0), stop=(c == KC - 1 and not ZR))
                if ZR:
                    last = pe.matmul(ps[:, t, :], zT[0:ZR, t * P:(t + 1) * P], zw[:, :], start=False, stop=True)
                last.then_inc(done, 1)

        @block.scalar
        def _(act):
            for t in range(NT):
                act.wait_ge(done, t + 1)
                if t >= 2:
                    act.wait_ge(x_done, t - 1)
                act.activation(th[:, t % 2, :], ps[:, t, :], ACT.Tanh, scale=half).then_inc(tanh_done, 1)

        @block.vector
        def _(dve):
            chain = Chain(dve, step)
            for t in range(NT):
                dve.wait_ge(tanh_done, t + 1)
                gate_steps(core, None, dve, t, ps[:, t, :], th[:, t % 2, :], gated[:, :], chain, x_done)
                dve.wait_ge(x_done, t + 1)


def lora_top1(core, name, zT):
    ins, ps, xnT = core.ins, core.ps, core.xnT
    NE, R = 4, 8
    C = NE + NE * R
    with Stage(core, name) as st:
        w = st.sb("w", [P, KC, C])
        bias = st.sb("bias", [P, NE])
        iota = st.sb("iota", [P, 8])
        logits = st.sb("logits", [P, NT, 8])
        best = st.sb("best", [P, NT, 8])
        where = st.sb("where", [P, NT, 8], U32)
        wheref = st.sb("wheref", [P, NT, 8])
        pick = st.sb("pick", [P, NT, NE])
        z = st.sb("z", [P, NT, NE * R])
        loaded, done, step, z_done = st.sem("loaded"), st.sem("done"), st.sem("step"), st.sem("z_done")
        turned, kept = st.sem("turned"), st.sem("kept")
        block = st.block()

        @block.sync
        def _(sp):
            sp.dma_start(w[:, :, :], ins["l1_wz"]).then_inc(loaded, 16)
            sp.dma_start(bias[:, :], ins["l1_bz"].partition_broadcast(P)).then_inc(loaded, 16)
            sp.dma_start(iota[:, :], ins["iota8"].partition_broadcast(P)).then_inc(loaded, 16)

        @block.tensor
        def _(pe):
            pe.wait_ge(loaded, 48)
            for t in range(NT):
                for c in range(KC):
                    last = pe.matmul(ps[:, 0, t * C:(t + 1) * C], xnT[:, c, t * P:(t + 1) * P], w[:, c, :],
                                     start=(c == 0), stop=(c == KC - 1))
            last.then_inc(done, 1)
            pe.wait_ge(z_done, 1)
            for t in range(NT):
                last = pe.transpose(ps[0:NE * R, 1 + t // 4, (t % 4) * P:(t % 4 + 1) * P], z[:, t, :], core.ident[:, :])
            last.then_inc(turned, 1)

        @block.vector
        def _(dve):
            chain = Chain(dve, step)
            got = ps[:, 0, 0:NT * C].rearrange("p (t c) -> p t c", c=C)
            chain(dve.memset(logits[:, :, :], -3e38))
            dve.wait_ge(done, 1)
            dve.wait_ge(loaded, 48)
            chain(dve.tensor_tensor(logits[:, :, 0:NE], got[:, :, 0:NE],
                                    bias[:, :].unsqueeze(1).broadcast_to([P, NT, NE]), ALU.add))
            for t in range(NT):
                last = dve.max(best[:, t, :], logits[:, t, :])
            chain(last)
            for t in range(NT):
                last = dve.max_index(where[:, t, :], best[:, t, :], logits[:, t, :])
            chain(last)
            chain(dve.tensor_copy(wheref[:, :, :], where[:, :, :]))
            chain(dve.tensor_tensor(pick[:, :, :], iota[:, 0:NE].unsqueeze(1).broadcast_to([P, NT, NE]),
                                    wheref[:, :, 0:1].broadcast_to([P, NT, NE]), ALU.is_equal))
            for t in range(NT):
                last = dve.tensor_tensor(z[:, t, :].rearrange("p (e r) -> p e r", e=NE),
                                         got[:, t, NE:C].rearrange("p (e r) -> p e r", e=NE),
                                         pick[:, t, :].unsqueeze(2).broadcast_to([P, NE, R]), ALU.mult)
            last.then_inc(z_done, 1)
            dve.wait_ge(turned, 1)
            dve.tensor_copy(zT[0:NE * R, :].rearrange("p (h n) -> p h n", h=2), ps[0:NE * R, 1:3, :]).then_inc(kept, 1)


def lora_by_batch(core, name, zT):
    ins, ps, xnT = core.ins, core.ps, core.xnT
    NA, R, S = 3, 16, 4
    C = NA * R
    with Stage(core, name) as st:
        w = st.sb("w", [P, KC, C])
        starts = st.sb("starts", [P, S], I32)
        startf = st.sb("startf", [P, S])
        row = st.sb("row", [P, 1])
        past = st.sb("past", [P, B, S])
        seg = st.sb("seg", [P, B])
        pick = st.sb("pick", [P, B])
        loaded, done, step, kept = st.sem("loaded"), st.sem("done"), st.sem("step"), st.sem("kept")
        block = st.block()

        @block.sync
        def _(sp):
            sp.dma_start(w[:, :, :], ins["l2_wz"]).then_inc(loaded, 16)
            sp.dma_start(starts[:, :], ins["l2_starts"].partition_broadcast(P)).then_inc(loaded, 16)
            sp.dma_start(row[:, :], ins["adapter_of_row"]).then_inc(loaded, 16)

        @block.tensor
        def _(pe):
            pe.wait_ge(loaded, 48)
            for b in range(B):
                for c in range(KC):
                    last = pe.matmul(ps[0:C, b, :], w[:, c, :], xnT[:, c, b * T:(b + 1) * T],
                                     start=(c == 0), stop=(c == KC - 1))
            last.then_inc(done, 1)

        @block.vector
        def _(dve):
            chain = Chain(dve, step)
            chain(dve.memset(zT[:, :], 1.0))
            dve.wait_ge(loaded, 48)
            chain(dve.tensor_copy(startf[:, :], starts[:, :]))
            for b in range(B):
                last = dve.tensor_scalar(past[:, b, :], startf[:, :], float(b), None, ALU.is_le)
            chain(last)
            chain(dve.tensor_reduce(seg[:, :], past[:, :, :], AX.X, ALU.add))
            chain(dve.tensor_scalar(seg[:, :], seg[:, :], -2.0, float(NA - 1), ALU.add, ALU.min))
            chain(dve.tensor_scalar(pick[:, :], seg[:, :], row[:, 0:1], None, ALU.is_equal))
            dve.wait_ge(done, 1)
            for b in range(B):
                last = dve.tensor_scalar(zT[0:C, b * T:(b + 1) * T], ps[0:C, b, :], pick[0:C, b:b + 1], None, ALU.mult)
            last.then_inc(kept, 1)


def decays(core, name, rows_d, lw, ew, wst, eglast=None):
    ins, ps, xnT = core.ins, core.ps, core.xnT
    H = 32
    with Stage(core, name) as st:
        w = st.sb("w", [P, KC, H])
        dtb = st.sb("dtb", [P, H])
        ab = st.sb("ab", [P, H])
        ea = st.sb("ea", [P, H])
        tri = st.sb("tri", [P, P])
        ones = st.sb("ones", [P, P])
        z = st.sb("z", [P, NT, H])
        az = st.sb("az", [P, NT, H])
        dt = st.sb("dt", [P, NT, H])
        g = st.sb("g", [P, NT, H])
        G = st.sb("G", [P, NT, H])
        lndt = st.sb("lndt", [P, NT, H])
        GT = st.sb("GT", [H, N])
        loaded, done, step = st.sem("loaded"), st.sem("done"), st.sem("step")
        z_done, a_done, sp_done, dt_done, ln_done = (st.sem("z_done"), st.sem("a_done"), st.sem("sp_done"),
                                                     st.sem("dt_done"), st.sem("ln_done"))
        g_done, G_done, G_kept, d_done, turned, GT_kept, stored = (
            st.sem("g_done"), st.sem("G_done"), st.sem("G_kept"), st.sem("d_done"), st.sem("turned"),
            st.sem("GT_kept"), st.sem("stored"))
        act_step = st.sem("act_step")
        block = st.block()

        @block.sync
        def _(sp):
            sp.dma_start(w[:, :, :], ins["l1_win"]).then_inc(loaded, 16)
            sp.dma_start(dtb[:, :], ins["l1_dtb"].partition_broadcast(P)).then_inc(loaded, 16)
            sp.dma_start(ab[:, :], ins["l1_ab"].partition_broadcast(P)).then_inc(loaded, 16)
            sp.dma_start(tri[:, :], ins["tri"]).then_inc(loaded, 16)
            sp.wait_ge(GT_kept, 2)
            sp.dma_start(rows_d, GT[:, :]).then_inc(stored, 16)
            sp.wait_ge(stored, 16)

        @block.tensor
        def _(pe):
            pe.wait_ge(loaded, 64)
            for t in range(NT):
                for c in range(KC):
                    last = pe.matmul(ps[:, 0, t * H:(t + 1) * H], xnT[:, c, t * P:(t + 1) * P], w[:, c, :],
                                     start=(c == 0), stop=(c == KC - 1))
            last.then_inc(done, 1)
            pe.wait_ge(g_done, 1)
            pe.matmul(ps[:, 1, 0:NT * H], tri[:, :], g[:, :, :].rearrange("p t h -> p (t h)"), start=True, stop=True)
            pe.matmul(ps[:, 2, 0:NT * H], ones[:, :], g[:, :, :].rearrange("p t h -> p (t h)"),
                      start=True, stop=True).then_inc(G_done, 1)
            pe.wait_ge(G_kept, 1)
            for t in range(NT):
                last = pe.transpose(ps[0:H, 3 + t // 4, (t % 4) * P:(t % 4 + 1) * P], G[:, t, :], core.ident[:, :])
            last.then_inc(turned, 1)

        def flat(a):
            return a[:, :, :].rearrange("p t h -> p (t h)")

        @block.scalar
        def _(act):
            act.wait_ge(loaded, 64)
            act.activation(ea[:, :], ab[:, :], ACT.Exp).then_inc(a_done, 1)
            act.wait_ge(z_done, 1)
            act.activation(az[:, :, :], az[:, :, :], ACT.Exp, scale=-1.0).then_inc(act_step, 1)
            act.wait_ge(act_step, 1)
            act.activation(az[:, :, :], az[:, :, :], ACT.Ln, bias=1.0).then_inc(sp_done, 1)
            act.wait_ge(dt_done, 1)
            act.activation(lndt[:, :, :], dt[:, :, :], ACT.Ln).then_inc(ln_done, 1)
            act.wait_ge(d_done, 1)
            act.activation(wst[:, :, :], wst[:, :, :], ACT.Exp).then_inc(act_step, 1)

        @block.vector
        def _(dve):
            chain = Chain(dve, step)
            chain(dve.memset(ones[:, :], 1.0))
            dve.wait_ge(loaded, 64)
            dve.wait_ge(done, 1)
            chain(dve.tensor_tensor(z[:, :, :], ps[:, 0, 0:NT * H].rearrange("p (t h) -> p t h", h=H),
                                    dtb[:, :].unsqueeze(1).broadcast_to([P, NT, H]), ALU.add))
            chain(dve.tensor_scalar(az[:, :, :], z[:, :, :], -1.0, None, ALU.mult))
            dve.tensor_tensor(az[:, :, :], az[:, :, :], z[:, :, :], ALU.max).then_inc(z_done, 1)
            dve.wait_ge(sp_done, 1)
            dve.scalar_tensor_tensor(out=dt[:, :, :], in0=z[:, :, :], scalar=0.0, in1=az[:, :, :],
                                     op0=ALU.max, op1=ALU.add).then_inc(dt_done, 1)
            dve.wait_ge(dt_done, 1)
            dve.wait_ge(a_done, 1)
            dve.scalar_tensor_tensor(out=g[:, :, :], in0=dt[:, :, :], scalar=-1.0,
                                     in1=ea[:, :].unsqueeze(1).broadcast_to([P, NT, H]),
                                     op0=ALU.mult, op1=ALU.mult).then_inc(g_done, 1)
            dve.wait_ge(G_done, 1)
            dve.tensor_copy(flat(G), ps[:, 1, 0:NT * H]).then_inc(G_kept, 1)
            dve.wait_ge(G_kept, 1)
            dve.wait_ge(ln_done, 1)
            chain(dve.tensor_tensor(lw[:, :, :], G[:, :, :], lndt[:, :, :], ALU.subtract))
            dve.tensor_tensor(flat(wst), ps[:, 2, 0:NT * H], flat(lw), ALU.subtract).then_inc(d_done, 1)
            dve.wait_ge(turned, 1)
            dve.tensor_copy(GT[:, :].rearrange("p (h n) -> p h n", h=2), ps[0:H, 3:5, :]).then_inc(GT_kept, 2)


def retention(core, name, rows_d, lw, wst):
    nc, ins, ps, xnT, mixed = core.nc, core.ins, core.ps, core.xnT, core.mixed
    KV, R, H = 8, 4, 32
    with Stage(core, name) as st:
        wq = st.sb("wq", [P, KC, R * P])
        wg = st.sb("wg", [P, KC, R * P])
        wo = st.sb("wo", [P, R, D])
        wk = st.sb("wk", [P, KC, P])
        wv = st.sb("wv", [P, KC, P])
        cos = st.sb("cos", [P, T])
        sin = st.sb("sin", [P, T])
        gw = st.sb("gw", [P, 1])
        limit = st.sb("limit", [P, P])
        ones = st.sb("ones", [P, P])
        qT = st.sb("qT", [P, R, N])
        silu = st.sb("silu", [P, R, N])
        kT = st.sb("kT", [P, N])
        ktm = st.sb("ktm", [P, NT, P])
        v = st.sb("v", [P, NT, P])
        rows = st.sb("rows", [P, R, N])
        dec = st.sb("dec", [P, NT, R * P])
        lws = st.sb("lws", [P, NT, R])
        wsts = st.sb("wsts", [P, NT, R])
        ra = st.sb("ra", [P, 2, T])
        rb = st.sb("rb", [P, 2, T])
        sc = st.sb("sc", [P, R * P])
        qg = st.sb("qg", [P, R, P])
        vw = st.sb("vw", [P, R, P])
        state = st.sb("state", [P, R * P])
        y2 = st.sb("y2", [P, R * P])
        rms = st.sb("rms", [P, R * P])
        ry = st.sb("ry", [P, R * P])
        th = st.sb("th", [P, 2, T])
        eps = st.sb("eps", [P, 1])

        consts_in, ones_made = st.sem("consts_in"), st.sem("ones_made")
        w_in, rows_in, freed = st.sem("w_in"), st.sem("rows_in"), st.sem("freed")
        turn_done = st.sem("turn_done")
        jobs_done = st.sem("jobs_done")
        kept_v, kept_s = st.sem("kept_v"), st.sem("kept_s")
        dstep, gate_done = st.sem("dstep"), st.sem("gate_done")
        raw_done, dec_done, erow_done = st.sem("raw_done"), st.sem("dec_done"), st.sem("erow_done")
        s_done, sc_done, qg_done, vw_done, y_done, st_done, cs_done = (
            st.sem("s_done"), st.sem("sc_done"), st.sem("qg_done"), st.sem("vw_done"), st.sem("y_done"),
            st.sem("st_done"), st.sem("cs_done"))
        y2_done, ms_done, rms_done, ry_done, z_done, added = (
            st.sem("y2_done"), st.sem("ms_done"), st.sem("rms_done"), st.sem("ry_done"), st.sem("wo_done"),
            st.sem("added"))
        kt_done, ktm_done, cleared = st.sem("kt_done"), st.sem("ktm_done"), st.sem("cleared")
        block = st.block()

        jobs = [("k", 0, b) for b in range(B)] + [("v", 0, b) for b in range(B)]
        for h in range(R):
            for b in range(B):
                jobs += [("q", h, b), ("g", h, b)]
        NJ = len(jobs)
        ROPE = [n for n, j in enumerate(jobs) if j[0] in "kq"]
        SIDE = [n for n, j in enumerate(jobs) if j[0] in "vg"]

        @block.sync
        def _(sp):
            sp.dma_start(cos[:, :], ins["cos"]).then_inc(consts_in, 16)
            sp.dma_start(sin[:, :], ins["sin"]).then_inc(consts_in, 16)
            sp.dma_start(gw[:, :], ins["l1_gw"]).then_inc(consts_in, 16)
            sp.dma_start(limit[:, :], ins["limit"]).then_inc(consts_in, 16)
            with sp.Fori(0, KV) as kv:
                sp.wait_ge(turn_done, kv + 1)
                sp.sem_inc(freed, 1)
                sp.dma_start(wk[:, :, :], ins["l1_wk"][kv]).then_inc(w_in, 16)
                sp.dma_start(wv[:, :, :], ins["l1_wv"][kv]).then_inc(w_in, 16)
                sp.dma_start(wq[:, :, :], ins["l1_wq"][kv]).then_inc(w_in, 16)
                sp.dma_start(wg[:, :, :], ins["l1_wg"][kv]).then_inc(w_in, 16)
                sp.dma_start(wo[:, :, :], ins["l1_wo"][kv]).then_inc(w_in, 16)
                sp.dma_start(rows[:, :, :], rows_d[kv].partition_broadcast(P)).then_inc(rows_in, 16)

        @block.tensor
        def _(pe):
            pe.sem_inc(turn_done, 1)
            pe.wait_ge(ones_made, 1)
            with pe.Fori(0, KV) as kv:
                pe.wait_ge(w_in, kv * 80 + 80)
                pe.wait_ge(added, kv * NT + 1)
                for n, (kind, h, b) in enumerate(jobs):
                    if n >= 6:
                        m = n - 6
                        if m in ROPE:
                            pe.wait_ge(kept_v, kv * len(ROPE) + ROPE.index(m) + 1)
                        else:
                            pe.wait_ge(kept_s, kv * len(SIDE) + SIDE.index(m) + 1)
                    out = ps[:, n % 6, :]
                    if kind == "v":
                        for i in range(QT):
                            t = b * QT + i
                            for c in range(KC):
                                last = pe.matmul(out[:, i * P:(i + 1) * P], xnT[:, c, t * P:(t + 1) * P], wv[:, c, :],
                                                 start=(c == 0), stop=(c == KC - 1))
                    else:
                        w = {"k": wk, "q": wq, "g": wg}[kind]
                        for c in range(KC):
                            last = pe.matmul(out, w[:, c, h * P:(h + 1) * P], xnT[:, c, b * T:(b + 1) * T],
                                             start=(c == 0), stop=(c == KC - 1))
                    last.then_inc(jobs_done, 1)
                pe.wait_ge(kept_v, kv * len(ROPE) + 2)
                for t in range(NT):
                    last = pe.transpose(ps[:, 6 + t // 4, (t % 4) * P:(t % 4 + 1) * P], kT[:, t * P:(t + 1) * P],
                                        core.ident[:, :])
                last.then_inc(kt_done, 1)
                pe.wait_ge(kept_v, kv * len(ROPE) + len(ROPE))
                pe.wait_ge(kept_s, kv * len(SIDE) + len(SIDE))
                pe.wait_ge(ktm_done, kv + 1)
                for t in range(NT):
                    c = t % QT
                    T1 = kv * NT + t + 1
                    if t >= 1:
                        pe.wait_ge(sc_done, T1 - 1)
                    pe.matmul(ps[:, 0, :], kT[:, t * P:(t + 1) * P], qT[:, :, t * P:(t + 1) * P],
                              start=True, stop=True).then_inc(s_done, 1)
                    pe.wait_ge(sc_done, T1)
                    if t >= 1:
                        pe.wait_ge(ry_done, T1 - 1)
                    pe.wait_ge(qg_done, T1)
                    last = pe.matmul(ps[:, 1, :], v[:, t, :], sc[:, :], start=True, stop=True)
                    if c > 0:
                        pe.wait_ge(st_done, T1 - 1)
                        for h in range(R):
                            last = pe.matmul(ps[:, 1, h * P:(h + 1) * P], state[:, h * P:(h + 1) * P], qg[:, h, :],
                                             start=False, stop=True, skip_group_check=True)
                    last.then_inc(y_done, 1)
                    pe.wait_ge(vw_done, T1)
                    if t >= 1:
                        pe.wait_ge(st_done, T1 - 1)
                    pe.matmul(ps[:, 2, :], ktm[:, t, :], vw[:, :, :].rearrange("p h e -> p (h e)"),
                              start=True, stop=True).then_inc(cs_done, 1)
                    pe.wait_ge(y2_done, T1)
                    pe.matmul(ps[:, 3, :], ones[:, :], y2[:, :], start=True, stop=True).then_inc(ms_done, 1)
                    pe.wait_ge(ry_done, T1)
                    if t >= 1:
                        pe.wait_ge(added, T1)
                    for h in range(R):
                        last = pe.matmul(ps[:, 4, :], ry[:, h * P:(h + 1) * P], wo[:, h, :],
                                         start=(h == 0), stop=(h == R - 1))
                    last.then_inc(z_done, 1)
                pe.wait_ge(z_done, kv * NT + NT)
                pe.sem_inc(turn_done, 1)

        @block.scalar
        def _(act):
            with act.Fori(0, KV) as kv:
                for n, (kind, h, b) in enumerate(jobs):
                    if kind not in "vg":
                        continue
                    act.wait_ge(jobs_done, kv * NJ + n + 1)
                    if kind == "v":
                        act.activation(v[:, b * QT:(b + 1) * QT, :].rearrange("p i e -> p (i e)"), ps[:, n % 6, :],
                                       ACT.Copy).then_inc(kept_s, 1)
                    else:
                        m = h * B + b
                        if m >= 2:
                            act.wait_ge(gate_done, kv * (R * B) + m - 1)
                        act.activation(th[:, b, :], ps[:, n % 6, :], ACT.Tanh, scale=0.5)
                        act.activation(silu[:, h, b * T:(b + 1) * T], ps[:, n % 6, :], ACT.Copy,
                                       scale=0.5).then_inc(kept_s, 1)
                act.wait_ge(raw_done, kv + 1)
                act.activation(dec[:, :, :], dec[:, :, :], ACT.Exp).then_inc(dec_done, 1)
                act.activation(rows[:, :, :], rows[:, :, :], ACT.Exp).then_inc(erow_done, 1)
                for t in range(NT):
                    T1 = kv * NT + t + 1
                    act.wait_ge(y_done, T1)
                    act.activation(y2[:, :], ps[:, 1, :], ACT.Square).then_inc(y2_done, 1)
                    act.wait_ge(ms_done, T1)
                    act.activation(rms[:, :], ps[:, 3, :], ACT.Sqrt, bias=eps[:, 0:1], scale=1.0 / P).then_inc(rms_done, 1)

        @block.gpsimd
        def _(pool):
            pool.memset(eps[:, :], EPS).then_inc(cleared, 1)
            pool.memset(mixed[:, :, :], 0.0).then_inc(cleared, 1)
            with pool.Fori(0, KV) as kv:
                pool.wait_ge(erow_done, kv + 1)
                pool.wait_ge(kept_v, kv * len(ROPE) + len(ROPE))
                pool.wait_ge(kept_s, kv * len(SIDE) + len(SIDE))
                for t in range(NT):
                    T1 = kv * NT + t + 1
                    if t >= 1:
                        pool.wait_ge(y_done, T1 - 1)
                    pool.tensor_tensor(qg[:, :, :], qT[:, :, t * P:(t + 1) * P], rows[:, :, t * P:(t + 1) * P],
                                       ALU.mult).then_inc(qg_done, 1)
                    if t >= 1:
                        pool.wait_ge(cs_done, T1 - 1)
                    pool.tensor_tensor(vw[:, :, :], v[:, t, :].unsqueeze(1).broadcast_to([P, R, P]),
                                       wsts[:, t, :].unsqueeze(2).broadcast_to([P, R, P]), ALU.mult).then_inc(vw_done, 1)

        @block.vector
        def _(dve):
            dve.sem_inc(added, 1)
            dve.memset(ones[:, :], 1.0).then_inc(ones_made, 1)
            dve.wait_ge(consts_in, 64)
            dve.wait_ge(cleared, 2)
            with dve.Fori(0, KV) as kv:
                count = [0]

                def chain(ins, per):
                    count[0] += 1
                    ins.then_inc(dstep, 1)
                    dve.wait_ge(dstep, kv * per + count[0])

                NSTEP = 1 + len(ROPE) + 2 * NT
                dve.tensor_copy(lws[:, :, :], lw[:, :, bass.ds(kv * R, R)])
                chain(dve.tensor_copy(wsts[:, :, :], wst[:, :, bass.ds(kv * R, R)]), NSTEP)
                dve.wait_ge(rows_in, kv * 16 + 16)
                for t in range(NT):
                    for h in range(R):
                        last = dve.scalar_tensor_tensor(
                            out=dec[:, t, h * P:(h + 1) * P], in0=rows[:, h, t * P:(t + 1) * P],
                            scalar=lws[:, t, h:h + 1], in1=limit[:, :], op0=ALU.subtract, op1=ALU.min)
                last.then_inc(raw_done, 1)
                for n, (kind, h, b) in enumerate(jobs):
                    if kind in "kq":
                        s = b
                        dve.wait_ge(jobs_done, kv * NJ + n + 1)
                        out = kT[:, b * T:(b + 1) * T] if kind == "k" else qT[:, h, b * T:(b + 1) * T]
                        dve.tensor_tensor(ra[:, s, :], ps[:, n % 6, :], cos[:, :], ALU.mult)
                        dve.tensor_tensor(rb[0:64, s, :], ps[64:128, n % 6, :], sin[0:64, :], ALU.mult)
                        chain(dve.tensor_tensor(rb[64:128, s, :], ps[0:64, n % 6, :], sin[64:128, :], ALU.mult), NSTEP)
                        ins_ = dve.tensor_tensor(out, ra[:, s, :], rb[:, s, :], ALU.add)
                        ins_.then_inc(kept_v, 1)
                    if kind == "g":
                        m = h * B + b
                        dve.wait_ge(kept_s, kv * len(SIDE) + SIDE.index(n) + 1)
                        dve.scalar_tensor_tensor(out=silu[:, h, b * T:(b + 1) * T], in0=th[:, b, :], scalar=1.0,
                                                 in1=silu[:, h, b * T:(b + 1) * T], op0=ALU.add,
                                                 op1=ALU.mult).then_inc(gate_done, 1)
                dve.wait_ge(kt_done, kv + 1)
                for half in range(2):
                    last = dve.tensor_copy(ktm[:, half * 4:(half + 1) * 4, :].rearrange("p i e -> p (i e)"),
                                           ps[:, 6 + half, :])
                last.then_inc(ktm_done, 1)
                dve.wait_ge(dec_done, kv + 1)
                dve.wait_ge(erow_done, kv + 1)
                dve.wait_ge(gate_done, (kv + 1) * (R * B))
                for t in range(NT):
                    c = t % QT
                    T1 = kv * NT + t + 1
                    dve.wait_ge(s_done, T1)
                    dve.tensor_tensor(sc[:, :], ps[:, 0, :], dec[:, t, :], ALU.mult).then_inc(sc_done, 1)
                    dve.wait_ge(cs_done, T1)
                    if c == 0:
                        last = dve.tensor_copy(state[:, :], ps[:, 2, :])
                    else:
                        for h in range(R):
                            last = dve.scalar_tensor_tensor(
                                out=state[:, h * P:(h + 1) * P], in0=state[:, h * P:(h + 1) * P],
                                scalar=rows[:, h, (t + 1) * P - 1:(t + 1) * P], in1=ps[:, 2, h * P:(h + 1) * P],
                                op0=ALU.mult, op1=ALU.add)
                    last.then_inc(st_done, 1)
                    dve.wait_ge(rms_done, T1)
                    chain(dve.reciprocal(rms[:, :], rms[:, :]), NSTEP)
                    chain(dve.scalar_tensor_tensor(out=y2[:, :], in0=ps[:, 1, :], scalar=gw[:, 0:1], in1=rms[:, :],
                                                   op0=ALU.mult, op1=ALU.mult), NSTEP)
                    dve.tensor_tensor(ry[:, :].rearrange("p (h n) -> p h n", h=R),
                                      y2[:, :].rearrange("p (h n) -> p h n", h=R), silu[:, :, t * P:(t + 1) * P],
                                      ALU.mult).then_inc(ry_done, 1)
                    dve.wait_ge(z_done, T1)
                    dve.tensor_tensor(mixed[:, t, :], mixed[:, t, :], ps[:, 4, :], ALU.add).then_inc(added, 1)
                assert count[0] == NSTEP


def build(nc, ins, out):
    ctx = ExitStack()
    with ctx:
        core = Core(nc, ctx, ins)
        load_inputs(core)

        layernorm(core, "ln0")
        with Stage(core, "mix0") as st:
            oT = st.sb("oT", [P, KC, N])
            attention(core, "l0", oT, G=4, E=16, scale=0.25, denominator=1.0, causal=True, shared_kv=True)
            project_out(core, "out0", oT, KC, P, ins["l0_wo"])
        experts(core, "ffn0")

        layernorm(core, "ln1")
        with Stage(core, "mix1") as st:
            lw = st.sb("lw", [P, NT, 32])
            wst = st.sb("wst", [P, NT, 32])
            rows_d = nc.dram_tensor("decay_rows", [8, 4, N], F32).ap()
            decays(core, "dec1", rows_d.rearrange("k h n -> (k h) n"), lw, None, wst)
            retention(core, "ret1", rows_d, lw, wst)
        with Stage(core, "gate1") as st:
            zT = st.sb("zT", [32, N])
            lora_top1(core, "top1", zT)
            dense_gate(core, "ffn1", ins["l1_wup"], zT, 32, ins["l1_zw"])

        layernorm(core, "ln2")
        with Stage(core, "mix2") as st:
            oT = st.sb("oT", [P, KC, N])
            attention(core, "l2", oT, G=4, E=16, scale=0.25, denominator=1.0, causal=True, shared_kv=False,
                      qk_bias=ins["l2_qkb"], v_bias=ins["l2_vb"])
            project_out(core, "out2", oT, KC, P, ins["l2_wo"], ins["l2_bo"])
        with Stage(core, "gate2") as st:
            zT = st.sb("zT", [49, N])
            lora_by_batch(core, "byb2", zT)
            dense_gate(core, "ffn2", ins["l2_w"], zT, 49, ins["l2_zw"])

        layernorm(core, "ln3")
        with Stage(core, "mix3") as st:
            oT = st.sb("oT", [P, 1, N])
            attention(core, "l3", oT, G=1, E=8, scale=1.0, denominator=8.0, causal=False, shared_kv=False,
                      qk_bias=ins["l3_qkb"], v_bias=ins["l3_vb"])
            project_out(core, "out3", oT, 1, 64, ins["l3_wo"], ins["l3_bo"])
        signed_gate(core, "ffn3", ins["l3_k"], ins["ei"], ins["l3_scale"], out)


def signed_gate(core, name, k_d, ei_d, scale_d, out_d):
    ps, xnT = core.ps, core.xnT
    with Stage(core, name) as st:
        k8 = st.sb("k8", [P, KC, D], mybir.dt.uint8)
        ei = st.sb("ei", [P, KC])
        w = st.sb("w", [P, KC, D])
        sc = st.sb("sc", [P, 1])
        f = st.sb("f", [P, 2, D])
        th = st.sb("th", [P, 2, D])
        gated = st.sb("gated", [P, D])
        loaded, made, done, f_done, tanh_done, x_done, step, stored = (
            st.sem("loaded"), st.sem("made"), st.sem("done"), st.sem("f_done"), st.sem("tanh_done"),
            st.sem("x_done"), st.sem("step"), st.sem("stored"))
        block = st.block()

        @block.sync
        def _(sp):
            sp.dma_start(k8[:, :, :], k_d).then_inc(loaded, 16)
            sp.dma_start(ei[:, :], ei_d).then_inc(loaded, 16)
            sp.dma_start(sc[:, :], scale_d.partition_broadcast(P)).then_inc(loaded, 16)
            for t in range(NT):
                sp.wait_ge(x_done, t + 1)
                sp.dma_start(out_d[t * P:(t + 1) * P, :], core.x[:, t, :]).then_inc(stored, 16)
            sp.wait_ge(stored, 16 * NT)

        @block.tensor
        def _(pe):
            pe.wait_ge(made, KC)
            for t in range(NT):
                for c in range(KC):
                    last = pe.matmul(ps[:, t, :], xnT[:, c, t * P:(t + 1) * P], w[:, c, :],
                                     start=(c == 0), stop=(c == KC - 1))
                last.then_inc(done, 1)

        @block.scalar
        def _(act):
            act.wait_ge(loaded, 48)
            for t in range(NT):
                act.wait_ge(done, t + 1)
                if t >= 2:
                    act.wait_ge(x_done, t - 1)
                act.activation(f[:, t % 2, :], ps[:, t, :], ACT.Copy, scale=sc[:, 0:1]).then_inc(f_done, 1)
                act.wait_ge(f_done, t + 1)
                act.activation(th[:, t % 2, :], f[:, t % 2, :], ACT.Tanh, scale=0.5).then_inc(tanh_done, 1)

        @block.vector
        def _(dve):
            chain = Chain(dve, step)
            dve.wait_ge(loaded, 48)
            for c in range(KC):
                dve.tensor_scalar(w[:, c, :], k8[:, c, :], ei[:, c:c + 1], None, ALU.mult).then_inc(made, 1)
            for t in range(NT):
                dve.wait_ge(tanh_done, t + 1)
                gate_steps(core, None, dve, t, f[:, t % 2, :], th[:, t % 2, :], gated[:, :], chain, x_done)
                dve.wait_ge(x_done, t + 1)


def laid_out(inputs):
    import numpy as np

    a = {k: np.asarray(v) for k, v in inputs.items()}
    f32 = np.float32

    def chunks(w):
        return np.ascontiguousarray(w.reshape(-1, P, w.shape[1]).transpose(1, 0, 2))

    def groups(w, n):
        k, m = w.shape
        return np.ascontiguousarray(w.reshape(k // P, P, m // n, n).transpose(2, 1, 0, 3))

    d = {"x": a["L0_attn_x"].reshape(N, D)}
    d["l0_wq"] = groups(a["L0_attn_wq"], P)
    d["l0_wk"] = chunks(np.tile(a["L0_attn_wk"], (1, U)))
    d["l0_wv"] = chunks(a["L0_attn_wv"])
    d["l0_wo"] = chunks(a["L0_attn_wo"])
    d["l0_wgate"] = chunks(a["L0_ffn_W_gate"])
    d["l0_bgate"] = a["L0_ffn_b_gate"]
    d["l0_we"] = np.ascontiguousarray(a["L0_ffn_W_e"].reshape(8, KC, P, D).transpose(0, 2, 1, 3))
    d["l0_be"] = a["L0_ffn_b_e"]
    d["l1_wq"] = groups(a["L1_attn_Wq"].T, 4 * P)
    d["l1_wg"] = groups(a["L1_attn_Wg"].T, 4 * P)
    d["l1_wk"] = groups(a["L1_attn_Wk"].T, P)
    d["l1_wv"] = groups(a["L1_attn_Wv"].T, P)
    d["l1_wo"] = np.ascontiguousarray(a["L1_attn_Wo"].T.reshape(8, 4, P, D).transpose(0, 2, 1, 3))
    d["l1_win"] = chunks(a["L1_attn_Win"].T)
    d["l1_dtb"] = a["L1_attn_dt_bias"]
    d["l1_ab"] = a["L1_attn_A_log_bias"]
    d["l1_gw"] = a["L1_attn_gnorm_w"].reshape(P, 1)
    d["l1_wup"] = chunks(a["L1_ffn_W_up"].T)
    d["l1_wz"] = chunks(np.concatenate([a["L1_ffn_gate_w"], a["L1_ffn_lora_A"].reshape(32, D)], 0).T)
    d["l1_bz"] = a["L1_ffn_expert_bias"]
    d["l1_zw"] = np.ascontiguousarray(a["L1_ffn_lora_B"].transpose(0, 2, 1).reshape(32, D))
    for n, k in (("q", "Wq"), ("k", "Wk"), ("v", "Wv")):
        d["l2_w" + n] = groups(a["L2_attn_" + k].T, P)
    d["l2_qkb"] = np.ascontiguousarray(np.stack([a["L2_attn_bq"].reshape(4, P), a["L2_attn_bk"].reshape(4, P)], 2))
    d["l2_vb"] = a["L2_attn_bv"].reshape(4, P)
    d["l2_wo"] = chunks(a["L2_attn_Wo"].T)
    d["l2_bo"] = a["L2_attn_bo"]
    d["l2_w"] = chunks(a["L2_ffn_weight"].T)
    d["l2_wz"] = chunks(a["L2_ffn_lora_A"].reshape(48, D).T)
    d["l2_zw"] = np.concatenate([a["L2_ffn_lora_B"].transpose(0, 2, 1).reshape(48, D), a["L2_ffn_bias"][None]], 0)
    d["l2_starts"] = a["L2_ffn_lora_start_indices"]
    qk = a["L3_attn_Wqk_w"].reshape(64, 2, D)
    qkb = a["L3_attn_Wqk_b"].reshape(64, 2)
    pad = np.zeros((64, D), f32)
    d["l3_wq"] = groups(np.concatenate([qk[:, 0], pad], 0).T, P)
    d["l3_wk"] = groups(np.concatenate([qk[:, 1], pad], 0).T, P)
    d["l3_wv"] = groups(a["L3_attn_Wv_w"].T, 64)
    d["l3_qkb"] = np.concatenate([qkb, np.zeros((64, 2), f32)], 0)[None]
    d["l3_vb"] = a["L3_attn_Wv_b"].reshape(1, 64)
    d["l3_wo"] = np.ascontiguousarray(a["L3_attn_Wo_w"].T).reshape(64, 1, D)
    d["l3_bo"] = a["L3_attn_Wo_b"]
    d["l3_k"] = np.ascontiguousarray(a["L3_ffn_kernel"].reshape(KC, P, D).transpose(1, 0, 2))
    d["l3_scale"] = a["L3_ffn_scale"].reshape(1)
    i, j = np.arange(P)[:, None], np.arange(P)[None, :]
    d["ident"] = np.eye(P, dtype=f32)
    d["masks"] = np.ascontiguousarray(np.stack([np.where(j > i, NEG, 0), np.where(i > j, NEG, 0)], 1).astype(f32))
    d["minus1"] = np.ascontiguousarray(
        np.broadcast_to(-np.eye(P, U, dtype=f32)[:, :, None], (P, U, P)))
    for E in (16, 8):
        d[f"headmask{E}"] = (np.arange(P)[:, None] // E == np.arange(U)[None]).astype(f32)
    d["tri"] = (i <= j).astype(f32)
    d["limit"] = np.where(j >= i, 80.0, NEG).astype(f32)
    d["iota8"] = np.arange(8, dtype=f32)
    d["adapter_of_row"] = (np.arange(P, dtype=f32) // 16).astype(f32).reshape(P, 1)
    inv = 1.0 / 10000.0 ** (np.arange(0, P, 2, dtype=f32) / f32(P))
    ang = np.arange(T, dtype=f32)[None, :] * inv.astype(f32)[:, None]
    d["cos"] = np.concatenate([np.cos(ang), np.cos(ang)], 0).astype(f32)
    d["sin"] = np.concatenate([-np.sin(ang), np.sin(ang)], 0).astype(f32)
    ex = round(D * 0.8)
    d["ei"] = np.where(np.arange(D) < ex, 1.0, -0.8 / (1.0 - 0.8)).astype(f32).reshape(KC, P).T.copy()
    return d


def kernel(**inputs):
    import numpy as np
    import concourse.bacc as bacc
    from concourse.bass_utils import run_bass_kernel_spmd

    nc = bacc.Bacc("TRN2", target_bir_lowering=False, num_devices=1)
    arrays, ins = {}, {}
    for name, array in laid_out(inputs).items():
        arrays[f"in_{name}"] = array = np.ascontiguousarray(array)
        ins[name] = nc.dram_tensor(f"in_{name}", array.shape, mybir.dt.from_np(array.dtype), kind="ExternalInput").ap()
    out = nc.dram_tensor("out_x", (N, D), F32, kind="ExternalOutput").ap()
    build(nc, ins, out)
    result = run_bass_kernel_spmd(nc, [arrays], core_ids=[0])
    return result.results[0]["out_x"].reshape(B, T, D)
```

```python
from contextlib import ExitStack

import concourse.bass as bass
from concourse import mybir

F32 = mybir.dt.float32
F32R = mybir.dt.float32r
BF16 = mybir.dt.bfloat16
I32 = mybir.dt.int32
U32 = mybir.dt.uint32
ALU = mybir.AluOpType
ACT = mybir.ActivationFunctionType
AX = mybir.AxisListType

P = 128
B = 2
T = 512
N = B * T
NT = N // P
QT = T // P
D = 512
KC = D // P
EPS = 1e-5
NEG = -1e30
U = 8


class Core:

    def __init__(self, nc, ctx, ins):
        self.nc = nc
        self.ins = ins
        self.x = ctx.enter_context(nc.sbuf_tensor("x_sb", [P, NT, D], F32))
        self.xh = ctx.enter_context(nc.sbuf_tensor("xnT_high", [P, KC, N], F32R))
        self.xl = ctx.enter_context(nc.sbuf_tensor("xnT_low", [P, KC, N], F32R))
        self.mixed = ctx.enter_context(nc.sbuf_tensor("mixed", [P, NT, D], F32))
        self.ident = ctx.enter_context(nc.sbuf_tensor("ident", [P, P], F32))
        self.identb = ctx.enter_context(nc.sbuf_tensor("identb", [P, P], BF16))
        self.ps = ctx.enter_context(nc.psum_tensor("banks", [P, 8, 512], F32))


class Stage:

    def __init__(self, core, name):
        self.core, self.nc, self.name = core, core.nc, name
        self.ctx, self.sems = ExitStack(), []

    def __enter__(self):
        return self

    def __exit__(self, *a):
        self.ctx.close()
        if self.sems:
            self.nc.clear_and_free_semaphores(self.sems)
            self.nc.all_engine_barrier()

    def sb(self, name, shape, dt=F32):
        return self.ctx.enter_context(self.nc.sbuf_tensor(f"{self.name}_{name}", shape, dt))

    def sem(self, name):
        self.sems.append(self.nc.alloc_semaphore(f"{self.name}_{name}"))
        return self.sems[-1]

    def block(self):
        return self.ctx.enter_context(self.nc.Block())


def f32(ap):
    return ap.bitcast(F32)


def product(pe, out, lhs, rhs, start=True, stop=True):
    n = len(lhs)
    for c in range(n):
        (lh, ll), (rh, rl) = lhs[c], rhs[c]
        pe.matmul(out, lh, rh, start=(start and c == 0), stop=False)
        pe.matmul(out, lh, rl, start=False, stop=False)
        last = pe.matmul(out, ll, rh, start=False, stop=(stop and c == n - 1))
    return last


def xrows(core, t0, n):
    return [(core.xh[:, c, t0:t0 + n], core.xl[:, c, t0:t0 + n]) for c in range(KC)]


class Chain:

    def __init__(self, eng, sem):
        self.eng, self.sem, self.n = eng, sem, 0

    def __call__(self, ins):
        self.n += 1
        ins.then_inc(self.sem, 1)
        self.eng.wait_ge(self.sem, self.n)


def load_inputs(core):
    with Stage(core, "load") as st:
        loaded, made = st.sem("loaded"), st.sem("ident_made")
        block = st.block()

        @block.sync
        def _(sp):
            sp.dma_start(core.x[:, :, :], core.ins["x"].rearrange("(t p) d -> p t d", p=P)).then_inc(loaded, 16)
            sp.dma_start(core.ident[:, :], core.ins["ident"]).then_inc(loaded, 16)

        @block.vector
        def _(dve):
            dve.wait_ge(loaded, 32)
            dve.tensor_copy(core.identb[:, :], core.ident[:, :]).then_inc(made, 1)
            dve.wait_ge(made, 1)


def layernorm(core, name):
    x, ps = core.x, core.ps
    with Stage(core, name) as st:
        xn = st.sb("xn", [P, NT, D])
        stats = st.sb("stats", [P, NT, 6])
        mv = st.sb("mean_var", [P, NT, 2])
        var = st.sb("var", [P, NT])
        std = st.sb("std", [P, NT])
        rstd = st.sb("rstd", [P, NT])
        step, var_ready, std_ready = st.sem("step"), st.sem("var_ready"), st.sem("std_ready")
        xn_ready, turned, high_kept, low_kept = (st.sem("xn_ready"), st.sem("turned"), st.sem("high_kept"),
                                                 st.sem("low_kept"))
        block = st.block()

        def turned_tile(t):
            return ps[:, t, :].rearrange("p (c n) -> p c n", c=KC)

        @block.vector
        def _(dve):
            chain = Chain(dve, step)
            for t in range(NT):
                last = dve.bn_stats(stats[:, t, :], x[:, t, :])
            chain(last)
            for t in range(NT):
                last = dve.bn_aggr(mv[:, t, :], stats[:, t, :])
            chain(last)
            dve.tensor_scalar(var[:, :], mv[:, :, 1], EPS, None, ALU.add).then_inc(var_ready, 1)
            dve.wait_ge(std_ready, 1)
            chain(dve.reciprocal(rstd[:, :], std[:, :]))
            for t in range(NT):
                dve.tensor_scalar(xn[:, t, :], x[:, t, :], mv[:, t, 0:1], rstd[:, t:t + 1],
                                  ALU.subtract, ALU.mult).then_inc(xn_ready, 1)
            for t in range(NT):
                dve.wait_ge(high_kept, t + 1)
                dve.tensor_tensor(core.xl[:, :, t * P:(t + 1) * P], turned_tile(t),
                                  f32(core.xh[:, :, t * P:(t + 1) * P]), ALU.subtract).then_inc(low_kept, 1)

        @block.scalar
        def _(act):
            act.wait_ge(var_ready, 1)
            act.activation(std[:, :], var[:, :], ACT.Sqrt).then_inc(std_ready, 1)
            for t in range(NT):
                act.wait_ge(turned, t + 1)
                act.activation(core.xh[:, :, t * P:(t + 1) * P], turned_tile(t), ACT.Copy).then_inc(high_kept, 1)

        @block.tensor
        def _(pe):
            for t in range(NT):
                pe.wait_ge(xn_ready, t + 1)
                for c in range(KC):
                    last = pe.transpose(ps[:, t, c * P:(c + 1) * P], xn[:, t, c * P:(c + 1) * P], core.ident[:, :])
                last.then_inc(turned, 1)


def attention(core, name, oh, ol, G, E, scale, denominator, causal, shared_kv, qk_bias=None, v_bias=None):
    ins, ps = core.ins, core.ps
    W = E + 1
    M = U * E
    parts = 1 if causal else 2
    if causal:
        qside = [[(3, 0, 512), (2, 512, 384), (0, 896, 128), (1, 1024, 256)]]
        kside = [[(0, 0, 512), (1, 512, 384), (3, 896, 128), (2, 1024, 256)]]
    else:
        qside = kside = [[(0, 0, 512), (1, 512, 512)], [(2, 0, 512), (3, 512, 512)]]
    SIZE = 1280 if causal else 1024
    NU = U * parts
    LAG = 1
    NW = 1 if shared_kv else 3
    NB = (qk_bias is not None) + (v_bias is not None)
    VB = 2
    with Stage(core, name) as st:
        w = st.sb("w", [P, NW, KC, P])
        wh = st.sb("wh", [P, NW, KC, P], F32R)
        wl = st.sb("wl", [P, NW, KC, P], F32R)
        qh = st.sb("qh", [P, 2, T], F32R)
        ql = st.sb("ql", [P, 2, T], F32R)
        qf = st.sb("qf", [P, T])
        kf = st.sb("kf", [P, T])
        KS = B if shared_kv else 1
        kh = st.sb("kh", [P, KS, T], F32R)
        kl = st.sb("kl", [P, KS, T], F32R)
        kmh = st.sb("kmask_high", [P, U, T], F32R)
        kml = st.sb("kmask_low", [P, U, T], F32R)
        vaug = st.sb("vaug", [P, VB, QT, 1 if shared_kv else U, W])
        mcol = st.sb("mcol", [P, QT, P])
        mT = st.sb("mT", [P, T], BF16)
        probs = st.sb("probs", [P, 2, 1280 if causal else 2048])
        rec = st.sb("rec", [P, QT, U])
        o = st.sb("o", [P, QT, M])
        headmask = st.sb("headmask", [P, U])
        minus1b = st.sb("minus1b", [P, U, P], BF16)
        masks = st.sb("masks", [P, 2, P])
        masksb = st.sb("masksb", [P, 2, P], BF16)
        qkb = st.sb("qkb", [P, 2])
        vb = st.sb("vb", [P, M])

        consts_in, consts_made = st.sem("consts_in"), st.sem("consts_made")
        w_in, bias_in = st.sem("w_in"), st.sem("bias_in")
        w_high, w_low, freed = st.sem("w_high"), st.sem("w_low"), st.sem("freed")
        projected = st.sem("projected")
        q_full, q_high, q_low = st.sem("q_full"), st.sem("q_high"), st.sem("q_low")
        k_full, k_high, k_low, v_kept = st.sem("k_full"), st.sem("k_high"), st.sem("k_low"), st.sem("v_kept")
        k_masked = st.sem("k_masked")
        rows_scored, max_taken = st.sem("rows_scored"), st.sem("max_taken")
        max_turned, max_kept = st.sem("max_turned"), st.sem("max_kept")
        cols_scored, exp_done = st.sem("cols_scored"), st.sem("exp_done")
        pv_done, rec_done, normed = st.sem("pv_done"), st.sem("rec_done"), st.sem("normed")
        o_turned, o_high, o_kept = st.sem("o_turned"), st.sem("o_high"), st.sem("o_kept")
        kv_projected, kv_kept, kv_step = st.sem("kv_projected"), st.sem("kv_kept"), st.sem("kv_step")
        if shared_kv:
            wkv = st.sb("wkv", [P, KC, P + E])
            wkvh = st.sb("wkvh", [P, KC, P + E], F32R)
            wkvl = st.sb("wkvl", [P, KC, P + E], F32R)
        block = st.block()

        X = ps[:, 0:3, :].rearrange("p b n -> p (b n)")
        Y = ps[:, 3:6, :].rearrange("p b n -> p (b n)")
        OUT = ps[0:M, 2, :]

        def rounds(eng, turn):
            if G > 1:
                with eng.Fori(0, G - 1) as g:
                    for b in range(B):
                        turn(g, b, False)
            for b in range(B):
                turn(G - 1, b, b == B - 1)

        @block.sync
        def _(sp):
            sp.dma_start(headmask[:, :], ins[f"headmask{E}"]).then_inc(consts_in, 16)
            sp.dma_start(probs[:, 0, 0:U * P].rearrange("p (u n) -> p u n", u=U), ins["minus1"]).then_inc(consts_in, 16)
            sp.dma_start(masks[:, :, :], ins["masks"]).then_inc(consts_in, 16)
            if shared_kv:
                sp.dma_start(wkv[:, :, :], ins[name + "_wkv"]).then_inc(consts_in, 16)
            sp.dma_start(w[:, :, :, :], ins[name + "_wqkv"][0]).then_inc(w_in, 16)
            if NB:
                sp.dma_start(qkb[:, :], qk_bias[0]).then_inc(bias_in, 16)
                sp.dma_start(vb[:, :], v_bias[0].partition_broadcast(P)).then_inc(bias_in, 16)
            if G > 1:
                with sp.Fori(0, G - 1) as g:
                    sp.wait_ge(w_low, (g + 1) * NW)
                    sp.sem_inc(freed, 1)
                    sp.dma_start(w[:, :, :, :], ins[name + "_wqkv"][g + 1]).then_inc(w_in, 16)
                    if NB:
                        sp.wait_ge(k_low, (g + 1) * B)
                        sp.sem_inc(freed, 1)
                        sp.dma_start(qkb[:, :], qk_bias[g + 1]).then_inc(bias_in, 16)
                        sp.dma_start(vb[:, :], v_bias[g + 1].partition_broadcast(P)).then_inc(bias_in, 16)

        def split_low(eng, g):
            for i in range(NW):
                eng.wait_ge(w_high, g * NW + i + 1)
                eng.tensor_tensor(wl[:, i, :, :], w[:, i, :, :], f32(wh[:, i, :, :]), ALU.subtract).then_inc(w_low, 1)

        def split_high(act, g):
            act.wait_ge(w_in, g * 16 + 16)
            for i in range(NW):
                act.activation(wh[:, i, :, :], w[:, i, :, :], ACT.Copy).then_inc(w_high, 1)

        @block.gpsimd
        def _(pool):
            pool.wait_ge(consts_in, 48 + 16 * shared_kv)

            def mask(g, b, us, first):
                r = g * B + b
                pool.wait_ge(kv_kept if shared_kv else k_low, 6 if shared_kv else r + 1)
                for u in us:
                    if not first:
                        pool.wait_ge(cols_scored, (r - 1) * NU + (u + 1) * parts)
                    s = b if shared_kv else 0
                    m = headmask[:, u:u + 1].broadcast_to([P, T])
                    pool.tensor_tensor(kmh[:, u, :], f32(kh[:, s, :]), m, ALU.mult)
                    pool.tensor_tensor(kml[:, u, :], f32(kl[:, s, :]), m, ALU.mult).then_inc(k_masked, 1)

            split_low(pool, 0)
            mask(0, 0, range(U), True)

            def turn(g, b, last):
                if last:
                    return
                if b == 0:
                    mask(g, 1, range(U // 2), False)
                    if not (isinstance(g, int) and g == G - 1):
                        split_low(pool, g + 1)
                    mask(g, 1, range(U // 2, U), False)
                else:
                    mask(g + 1, 0, range(U), False)

            rounds(pool, turn)

        @block.tensor
        def _(pe):
            pe.wait_ge(consts_made, 4)

            def w_piece(i):
                return [(wh[:, i, c, :], wl[:, i, c, :]) for c in range(KC)]

            def project(g, b, first=False):
                r = g * B + b
                pe.wait_ge(w_low, g * NW + NW)
                if not first:
                    pe.wait_ge(max_taken, r * NU)
                last = product(pe, ps[:, 3, :], w_piece(0), xrows(core, b * T, T))
                if not shared_kv:
                    product(pe, ps[:, 4, :], w_piece(1), xrows(core, b * T, T))
                    for i in range(QT):
                        last = product(pe, ps[:, 5, i * M:(i + 1) * M], xrows(core, b * T + i * P, P),
                                       [(wh[:, 2, c, 0:M], wl[:, 2, c, 0:M]) for c in range(KC)])
                last.then_inc(projected, 1)

            def rows(g, b, n, S=Y, sets=1):
                r = g * B + b
                u, h = n // parts, n % parts
                if n == 0:
                    pe.wait_ge(q_low, r + 1)
                    if not shared_kv:
                        pe.wait_ge(k_full, r + 1)
                        pe.wait_ge(v_kept, r + 1)
                elif n >= sets:
                    pe.wait_ge(max_taken, r * NU + n + 1 - sets)
                pe.wait_ge(k_masked, r * U + u + 1)
                for i, off, size in qside[h]:
                    last = pe.matmul(S[:, off:off + size], qh[:, b, i * P:(i + 1) * P], kmh[:, u, 0:size],
                                     start=True, stop=not causal)
                    if causal:
                        last = pe.matmul(S[:, off + size - P:off + size], core.identb[:, :], masksb[:, 0, :],
                                         start=False, stop=True)
                last.then_inc(rows_scored, 1)

            def cols(g, b, n, first):
                r = g * B + b
                u, h = n // parts, n % parts
                if n == 0:
                    pe.wait_ge(max_kept, r + 1)
                else:
                    pe.wait_ge(exp_done, r * NU + n)
                for k, off, size in kside[h]:
                    if n == 0 and off == 2 * T and not first:
                        pe.wait_ge(o_kept, r)
                    q0 = T - size
                    out = X[:, off:off + size]
                    keys = slice(k * P, (k + 1) * P)
                    pe.matmul(out, kmh[:, u, keys], qh[:, b, q0:T], start=True, stop=False)
                    pe.matmul(out, kmh[:, u, keys], ql[:, b, q0:T], start=False, stop=False)
                    pe.matmul(out, kml[:, u, keys], qh[:, b, q0:T], start=False, stop=False)
                    last = pe.matmul(out, minus1b[:, u, :], mT[:, q0:T], start=False, stop=not causal)
                    if causal:
                        last = pe.matmul(X[:, off:off + P], core.identb[:, :], masksb[:, 1, :], start=False, stop=True)
                last.then_inc(cols_scored, 1)

            def weigh(g, b, u, first):
                r = g * B + b
                pe.wait_ge(exp_done, r * NU + (u + 1) * parts)
                if u == 0 and not first:
                    pe.wait_ge(normed, r)
                for i in range(QT):
                    lo = (i % 2) * U * W + u * W
                    keys = [k for k in range(QT) if k <= i or not causal]
                    for k in keys:
                        if causal:
                            off = next(off for kk, off, size in kside[0] if kk == k) + (i - k) * P
                        else:
                            off = k * T + i * P
                        last = pe.matmul(ps[:, 6 + i // 2, lo:lo + W], probs[:, u % 2, off:off + P],
                                         vaug[:, b, k, 0 if shared_kv else u, :],
                                         start=(k == keys[0]), stop=(k == keys[-1]))
                last.then_inc(pv_done, 1)

            def turn_out(r):
                pe.wait_ge(normed, r + 1)
                for i in range(QT):
                    last = pe.transpose(OUT[:, i * P:(i + 1) * P], o[:, i, :], core.ident[:, :])
                last.then_inc(o_turned, 1)

            def turn(g, b, last_round, first=False):
                r = g * B + b
                nxt = None if last_round else (g, 1) if b == 0 else (g + 1, 0)
                pe.wait_ge(max_taken, r * NU + NU)
                for i in range(QT):
                    last = pe.transpose(X[:, i * P:(i + 1) * P], mcol[:, i, :], core.ident[:, :])
                last.then_inc(max_turned, 1)
                if nxt:
                    project(*nxt)
                if not first:
                    turn_out(r - 1)
                for n in range(NU + LAG * parts):
                    if n < NU:
                        cols(g, b, n, first)
                    if n >= LAG * parts and nxt:
                        rows(*nxt, n - LAG * parts)
                    if n % parts == parts - 1 and parts <= n < NU + parts:
                        weigh(g, b, n // parts - 1, first)

            if shared_kv:
                pe.wait_ge(kv_step, 2)
                for b in range(B):
                    product(pe, ps[:, b, :], [(wkvh[:, c, 0:P], wkvl[:, c, 0:P]) for c in range(KC)],
                            xrows(core, b * T, T))
                for t in range(NT):
                    last = product(pe, ps[:, 2, t * E:(t + 1) * E], xrows(core, t * P, P),
                                   [(wkvh[:, c, P:P + E], wkvl[:, c, P:P + E]) for c in range(KC)])
                last.then_inc(kv_projected, 1)
            project(0, 0, first=True)
            if shared_kv:
                pe.wait_ge(kv_kept, 6)
            for n in range(NU):
                rows(0, 0, n, (Y, X)[n % 2], 2)
            if G == 1:
                turn(0, 0, False, first=True)
                turn(0, 1, True)
            else:
                turn(0, 0, False, first=True)
                turn(0, 1, False)
                if G > 2:
                    with pe.Fori(1, G - 1) as g:
                        for b in range(B):
                            turn(g, b, False)
                turn(G - 1, 0, False)
                turn(G - 1, 1, True)
            turn_out(G * B - 1)

        @block.scalar
        def _(act):
            if shared_kv:
                act.wait_ge(consts_in, 64)
                act.activation(wkvh[:, :, :], wkv[:, :, :], ACT.Copy).then_inc(kv_step, 1)
            split_high(act, 0)
            if shared_kv:
                act.wait_ge(kv_projected, 1)
                for b in range(B):
                    act.activation(kh[:, b, :], ps[:, b, :], ACT.Copy).then_inc(kv_kept, 1)

            def queries(g, b):
                r = g * B + b
                act.wait_ge(projected, r + 1)
                if qk_bias is not None:
                    act.wait_ge(bias_in, g * 32 + 32)
                    act.activation(qf[:, :], Y[:, 0:T], ACT.Identity, bias=qkb[:, 0:1]).then_inc(q_full, 1)
                    act.wait_ge(q_full, r + 1)
                    act.activation(qh[:, b, :], qf[:, :], ACT.Copy).then_inc(q_high, 1)
                else:
                    act.activation(qh[:, b, :], Y[:, 0:T], ACT.Copy).then_inc(q_high, 1)
                if not shared_kv:
                    act.wait_ge(k_full, r + 1)
                    act.activation(kh[:, 0, :], kf[:, :], ACT.Copy).then_inc(k_high, 1)

            def keep_out(g, b):
                r = g * B + b
                act.wait_ge(o_turned, r + 1)
                act.activation(oh[0:M, g, b * T:(b + 1) * T], OUT, ACT.Copy).then_inc(o_high, 1)

            def turn(g, b, last, first=False):
                r = g * B + b
                act.wait_ge(max_turned, r + 1)
                act.activation(mT[:, :], X[:, 0:T], ACT.Copy).then_inc(max_kept, 1)
                if not last:
                    queries(*((g, 1) if b == 0 else (g + 1, 0)))
                if not first:
                    keep_out(*((g - 1, 1) if b == 0 else (g, 0)))
                for n in range(NU):
                    act.wait_ge(cols_scored, r * NU + n + 1)
                    u, h = n // parts, n % parts
                    if u >= 2 and h == 0:
                        act.wait_ge(pv_done, r * U + u - 1)
                    act.activation(probs[:, u % 2, h * 1024:h * 1024 + SIZE], X[:, 0:SIZE], ACT.Exp,
                                   scale=scale).then_inc(exp_done, 1)
                    if n == 0 and b == 0 and not (isinstance(g, int) and g == G - 1):
                        split_high(act, g + 1)

            queries(0, 0)
            turn(0, 0, False, first=True)
            turn(0, 1, G == 1)
            if G > 1:
                if G > 2:
                    with act.Fori(1, G - 1) as g:
                        for b in range(B):
                            turn(g, b, False)
                turn(G - 1, 0, False)
                turn(G - 1, 1, True)
            keep_out(G - 1, 1)

        @block.vector
        def _(dve):
            dve.memset(mcol[:, :, :], 0.0).then_inc(consts_made, 1)
            dve.memset(vaug[:, :, :, :, :], denominator).then_inc(consts_made, 1)
            dve.wait_ge(consts_in, 48 + 16 * shared_kv)
            dve.tensor_copy(minus1b[:, :, :], probs[:, 0, 0:U * P].rearrange("p (u n) -> p u n", u=U)).then_inc(consts_made, 1)
            dve.tensor_copy(masksb[:, :, :], masks[:, :, :]).then_inc(consts_made, 1)
            dve.wait_ge(consts_made, 2)
            if shared_kv:
                dve.wait_ge(kv_step, 1)
                dve.tensor_tensor(wkvl[:, :, :], wkv[:, :, :], f32(wkvh[:, :, :]), ALU.subtract).then_inc(kv_step, 1)
                dve.wait_ge(kv_projected, 1)
                for b in range(B):
                    dve.tensor_copy(vaug[:, b, :, 0, 0:E], ps[:, 2, b * QT * E:(b + 1) * QT * E]
                                    .rearrange("p (i e) -> p i e", i=QT)).then_inc(kv_kept, 1)
                dve.wait_ge(kv_kept, 4)
                for b in range(B):
                    dve.tensor_tensor(kl[:, b, :], ps[:, b, :], f32(kh[:, b, :]), ALU.subtract).then_inc(kv_kept, 1)

            def projections(g, b):
                r = g * B + b
                if not shared_kv:
                    dve.wait_ge(projected, r + 1)
                    if qk_bias is not None:
                        dve.wait_ge(bias_in, g * 32 + 32)
                    dve.tensor_scalar(kf[:, :], Y[:, T:2 * T], qkb[:, 1:2], None, ALU.add).then_inc(k_full, 1)
                    for i in range(QT):
                        last = dve.tensor_tensor(vaug[:, b, i, :, 0:E],
                                                 Y[:, 2 * T + i * M:2 * T + (i + 1) * M].rearrange("p (u e) -> p u e", u=U),
                                                 vb[:, :].rearrange("p (u e) -> p u e", u=U), ALU.add)
                    dve.wait_ge(k_full, r + 1)
                dve.wait_ge(q_high, r + 1)
                dve.tensor_tensor(ql[:, b, :], qf[:, :] if qk_bias is not None else Y[:, 0:T], f32(qh[:, b, :]),
                                  ALU.subtract).then_inc(q_low, 1)
                if not shared_kv:
                    last.then_inc(v_kept, 1)
                    dve.wait_ge(k_high, r + 1)
                    dve.tensor_tensor(kl[:, 0, :], kf[:, :], f32(kh[:, 0, :]), ALU.subtract).then_inc(k_low, 1)

            def maxima(g, b, n, S=Y):
                dve.wait_ge(rows_scored, (g * B + b) * NU + n + 1)
                u, h = n // parts, n % parts
                for i, off, size in qside[h]:
                    last = dve.reduce_max(mcol[:, i, u:u + 1], S[:, off:off + size], AX.X)
                last.then_inc(max_taken, 1)

            def low_out(g, b):
                r = g * B + b
                dve.wait_ge(o_high, r + 1)
                dve.tensor_tensor(ol[0:M, g, b * T:(b + 1) * T], OUT,
                                  f32(oh[0:M, g, b * T:(b + 1) * T]), ALU.subtract).then_inc(o_kept, 1)

            def turn(g, b, last_round, first=False):
                r = g * B + b
                nxt = None if last_round else (g, 1) if b == 0 else (g + 1, 0)
                if nxt:
                    projections(*nxt)
                if not first:
                    low_out(*((g - 1, 1) if b == 0 else (g, 0)))
                if nxt:
                    for n in range(NU):
                        maxima(*nxt, n)
                dve.wait_ge(pv_done, r * U + U)
                for half in range(2):
                    pv = ps[:, 6 + half, 0:2 * U * W].rearrange("p (n e) -> p n e", e=W)
                    last = dve.reciprocal(rec[:, 2 * half:2 * half + 2, :].rearrange("p i u -> p (i u)"), pv[:, :, E])
                last.then_inc(rec_done, 1)
                dve.wait_ge(rec_done, r + 1)
                for half in range(2):
                    pv = ps[:, 6 + half, 0:2 * U * W].rearrange("p (n e) -> p n e", e=W)
                    rb = rec[:, 2 * half:2 * half + 2, :].rearrange("p i u -> p (i u)").unsqueeze(2)
                    last = dve.tensor_tensor(
                        o[:, 2 * half:2 * half + 2, :].rearrange("p i (u e) -> p (i u) e", u=U),
                        pv[:, :, 0:E], rb.broadcast_to([P, 2 * U, E]), ALU.mult)
                last.then_inc(normed, 1)

            projections(0, 0)
            for n in range(NU):
                maxima(0, 0, n, (Y, X)[n % 2])
            turn(0, 0, False, first=True)
            turn(0, 1, G == 1)
            if G > 1:
                if G > 2:
                    with dve.Fori(1, G - 1) as g:
                        for b in range(B):
                            turn(g, b, False)
                turn(G - 1, 0, False)
                turn(G - 1, 1, True)
            low_out(G - 1, 1)


def project_out(core, name, oh, ol, G, M, w_d, bias_d=None):
    ps, mixed = core.ps, core.mixed
    with Stage(core, name) as st:
        w = st.sb("w", [M, G, D])
        wh = st.sb("wh", [M, G, D], F32R)
        wl = st.sb("wl", [M, G, D], F32R)
        bias = st.sb("bias", [P, D])
        w_in, done, w_high, w_low = st.sem("w_in"), st.sem("done"), st.sem("w_high"), st.sem("w_low")
        kept = st.sem("kept_v"), st.sem("kept_s")
        block = st.block()

        @block.sync
        def _(sp):
            for g in range(G):
                sp.dma_start(w[:, g, :], w_d[:, g, :]).then_inc(w_in, 16)
                sp.wait_ge(w_in, 16 * (g + 1))
            if bias_d is not None:
                sp.dma_start(bias[:, :], bias_d.partition_broadcast(P)).then_inc(w_in, 16)

        @block.tensor
        def _(pe):
            pe.wait_ge(w_low, G)
            for t in range(NT):
                product(pe, ps[:, t, :], [(oh[0:M, g, t * P:(t + 1) * P], ol[0:M, g, t * P:(t + 1) * P]) for g in range(G)],
                        [(wh[:, g, :], wl[:, g, :]) for g in range(G)]).then_inc(done, 1)

        @block.vector
        def _(dve):
            for g in range(G):
                dve.wait_ge(w_high, g + 1)
                dve.tensor_tensor(wl[:, g, :], w[:, g, :], f32(wh[:, g, :]), ALU.subtract).then_inc(w_low, 1)
            if bias_d is not None:
                dve.wait_ge(w_in, 16 * (G + 1))
            for t in range(NT) if bias_d is not None else range(0, NT, 2):
                dve.wait_ge(done, t + 1)
                if bias_d is not None:
                    dve.tensor_tensor(mixed[:, t, :], ps[:, t, :], bias[:, :], ALU.add).then_inc(kept[0], 1)
                else:
                    dve.tensor_copy(mixed[:, t, :], ps[:, t, :]).then_inc(kept[0], 1)

        @block.scalar
        def _(act):
            for g in range(G):
                act.wait_ge(w_in, 16 * (g + 1))
                act.activation(wh[:, g, :], w[:, g, :], ACT.Copy).then_inc(w_high, 1)
            if bias_d is None:
                for t in range(1, NT, 2):
                    act.wait_ge(done, t + 1)
                    act.activation(mixed[:, t, :], ps[:, t, :], ACT.Copy).then_inc(kept[1], 1)


def gate_steps(core, eng_wait, dve, t, f, th, gated, chain, x_done):
    chain(dve.scalar_tensor_tensor(out=gated, in0=th, scalar=1.0, in1=f, op0=ALU.add, op1=ALU.mult))
    chain(dve.scalar_tensor_tensor(out=gated, in0=gated, scalar=0.5, in1=core.mixed[:, t, :],
                                   op0=ALU.mult, op1=ALU.mult))
    dve.tensor_tensor(core.x[:, t, :], core.x[:, t, :], gated, ALU.add).then_inc(x_done, 1)


def experts(core, name):
    ins, ps = core.ins, core.ps
    NE = 8
    with Stage(core, name) as st:
        wg = st.sb("wg", [P, KC, NE])
        wgh = st.sb("wgh", [P, KC, NE], F32R)
        wgl = st.sb("wgl", [P, KC, NE], F32R)
        bg = st.sb("bg", [P, NE])
        we = st.sb("we", [P, 2, KC, D])
        weh = st.sb("weh", [P, 2, KC, D], F32R)
        wel = st.sb("wel", [P, 2, KC, D], F32R)
        be = st.sb("be", [P, 2, D])
        logits = st.sb("logits", [P, NT, NE])
        best = st.sb("best", [P, NT, 8])
        where = st.sb("where", [P, NT, 8], U32)
        wheref = st.sb("wheref", [P, NT, 8])
        iota = st.sb("iota", [P, NE])
        pick = st.sb("pick", [P, 2, NT, NE])
        share = st.sb("share", [P, NT, NE])
        now = st.sb("now", [P, 2, NT])
        biased = st.sb("biased", [P, 2, D])
        acted = st.sb("acted", [P, 2, D])
        f = st.sb("f", [P, NT, D])
        th = st.sb("th", [P, 2, D])
        gated = st.sb("gated", [P, D])
        step, consts_in = st.sem("step"), st.sem("consts_in")
        w_in = st.sem("w_in0"), st.sem("w_in1")
        w_high, w_low, gate_split = st.sem("w_high"), st.sem("w_low"), st.sem("gate_split")
        b_used, freed = st.sem("b_used"), st.sem("freed")
        logits_done, mm_done, biased_done, acted_done, summed = (
            st.sem("logits_done"), st.sem("mm_done"), st.sem("biased_done"), st.sem("acted_done"), st.sem("summed"))
        cleared, now_done = st.sem("cleared"), st.sem("now_done")
        tanh_done, x_done = st.sem("tanh_done"), st.sem("x_done")
        block = st.block()

        def each(eng, one):
            one(0, 0, True, False)
            one(0, 1, True, False)
            with eng.Fori(1, NE // 2 - 1) as j:
                for s in range(2):
                    one(j, s, False, False)
            one(NE // 2 - 1, 0, False, False)
            one(NE // 2 - 1, 1, False, True)

        @block.sync
        def _(sp):
            sp.dma_start(wg[:, :, :], ins["l0_wgate"]).then_inc(consts_in, 16)
            sp.dma_start(bg[:, :], ins["l0_bgate"].partition_broadcast(P)).then_inc(consts_in, 16)
            sp.dma_start(iota[:, :], ins["iota8"].partition_broadcast(P)).then_inc(consts_in, 16)

            def load(j, s, first, last):
                e = j * 2 + s
                if not first:
                    sp.wait_ge(w_low, (e - 1) * KC)
                    sp.sem_inc(freed, 1)
                    sp.wait_ge(b_used, e - 1)
                    sp.sem_inc(freed, 1)
                sp.dma_start(we[:, s, :, :], ins["l0_we"][e]).then_inc(w_in[s], 16)
                sp.dma_start(be[:, s, :], ins["l0_be"][e].partition_broadcast(P)).then_inc(w_in[s], 16)

            each(sp, load)

        @block.tensor
        def _(pe):
            pe.wait_ge(gate_split, 2)
            for t in range(NT):
                last = product(pe, ps[:, 7, t * NE:(t + 1) * NE], xrows(core, t * P, P),
                               [(wgh[:, c, :], wgl[:, c, :]) for c in range(KC)])
            last.then_inc(logits_done, 1)

            def compute(j, s, first, last):
                e = j * 2 + s
                pe.wait_ge(w_low, e * KC + KC)
                for t in range(NT):
                    n = s * NT + t
                    if not first or n >= 4:
                        pe.wait_ge(biased_done, e * NT + t - 3)
                    product(pe, ps[:, n % 4, :], xrows(core, t * P, P),
                            [(weh[:, s, c, :], wel[:, s, c, :]) for c in range(KC)]).then_inc(mm_done, 1)

            each(pe, compute)

        @block.vector
        def _(dve):
            chain = Chain(dve, step)
            dve.wait_ge(consts_in, 48)
            dve.wait_ge(gate_split, 1)
            dve.tensor_tensor(wgl[:, :, :], wg[:, :, :], f32(wgh[:, :, :]), ALU.subtract).then_inc(gate_split, 1)
            dve.wait_ge(logits_done, 1)
            chain(dve.tensor_tensor(logits[:, :, :], ps[:, 7, 0:NT * NE].rearrange("p (t e) -> p t e", e=NE),
                                    bg[:, :].unsqueeze(1).broadcast_to([P, NT, NE]), ALU.add))
            for t in range(NT):
                last = dve.max(best[:, t, :], logits[:, t, :])
            chain(last)
            for t in range(NT):
                last = dve.max_index(where[:, t, :], best[:, t, :], logits[:, t, :])
            chain(last)
            chain(dve.tensor_copy(wheref[:, :, :], where[:, :, :]))
            for k in range(2):
                last = dve.tensor_tensor(pick[:, k, :, :], iota[:, :].unsqueeze(1).broadcast_to([P, NT, NE]),
                                         wheref[:, :, k:k + 1].broadcast_to([P, NT, NE]), ALU.is_equal)
            chain(last)
            chain(dve.tensor_tensor(share[:, :, :], pick[:, 0, :, :], pick[:, 1, :, :], ALU.add))
            chain(dve.tensor_scalar(share[:, :, :], share[:, :, :], 0.5, None, ALU.mult))

            def add_bias(j, s, first, last):
                e = j * 2 + s
                if not first:
                    dve.wait_ge(acted_done, (e - 1) * NT)
                dve.tensor_copy(now[:, s, :].unsqueeze(2), share[:, :, bass.ds(e, 1)]).then_inc(now_done, 1)
                dve.wait_ge(w_in[s], j * 32 + 32)
                for t in range(NT):
                    n = s * NT + t
                    dve.wait_ge(mm_done, e * NT + t + 1)
                    if not first or n >= 2:
                        dve.wait_ge(acted_done, e * NT + t - 1)
                    dve.tensor_tensor(biased[:, t % 2, :], ps[:, n % 4, :], be[:, s, :], ALU.add).then_inc(biased_done, 1)
                dve.wait_ge(biased_done, e * NT + NT)
                dve.sem_inc(b_used, 1)

            each(dve, add_bias)
            for t in range(NT):
                dve.wait_ge(tanh_done, t + 1)
                gate_steps(core, None, dve, t, f[:, t, :], th[:, t % 2, :], gated[:, :], chain, x_done)
                dve.wait_ge(x_done, t + 1)

        @block.scalar
        def _(act):
            def split(e1, s1, c):
                act.activation(weh[:, s1, c, :], we[:, s1, c, :], ACT.Copy).then_inc(w_high, 1)

            act.wait_ge(consts_in, 48)
            act.activation(wgh[:, :, :], wg[:, :, :], ACT.Copy).then_inc(gate_split, 1)
            act.wait_ge(w_in[0], 32)
            for c in range(KC):
                split(0, 0, c)

            def activate(j, s, first, last):
                e = j * 2 + s
                if not last:
                    act.wait_ge(w_in[1 - s], j * 32 + 32 + 32 * s)
                    if not (first and s == 0):
                        act.wait_ge(mm_done, e * NT)
                act_now = now[:, s, :]
                act.wait_ge(now_done, e + 1)
                for t in range(NT):
                    n = s * NT + t
                    if not last and t % 2 == 0:
                        split(None, 1 - s, t // 2)
                    act.wait_ge(biased_done, e * NT + t + 1)
                    if not first or n >= 2:
                        act.wait_ge(summed, e * NT + t - 1)
                    act.activation(acted[:, t % 2, :], biased[:, t % 2, :], ACT.Relu,
                                   scale=act_now[:, t:t + 1]).then_inc(acted_done, 1)

            each(act, activate)
            for t in range(NT):
                act.wait_ge(summed, NE * NT)
                if t >= 2:
                    act.wait_ge(x_done, t - 1)
                act.activation(th[:, t % 2, :], f[:, t, :], ACT.Tanh, scale=0.5).then_inc(tanh_done, 1)

        @block.gpsimd
        def _(pool):
            def low(e1, s1, c):
                pool.wait_ge(w_high, e1 * KC + c + 1)
                pool.tensor_tensor(wel[:, s1, c, :], we[:, s1, c, :], f32(weh[:, s1, c, :]),
                                   ALU.subtract).then_inc(w_low, 1)

            for c in range(KC):
                low(0, 0, c)
            pool.memset(f[:, :, :], 0.0).then_inc(cleared, 1)
            pool.wait_ge(cleared, 1)

            def add(j, s, first, last):
                e = j * 2 + s
                for t in range(NT):
                    if not last and t % 2 == 0:
                        low(e + 1, 1 - s, t // 2)
                    pool.wait_ge(acted_done, e * NT + t + 1)
                    if not first or s == 1:
                        pool.wait_ge(summed, e * NT + t - NT + 1)
                    pool.tensor_tensor(f[:, t, :], f[:, t, :], acted[:, t % 2, :], ALU.add).then_inc(summed, 1)

            each(pool, add)


def dense_gate(core, name, w_d, zT=None, ZR=0, zw_d=None, half=0.5, out_d=None):
    ps = core.ps
    with Stage(core, name) as st:
        w = st.sb("w", [P, KC, D])
        wh = st.sb("wh", [P, KC, D], F32R)
        wl = st.sb("wl", [P, KC, D], F32R)
        zw = st.sb("zw", [P, D])
        th = st.sb("th", [P, 2, D])
        fsb = st.sb("fsb", [P, 2, D])
        gated = st.sb("gated", [P, D])
        w_in, done, tanh_done, x_done = st.sem("w_in"), st.sem("done"), st.sem("tanh_done"), st.sem("x_done")
        step, stored, w_high, w_low = st.sem("step"), st.sem("stored"), st.sem("w_high"), st.sem("w_low")
        block = st.block()

        @block.sync
        def _(sp):
            sp.dma_start(w[:, :, :], w_d).then_inc(w_in, 16)
            if ZR:
                sp.dma_start(zw[:, :], zw_d).then_inc(w_in, 16)
            if out_d is not None:
                for t in range(NT):
                    sp.wait_ge(x_done, t + 1)
                    sp.dma_start(out_d[t * P:(t + 1) * P, :], core.x[:, t, :]).then_inc(stored, 16)
                sp.wait_ge(stored, 16 * NT)

        @block.tensor
        def _(pe):
            pe.wait_ge(w_in, 32 if ZR else 16)
            pe.wait_ge(w_low, KC)
            for t in range(NT):
                last = product(pe, ps[:, t, :], xrows(core, t * P, P), [(wh[:, c, :], wl[:, c, :]) for c in range(KC)],
                               stop=not ZR)
                if ZR:
                    last = pe.matmul(ps[:, t, :], zT[:, t * P:(t + 1) * P], zw[:, :], start=False, stop=True)
                last.then_inc(done, 1)

        @block.scalar
        def _(act):
            act.wait_ge(w_in, 32 if ZR else 16)
            for c in range(KC):
                act.activation(wh[:, c, :], w[:, c, :], ACT.Copy).then_inc(w_high, 1)
            for t in range(NT):
                act.wait_ge(done, t + 1)
                if t >= 2:
                    act.wait_ge(x_done, t - 1)
                act.activation(th[:, t % 2, :], ps[:, t, :], ACT.Tanh, scale=half).then_inc(tanh_done, 1)

        @block.vector
        def _(dve):
            chain = Chain(dve, step)
            for c in range(KC):
                dve.wait_ge(w_high, c + 1)
                dve.tensor_tensor(wl[:, c, :], w[:, c, :], f32(wh[:, c, :]), ALU.subtract).then_inc(w_low, 1)
            for t in range(NT):
                dve.wait_ge(tanh_done, t + 1)
                gate_steps(core, None, dve, t, ps[:, t, :], th[:, t % 2, :], gated[:, :], chain, x_done)
                dve.wait_ge(x_done, t + 1)


def lora_top1(core, name, zT):
    ins, ps = core.ins, core.ps
    NE, R = 4, 8
    C = NE + NE * R
    with Stage(core, name) as st:
        w = st.sb("w", [P, KC, C])
        wh = st.sb("wh", [P, KC, C], F32R)
        wl = st.sb("wl", [P, KC, C], F32R)
        w_split = st.sem("w_split")
        bias = st.sb("bias", [P, NE])
        iota = st.sb("iota", [P, 8])
        logits = st.sb("logits", [P, NT, 8])
        best = st.sb("best", [P, NT, 8])
        where = st.sb("where", [P, NT, 8], U32)
        wheref = st.sb("wheref", [P, NT, 8])
        pick = st.sb("pick", [P, NT, NE])
        z = st.sb("z", [P, NT, NE * R])
        loaded, done, step, z_done = st.sem("loaded"), st.sem("done"), st.sem("step"), st.sem("z_done")
        turned, kept = st.sem("turned"), st.sem("kept")
        block = st.block()

        @block.sync
        def _(sp):
            sp.dma_start(w[:, :, :], ins["l1_wz"]).then_inc(loaded, 16)
            sp.dma_start(bias[:, :], ins["l1_bz"].partition_broadcast(P)).then_inc(loaded, 16)
            sp.dma_start(iota[:, :], ins["iota8"].partition_broadcast(P)).then_inc(loaded, 16)

        @block.tensor
        def _(pe):
            pe.wait_ge(w_split, 2)
            for t in range(NT):
                last = product(pe, ps[:, 0, t * C:(t + 1) * C], xrows(core, t * P, P),
                               [(wh[:, c, :], wl[:, c, :]) for c in range(KC)])
            last.then_inc(done, 1)
            pe.wait_ge(z_done, 1)
            for t in range(NT):
                last = pe.transpose(ps[0:NE * R, 1 + t // 4, (t % 4) * P:(t % 4 + 1) * P], z[:, t, :], core.ident[:, :])
            last.then_inc(turned, 1)

        @block.vector
        def _(dve):
            chain = Chain(dve, step)
            got = ps[:, 0, 0:NT * C].rearrange("p (t c) -> p t c", c=C)
            chain(dve.memset(logits[:, :, :], -3e38))
            chain(dve.memset(zT[:, :], 0.0))
            dve.wait_ge(loaded, 48)
            dve.tensor_copy(wh[:, :, :], w[:, :, :]).then_inc(w_split, 1)
            dve.wait_ge(w_split, 1)
            dve.tensor_tensor(wl[:, :, :], w[:, :, :], f32(wh[:, :, :]), ALU.subtract).then_inc(w_split, 1)
            dve.wait_ge(done, 1)
            chain(dve.tensor_tensor(logits[:, :, 0:NE], got[:, :, 0:NE],
                                    bias[:, :].unsqueeze(1).broadcast_to([P, NT, NE]), ALU.add))
            for t in range(NT):
                last = dve.max(best[:, t, :], logits[:, t, :])
            chain(last)
            for t in range(NT):
                last = dve.max_index(where[:, t, :], best[:, t, :], logits[:, t, :])
            chain(last)
            chain(dve.tensor_copy(wheref[:, :, :], where[:, :, :]))
            chain(dve.tensor_tensor(pick[:, :, :], iota[:, 0:NE].unsqueeze(1).broadcast_to([P, NT, NE]),
                                    wheref[:, :, 0:1].broadcast_to([P, NT, NE]), ALU.is_equal))
            for t in range(NT):
                last = dve.tensor_tensor(z[:, t, :].rearrange("p (e r) -> p e r", e=NE),
                                         got[:, t, NE:C].rearrange("p (e r) -> p e r", e=NE),
                                         pick[:, t, :].unsqueeze(2).broadcast_to([P, NE, R]), ALU.mult)
            last.then_inc(z_done, 1)
            dve.wait_ge(turned, 1)
            dve.tensor_copy(zT[0:NE * R, :].rearrange("p (h n) -> p h n", h=2), ps[0:NE * R, 1:3, :]).then_inc(kept, 1)


def lora_by_batch(core, name, zT):
    ins, ps = core.ins, core.ps
    NA, S = 3, 4
    with Stage(core, name) as st:
        w = st.sb("w", [P, KC, P])
        wh = st.sb("wh", [P, KC, P], F32R)
        wl = st.sb("wl", [P, KC, P], F32R)
        w_split = st.sem("w_split")
        starts = st.sb("starts", [P, S], I32)
        startf = st.sb("startf", [P, S])
        row = st.sb("row", [P, 2])
        past = st.sb("past", [P, B, S])
        seg = st.sb("seg", [P, B])
        pick = st.sb("pick", [P, B])
        loaded, done, step, kept = st.sem("loaded"), st.sem("done"), st.sem("step"), st.sem("kept")
        block = st.block()

        @block.sync
        def _(sp):
            sp.dma_start(w[:, :, :], ins["l2_wz"]).then_inc(loaded, 16)
            sp.dma_start(starts[:, :], ins["l2_starts"].partition_broadcast(P)).then_inc(loaded, 16)
            sp.dma_start(row[:, :], ins["adapter_of_row"]).then_inc(loaded, 16)

        @block.tensor
        def _(pe):
            pe.wait_ge(w_split, 2)
            for b in range(B):
                last = product(pe, ps[:, b, :], [(wh[:, c, :], wl[:, c, :]) for c in range(KC)], xrows(core, b * T, T))
            last.then_inc(done, 1)

        @block.vector
        def _(dve):
            chain = Chain(dve, step)
            dve.wait_ge(loaded, 48)
            dve.tensor_copy(wh[:, :, :], w[:, :, :]).then_inc(w_split, 1)
            dve.wait_ge(w_split, 1)
            dve.tensor_tensor(wl[:, :, :], w[:, :, :], f32(wh[:, :, :]), ALU.subtract).then_inc(w_split, 1)
            chain(dve.tensor_copy(startf[:, :], starts[:, :]))
            for b in range(B):
                last = dve.tensor_scalar(past[:, b, :], startf[:, :], float(b), None, ALU.is_le)
            chain(last)
            chain(dve.tensor_reduce(seg[:, :], past[:, :, :], AX.X, ALU.add))
            chain(dve.tensor_scalar(seg[:, :], seg[:, :], -2.0, float(NA - 1), ALU.add, ALU.min))
            chain(dve.tensor_scalar(pick[:, :], seg[:, :], row[:, 0:1], None, ALU.is_equal))
            dve.wait_ge(done, 1)
            for b in range(B):
                last = dve.tensor_scalar(zT[:, b * T:(b + 1) * T], ps[:, b, :], pick[:, b:b + 1], row[:, 1:2],
                                         ALU.mult, ALU.add)
            last.then_inc(kept, 1)


def decays(core, name, rows_d, lw, wst):
    ins, ps = core.ins, core.ps
    H = 32
    with Stage(core, name) as st:
        w = st.sb("w", [P, KC, H])
        wh = st.sb("wh", [P, KC, H], F32R)
        wl = st.sb("wl", [P, KC, H], F32R)
        w_split = st.sem("w_split")
        dtb = st.sb("dtb", [P, H])
        ab = st.sb("ab", [P, H])
        ea = st.sb("ea", [P, H])
        tri = st.sb("tri", [P, P])
        ones = st.sb("ones", [P, P])
        z = st.sb("z", [P, NT, H])
        az = st.sb("az", [P, NT, H])
        dt = st.sb("dt", [P, NT, H])
        g = st.sb("g", [P, NT, H])
        G = st.sb("G", [P, NT, H])
        lndt = st.sb("lndt", [P, NT, H])
        GT = st.sb("GT", [H, N])
        loaded, done, step = st.sem("loaded"), st.sem("done"), st.sem("step")
        z_done, a_done, sp_done, dt_done, ln_done = (st.sem("z_done"), st.sem("a_done"), st.sem("sp_done"),
                                                     st.sem("dt_done"), st.sem("ln_done"))
        g_done, G_done, G_kept, d_done, turned, GT_kept, stored = (
            st.sem("g_done"), st.sem("G_done"), st.sem("G_kept"), st.sem("d_done"), st.sem("turned"),
            st.sem("GT_kept"), st.sem("stored"))
        act_step = st.sem("act_step")
        block = st.block()

        @block.sync
        def _(sp):
            sp.dma_start(w[:, :, :], ins["l1_win"]).then_inc(loaded, 16)
            sp.dma_start(dtb[:, :], ins["l1_dtb"].partition_broadcast(P)).then_inc(loaded, 16)
            sp.dma_start(ab[:, :], ins["l1_ab"].partition_broadcast(P)).then_inc(loaded, 16)
            sp.dma_start(tri[:, :], ins["tri"]).then_inc(loaded, 16)
            sp.wait_ge(GT_kept, 2)
            for k in range(H // 4):
                sp.dma_start(rows_d[k].rearrange("t h n -> h t n"),
                             GT[4 * k:4 * k + 4, :].rearrange("h (t n) -> h t n", n=P)).then_inc(stored, 16)
            sp.wait_ge(stored, 16 * (H // 4))

        @block.tensor
        def _(pe):
            pe.wait_ge(w_split, 2)
            for t in range(NT):
                last = product(pe, ps[:, 0, t * H:(t + 1) * H], xrows(core, t * P, P),
                               [(wh[:, c, :], wl[:, c, :]) for c in range(KC)])
            last.then_inc(done, 1)
            pe.wait_ge(g_done, 1)
            pe.matmul(ps[:, 1, 0:NT * H], tri[:, :], g[:, :, :].rearrange("p t h -> p (t h)"), start=True, stop=True)
            pe.matmul(ps[:, 2, 0:NT * H], ones[:, :], g[:, :, :].rearrange("p t h -> p (t h)"),
                      start=True, stop=True).then_inc(G_done, 1)
            pe.wait_ge(G_kept, 1)
            for t in range(NT):
                last = pe.transpose(ps[0:H, 3 + t // 4, (t % 4) * P:(t % 4 + 1) * P], G[:, t, :], core.ident[:, :])
            last.then_inc(turned, 1)

        def flat(a):
            return a[:, :, :].rearrange("p t h -> p (t h)")

        @block.scalar
        def _(act):
            act.wait_ge(loaded, 64)
            act.activation(ea[:, :], ab[:, :], ACT.Exp).then_inc(a_done, 1)
            act.wait_ge(z_done, 1)
            act.activation(az[:, :, :], az[:, :, :], ACT.Exp, scale=-1.0).then_inc(act_step, 1)
            act.wait_ge(act_step, 1)
            act.activation(az[:, :, :], az[:, :, :], ACT.Ln, bias=1.0).then_inc(sp_done, 1)
            act.wait_ge(dt_done, 1)
            act.activation(lndt[:, :, :], dt[:, :, :], ACT.Ln).then_inc(ln_done, 1)
            act.wait_ge(d_done, 1)
            act.activation(wst[:, :, :], wst[:, :, :], ACT.Exp).then_inc(act_step, 1)

        @block.vector
        def _(dve):
            chain = Chain(dve, step)
            chain(dve.memset(ones[:, :], 1.0))
            dve.wait_ge(loaded, 64)
            dve.tensor_copy(wh[:, :, :], w[:, :, :]).then_inc(w_split, 1)
            dve.wait_ge(w_split, 1)
            dve.tensor_tensor(wl[:, :, :], w[:, :, :], f32(wh[:, :, :]), ALU.subtract).then_inc(w_split, 1)
            dve.wait_ge(done, 1)
            chain(dve.tensor_tensor(z[:, :, :], ps[:, 0, 0:NT * H].rearrange("p (t h) -> p t h", h=H),
                                    dtb[:, :].unsqueeze(1).broadcast_to([P, NT, H]), ALU.add))
            chain(dve.tensor_scalar(az[:, :, :], z[:, :, :], -1.0, None, ALU.mult))
            dve.tensor_tensor(az[:, :, :], az[:, :, :], z[:, :, :], ALU.max).then_inc(z_done, 1)
            dve.wait_ge(sp_done, 1)
            dve.scalar_tensor_tensor(out=dt[:, :, :], in0=z[:, :, :], scalar=0.0, in1=az[:, :, :],
                                     op0=ALU.max, op1=ALU.add).then_inc(dt_done, 1)
            dve.wait_ge(dt_done, 1)
            dve.wait_ge(a_done, 1)
            dve.scalar_tensor_tensor(out=g[:, :, :], in0=dt[:, :, :], scalar=-1.0,
                                     in1=ea[:, :].unsqueeze(1).broadcast_to([P, NT, H]),
                                     op0=ALU.mult, op1=ALU.mult).then_inc(g_done, 1)
            dve.wait_ge(G_done, 1)
            dve.tensor_copy(flat(G), ps[:, 1, 0:NT * H]).then_inc(G_kept, 1)
            dve.wait_ge(G_kept, 1)
            dve.wait_ge(ln_done, 1)
            chain(dve.tensor_tensor(lw[:, :, :], G[:, :, :], lndt[:, :, :], ALU.subtract))
            dve.tensor_tensor(flat(wst), ps[:, 2, 0:NT * H], flat(lw), ALU.subtract).then_inc(d_done, 1)
            dve.wait_ge(turned, 1)
            dve.tensor_copy(GT[:, :].rearrange("p (h n) -> p h n", h=2), ps[0:H, 3:5, :]).then_inc(GT_kept, 2)


def retention(core, name, rows_d, lw, wst):
    ins, ps, mixed = core.ins, core.ps, core.mixed
    KV, R = 8, 4
    NP = 2 + 3 * R
    RING = NP // 2
    C1 = QT - 1
    with Stage(core, name) as st:
        w = st.sb("w", [P, RING, D])
        wh = st.sb("wh", [P, 2, KC, P], F32R)
        wl = st.sb("wl", [P, 2, KC, P], F32R)
        woh = st.sb("woh", [P, R, D], F32R)
        wol = st.sb("wol", [P, R, D], F32R)
        cos = st.sb("cos", [P, T])
        sin = st.sb("sin", [P, T])
        gw = st.sb("gw", [P, 1])
        eps = st.sb("eps", [P, 1])
        limit = st.sb("limit", [P, P])
        ones = st.sb("ones", [P, P])
        qT = st.sb("qT", [P, R, N])
        silu = st.sb("silu", [P, R, N])
        kT = st.sb("kT", [P, N])
        ktm = st.sb("ktm", [P, NT, P])
        v = st.sb("v", [P, NT, P])
        rows = st.sb("rows", [P, 4, R, P])
        er = st.sb("er", [P, 3, R, P])
        lws = st.sb("lws", [P, NT, R])
        wsts = st.sb("wsts", [P, NT, R])
        a2 = st.sb("a2", [P, 2, D])
        b2 = st.sb("b2", [P, 2, D])
        c2 = st.sb("c2", [P, 2, D])
        vw = st.sb("vw", [P, 2, D])
        state = st.sb("state", [P, D])
        y2 = st.sb("y2", [P, 2, D])
        rinv = st.sb("rinv", [P, 2, D])
        rn = st.sb("rn", [P, D])
        ryh = st.sb("ryh", [P, 2, D], F32R)
        ryl = st.sb("ryl", [P, 2, D], F32R)

        consts_in, ones_made, cleared = st.sem("consts_in"), st.sem("ones_made"), st.sem("cleared")
        w_in = [st.sem(f"w_in{i}") for i in range(RING)]
        rows_in = [st.sem(f"rows_in{i}") for i in range(4)]
        w_high, w_low, freed = st.sem("w_high"), st.sem("w_low"), st.sem("freed")
        jobs_done, kept_v, kept_s = st.sem("jobs_done"), st.sem("kept_v"), st.sem("kept_s")
        dstep, gate_done, kt_done, ktm_done = st.sem("dstep"), st.sem("gate_done"), st.sem("kt_done"), st.sem("ktm_done")
        raw_done, dec_done, er_done = st.sem("raw_done"), st.sem("dec_done"), st.sem("er_done")
        s_done, sc_done, qg_done, vw_done = st.sem("s_done"), st.sem("sc_done"), st.sem("qg_done"), st.sem("vw_done")
        y_done, cs_done, st_done, y2_done = st.sem("y_done"), st.sem("cs_done"), st.sem("st_done"), st.sem("y2_done")
        ms_done, ln_done, rinv_done = st.sem("ms_done"), st.sem("ln_done"), st.sem("rinv_done")
        rn_done, ryh_done, ryl_done, wo_done, added = (st.sem("rn_done"), st.sem("ryh_done"), st.sem("ryl_done"),
                                                       st.sem("wo_done"), st.sem("added"))
        block = st.block()

        pieces, places = [("k", 0), ("v", 0)], [0, 1]
        for h in range(R):
            pieces += [("q", h), ("g", h)]
            places += [2 + 3 * h + (h == R - 1), 3 + 3 * h + (h == R - 1)]
        wo_places = [p for p in range(NP) if p not in places]
        jobs = [(kind, h, b) for kind, h in pieces for b in range(B)]
        NJ = len(jobs)
        ROPE = [n for n, j in enumerate(jobs) if j[0] in "kq"]
        SIDE = [n for n, j in enumerate(jobs) if j[0] in "vg"]
        PB = 6

        def reads(t):
            return (t // QT) * C1 + t % QT

        def adds(t):
            return (t // QT) * C1 + min(t % QT + 1, C1)

        def tile(a, t):
            return a[:, :, t * P:(t + 1) * P]

        def heads(a):
            return a.rearrange("p (h n) -> p h n", h=R)

        @block.sync
        def _(sp):
            sp.dma_start(cos[:, :], ins["cos"]).then_inc(consts_in, 16)
            sp.dma_start(sin[:, :], ins["sin"]).then_inc(consts_in, 16)
            sp.dma_start(gw[:, :], ins["l1_gw"]).then_inc(consts_in, 16)
            sp.dma_start(limit[:, :], ins["limit"]).then_inc(consts_in, 16)

            def load_w(kv, p):
                turn = kv + p // NP
                if not (isinstance(kv, int) and kv * NP + p < RING):
                    sp.wait_ge(w_low, kv * NP + p - RING + 1)
                    sp.sem_inc(freed, 1)
                sp.dma_start(w[:, p % RING, :], ins["l1_w"][turn, p % NP]).then_inc(w_in[p % RING], 16)

            def load_rows(kv, t):
                turn = kv + t // NT
                if not (isinstance(kv, int) and kv * NT + t < 4):
                    sp.wait_ge(er_done, kv * NT + t - 3)
                    sp.sem_inc(freed, 1)
                sp.dma_start(rows[:, t % 4, :, :], rows_d[turn, t % NT].partition_broadcast(P)).then_inc(rows_in[t % 4], 16)

            for p in range(RING):
                load_w(0, p)
            for t in range(4):
                load_rows(0, t)
            with sp.Fori(0, KV - 1) as kv:
                for p in range(RING, NP + RING):
                    load_w(kv, p)
                for t in range(4, NT + 4):
                    load_rows(kv, t)
            for p in range(RING, NP):
                load_w(KV - 1, p)
            for t in range(4, NT):
                load_rows(KV - 1, t)

        @block.tensor
        def _(pe):
            pe.wait_ge(ones_made, 1)
            with pe.Fori(0, KV) as kv:
                for n, (kind, h, b) in enumerate(jobs):
                    if n >= PB:
                        m = n - PB
                        if m in ROPE:
                            pe.wait_ge(kept_v, kv * len(ROPE) + ROPE.index(m) + 1)
                        else:
                            pe.wait_ge(kept_s, kv * len(SIDE) + SIDE.index(m) + 1)
                    p = n // B
                    if b == 0:
                        pe.wait_ge(w_low, kv * NP + places[p] + 1)
                    piece = [(wh[:, p % 2, c, :], wl[:, p % 2, c, :]) for c in range(KC)]
                    out = ps[:, n % PB, :]
                    if kind == "v":
                        for i in range(QT):
                            last = product(pe, out[:, i * P:(i + 1) * P], xrows(core, b * T + i * P, P), piece)
                    else:
                        last = product(pe, out, piece, xrows(core, b * T, T))
                    last.then_inc(jobs_done, 1)
                    if n == 7:
                        pe.wait_ge(kept_v, kv * len(ROPE) + 2)
                        pe.wait_ge(added, kv * NT + 1)
                        for t in range(NT):
                            last = pe.transpose(ps[:, 6 + t // 4, (t % 4) * P:(t % 4 + 1) * P],
                                                kT[:, t * P:(t + 1) * P], core.ident[:, :])
                        last.then_inc(kt_done, 1)
                pe.wait_ge(kept_v, kv * len(ROPE) + len(ROPE))
                pe.wait_ge(kept_s, kv * len(SIDE) + len(SIDE))
                pe.wait_ge(ktm_done, kv + 1)
                pe.wait_ge(w_low, kv * NP + NP)

                def scores(t):
                    if t >= 2:
                        pe.wait_ge(sc_done, kv * NT + t - 1)
                    pe.matmul(ps[:, t % 2, :], kT[:, t * P:(t + 1) * P], tile(qT, t),
                              start=True, stop=True).then_inc(s_done, 1)

                def outputs(t):
                    pe.wait_ge(sc_done, kv * NT + t + 1)
                    if t >= 3:
                        pe.wait_ge(rn_done, kv * NT + t - 2)
                    out = ps[:, 2 + t % 3, :]
                    last = pe.matmul(out, v[:, t, :], a2[:, t % 2, :], start=True, stop=True)
                    if t % QT > 0:
                        pe.wait_ge(qg_done, kv * 2 * C1 + reads(t))
                        pe.wait_ge(st_done, kv * 2 * C1 + adds(t - 1))
                        for h in range(R):
                            last = pe.matmul(out[:, h * P:(h + 1) * P], state[:, h * P:(h + 1) * P],
                                             b2[:, t % 2, h * P:(h + 1) * P],
                                             start=False, stop=True, skip_group_check=True)
                    last.then_inc(y_done, 1)

                def adding(t):
                    pe.wait_ge(vw_done, kv * 2 * C1 + adds(t))
                    if adds(t) > 1:
                        pe.wait_ge(st_done, kv * 2 * C1 + adds(t) - 1)
                    pe.matmul(ps[:, 5, :], ktm[:, t, :], vw[:, t % 2, :], start=True, stop=True).then_inc(cs_done, 1)

                def squares(t):
                    pe.wait_ge(y2_done, kv * NT + t + 1)
                    if t >= 1:
                        pe.wait_ge(ln_done, kv * NT + t)
                    pe.matmul(ps[:, 6, :], ones[:, :], y2[:, t % 2, :], start=True, stop=True).then_inc(ms_done, 1)

                def project(t):
                    pe.wait_ge(ryl_done, kv * NT + t + 1)
                    if t >= 1:
                        pe.wait_ge(added, kv * NT + t + 1)
                    product(pe, ps[:, 7, :],
                            [(ryh[:, t % 2, h * P:(h + 1) * P], ryl[:, t % 2, h * P:(h + 1) * P]) for h in range(R)],
                            [(woh[:, h, :], wol[:, h, :]) for h in range(R)]).then_inc(wo_done, 1)

                scores(0)
                for t in range(NT + 2):
                    if t + 1 < NT:
                        scores(t + 1)
                    if t < NT:
                        outputs(t)
                        if t % QT < C1:
                            adding(t)
                    if 1 <= t <= NT:
                        squares(t - 1)
                    if t >= 2:
                        project(t - 2)

        @block.scalar
        def _(act):
            with act.Fori(0, KV) as kv:

                def high(p):
                    act.wait_ge(w_in[p % RING], kv * 32 + (p // RING) * 16 + 16)
                    if p in wo_places:
                        out = woh[:, wo_places.index(p), :]
                    else:
                        j = places.index(p)
                        if j >= 2:
                            act.wait_ge(jobs_done, kv * NJ + (j - 1) * B)
                        out = wh[:, j % 2, :, :].rearrange("p c n -> p (c n)")
                    act.activation(out, w[:, p % RING, :], ACT.Copy).then_inc(w_high, 1)

                high(0)
                high(1)
                for n, (kind, h, b) in enumerate(jobs):
                    if kind == "v":
                        act.wait_ge(jobs_done, kv * NJ + n + 1)
                        act.activation(v[:, b * QT:(b + 1) * QT, :].rearrange("p i e -> p (i e)"), ps[:, n % PB, :],
                                       ACT.Copy).then_inc(kept_s, 1)
                    if kind == "g":
                        act.wait_ge(jobs_done, kv * NJ + n + 1)
                        m = h * B + b
                        if m >= 2:
                            act.wait_ge(gate_done, kv * (R * B) + m - 1)
                        act.activation(c2[:, b, :], ps[:, n % PB, :], ACT.Tanh, scale=0.5)
                        act.activation(silu[:, h, b * T:(b + 1) * T], ps[:, n % PB, :], ACT.Copy,
                                       scale=0.5).then_inc(kept_s, 1)
                    if n % B == 1 and n // B + 2 < len(pieces):
                        for p in range(places[n // B + 1] + 1, places[n // B + 2] + 1):
                            high(p)

                def decay(t):
                    act.wait_ge(raw_done, kv * NT + t + 1)
                    act.activation(c2[:, t % 2, :], c2[:, t % 2, :], ACT.Exp).then_inc(dec_done, 1)
                    if t >= 3:
                        act.wait_ge(y_done, kv * NT + t - 2)
                        act.wait_ge(st_done, kv * 2 * C1 + adds(t - 3))
                    act.activation(er[:, t % 3, :, :], rows[:, t % 4, :, :], ACT.Exp).then_inc(er_done, 1)

                decay(0)
                decay(1)
                for t in range(NT + 1):
                    if t < NT:
                        act.wait_ge(y_done, kv * NT + t + 1)
                        act.activation(y2[:, t % 2, :], ps[:, 2 + t % 3, :], ACT.Square).then_inc(y2_done, 1)
                    if t >= 1:
                        u = t - 1
                        act.wait_ge(ms_done, kv * NT + u + 1)
                        act.activation(rinv[:, u % 2, :], ps[:, 6, :], ACT.Ln, bias=eps[:, 0:1],
                                       scale=1.0 / P).then_inc(ln_done, 1)
                        act.wait_ge(ln_done, kv * NT + u + 1)
                        act.activation(rinv[:, u % 2, :], rinv[:, u % 2, :], ACT.Exp, scale=-0.5).then_inc(rinv_done, 1)
                    if t + 2 < NT:
                        decay(t + 2)
                    if t >= 1:
                        act.wait_ge(rn_done, kv * NT + u + 1)
                        if u >= 2:
                            act.wait_ge(wo_done, kv * NT + u - 1)
                        act.activation(ryh[:, u % 2, :], rn[:, :], ACT.Copy).then_inc(ryh_done, 1)

        @block.gpsimd
        def _(pool):
            pool.memset(eps[:, :], EPS).then_inc(cleared, 1)
            pool.memset(mixed[:, :, :], 0.0).then_inc(cleared, 1)
            with pool.Fori(0, KV) as kv:
                for p in range(NP):
                    pool.wait_ge(w_high, kv * NP + p + 1)
                    if p in wo_places:
                        out, hi = (a[:, wo_places.index(p), :] for a in (wol, woh))
                    else:
                        out, hi = (a[:, places.index(p) % 2, :, :].rearrange("p c n -> p (c n)") for a in (wl, wh))
                    pool.tensor_tensor(out, w[:, p % RING, :], f32(hi), ALU.subtract).then_inc(w_low, 1)
                pool.wait_ge(kept_v, kv * len(ROPE) + len(ROPE))
                pool.wait_ge(kept_s, kv * len(SIDE) + len(SIDE))
                for t in range(NT):
                    if t % QT > 0:
                        pool.wait_ge(er_done, kv * NT + t + 1)
                        if reads(t) > 2:
                            pool.wait_ge(y_done, kv * NT + t - 1)
                        pool.tensor_tensor(heads(b2[:, t % 2, :]), tile(qT, t), er[:, t % 3, :, :],
                                           ALU.mult).then_inc(qg_done, 1)
                    if t % QT < C1:
                        if adds(t) > 2:
                            pool.wait_ge(cs_done, kv * 2 * C1 + adds(t) - (1 if t % QT == 0 else 2))
                        pool.tensor_tensor(heads(vw[:, t % 2, :]), v[:, t, :].unsqueeze(1).broadcast_to([P, R, P]),
                                           wsts[:, t, :].unsqueeze(2).broadcast_to([P, R, P]),
                                           ALU.mult).then_inc(vw_done, 1)

        @block.vector
        def _(dve):
            dve.sem_inc(added, 1)
            dve.memset(ones[:, :], 1.0).then_inc(ones_made, 1)
            dve.wait_ge(consts_in, 64)
            dve.wait_ge(cleared, 2)
            with dve.Fori(0, KV) as kv:
                NSTEP = 1 + len(ROPE) + NT
                count = [0]

                def link(ins_):
                    count[0] += 1
                    ins_.then_inc(dstep, 1)
                    dve.wait_ge(dstep, kv * NSTEP + count[0])

                dve.tensor_copy(lws[:, :, :], lw[:, :, bass.ds(kv * R, R)])
                link(dve.tensor_copy(wsts[:, :, :], wst[:, :, bass.ds(kv * R, R)]))
                for n, (kind, h, b) in enumerate(jobs):
                    if kind in "kq":
                        dve.wait_ge(jobs_done, kv * NJ + n + 1)
                        out = kT[:, b * T:(b + 1) * T] if kind == "k" else qT[:, h, b * T:(b + 1) * T]
                        dve.tensor_tensor(a2[:, b, :], ps[:, n % PB, :], cos[:, :], ALU.mult)
                        dve.tensor_tensor(b2[0:64, b, :], ps[64:128, n % PB, :], sin[0:64, :], ALU.mult)
                        link(dve.tensor_tensor(b2[64:128, b, :], ps[0:64, n % PB, :], sin[64:128, :], ALU.mult))
                        dve.tensor_tensor(out, a2[:, b, :], b2[:, b, :], ALU.add).then_inc(kept_v, 1)
                    if kind == "g":
                        dve.wait_ge(kept_s, kv * len(SIDE) + SIDE.index(n) + 1)
                        dve.scalar_tensor_tensor(out=silu[:, h, b * T:(b + 1) * T], in0=c2[:, b, :], scalar=1.0,
                                                 in1=silu[:, h, b * T:(b + 1) * T], op0=ALU.add,
                                                 op1=ALU.mult).then_inc(gate_done, 1)
                    if n == 8:
                        dve.wait_ge(kt_done, kv + 1)
                        for half in range(2):
                            last = dve.tensor_copy(ktm[:, half * 4:(half + 1) * 4, :].rearrange("p i e -> p (i e)"),
                                                   ps[:, 6 + half, :])
                        last.then_inc(ktm_done, 1)
                dve.wait_ge(gate_done, kv * (R * B) + R * B)

                def exponents(t):
                    dve.wait_ge(rows_in[t % 4], kv * 32 + (t // 4) * 16 + 16)
                    if t >= 2:
                        dve.wait_ge(sc_done, kv * NT + t - 1)
                    for h in range(R):
                        last = dve.scalar_tensor_tensor(
                            out=c2[:, t % 2, h * P:(h + 1) * P], in0=rows[:, t % 4, h, :],
                            scalar=lws[:, t, h:h + 1], in1=limit[:, :], op0=ALU.subtract, op1=ALU.min)
                    last.then_inc(raw_done, 1)

                def decayed(t):
                    dve.wait_ge(s_done, kv * NT + t + 1)
                    dve.wait_ge(dec_done, kv * NT + t + 1)
                    dve.tensor_tensor(a2[:, t % 2, :], ps[:, t % 2, :], c2[:, t % 2, :], ALU.mult).then_inc(sc_done, 1)

                exponents(0)
                exponents(1)
                decayed(0)
                for t in range(NT + 3):
                    if 2 <= t < NT + 2:
                        dve.wait_ge(ryh_done, kv * NT + t - 1)
                        dve.tensor_tensor(ryl[:, t % 2, :], rn[:, :], f32(ryh[:, t % 2, :]), ALU.subtract).then_inc(ryl_done, 1)
                    if t + 1 < NT:
                        decayed(t + 1)
                    if t + 2 < NT:
                        exponents(t + 2)
                    if t >= 3:
                        dve.wait_ge(wo_done, kv * NT + t - 2)
                        dve.tensor_tensor(mixed[:, t - 3, :], mixed[:, t - 3, :], ps[:, 7, :], ALU.add).then_inc(added, 1)
                    if t < NT and t % QT < C1:
                        dve.wait_ge(cs_done, kv * 2 * C1 + adds(t))
                        if t % QT == 0:
                            last = dve.tensor_copy(state[:, :], ps[:, 5, :])
                        else:
                            dve.wait_ge(er_done, kv * NT + t + 1)
                            for h in range(R):
                                last = dve.scalar_tensor_tensor(
                                    out=state[:, h * P:(h + 1) * P], in0=state[:, h * P:(h + 1) * P],
                                    scalar=er[:, t % 3, h, P - 1:P], in1=ps[:, 5, h * P:(h + 1) * P],
                                    op0=ALU.mult, op1=ALU.add)
                        last.then_inc(st_done, 1)
                    if 1 <= t <= NT:
                        u = t - 1
                        dve.wait_ge(rinv_done, kv * NT + u + 1)
                        if u >= 1:
                            dve.wait_ge(ryl_done, kv * NT + u)
                        link(dve.scalar_tensor_tensor(out=rn[:, :], in0=ps[:, 2 + u % 3, :], scalar=gw[:, 0:1],
                                                      in1=rinv[:, u % 2, :], op0=ALU.mult, op1=ALU.mult))
                        dve.tensor_tensor(heads(rn[:, :]), heads(rn[:, :]), tile(silu, u), ALU.mult).then_inc(rn_done, 1)
                assert count[0] == NSTEP


def build(nc, ins, out):
    ctx = ExitStack()
    with ctx:
        core = Core(nc, ctx, ins)
        load_inputs(core)

        layernorm(core, "ln0")
        with Stage(core, "mix0") as st:
            oh, ol = st.sb("oh", [P, KC, N], F32R), st.sb("ol", [P, KC, N], F32R)
            attention(core, "l0", oh, ol, G=4, E=16, scale=0.25, denominator=1.0, causal=True, shared_kv=True)
            project_out(core, "out0", oh, ol, KC, P, ins["l0_wo"])
        experts(core, "ffn0")

        layernorm(core, "ln1")
        with Stage(core, "mix1") as st:
            lw = st.sb("lw", [P, NT, 32])
            wst = st.sb("wst", [P, NT, 32])
            rows_d = nc.dram_tensor("decay_rows", [8, NT, 4, P], F32).ap()
            decays(core, "dec1", rows_d, lw, wst)
            retention(core, "ret1", rows_d, lw, wst)
        with Stage(core, "gate1") as st:
            zT = st.sb("zT", [P, N])
            lora_top1(core, "top1", zT)
            dense_gate(core, "ffn1", ins["l1_wup"], zT, 32, ins["l1_zw"])

        layernorm(core, "ln2")
        with Stage(core, "mix2") as st:
            oh, ol = st.sb("oh", [P, KC, N], F32R), st.sb("ol", [P, KC, N], F32R)
            attention(core, "l2", oh, ol, G=4, E=16, scale=0.25, denominator=1.0, causal=True, shared_kv=False,
                      qk_bias=ins["l2_qkb"], v_bias=ins["l2_vb"])
            project_out(core, "out2", oh, ol, KC, P, ins["l2_wo"], ins["l2_bo"])
        with Stage(core, "gate2") as st:
            zT = st.sb("zT", [P, N])
            lora_by_batch(core, "byb2", zT)
            dense_gate(core, "ffn2", ins["l2_w"], zT, 49, ins["l2_zw"])

        layernorm(core, "ln3")
        with Stage(core, "mix3") as st:
            oh, ol = st.sb("oh", [P, 1, N], F32R), st.sb("ol", [P, 1, N], F32R)
            attention(core, "l3", oh, ol, G=1, E=8, scale=1.0, denominator=8.0, causal=False, shared_kv=False,
                      qk_bias=ins["l3_qkb"], v_bias=ins["l3_vb"])
            project_out(core, "out3", oh, ol, 1, 64, ins["l3_wo"], ins["l3_bo"])
        signed_gate(core, "ffn3", ins["l3_k"], ins["ei"], ins["l3_scale"], out)


def signed_gate(core, name, k_d, ei_d, scale_d, out_d):
    ps = core.ps
    with Stage(core, name) as st:
        k8 = st.sb("k8", [P, KC, D], mybir.dt.uint8)
        ei = st.sb("ei", [P, KC])
        w = st.sb("w", [P, KC, D], F32R)
        sc = st.sb("sc", [P, 1])
        f = st.sb("f", [P, 2, D])
        th = st.sb("th", [P, 2, D])
        gated = st.sb("gated", [P, D])
        loaded, made, done, f_done, tanh_done, x_done, step, stored = (
            st.sem("loaded"), st.sem("made"), st.sem("done"), st.sem("f_done"), st.sem("tanh_done"),
            st.sem("x_done"), st.sem("step"), st.sem("stored"))
        block = st.block()

        @block.sync
        def _(sp):
            sp.dma_start(k8[:, :, :], k_d).then_inc(loaded, 16)
            sp.dma_start(ei[:, :], ei_d).then_inc(loaded, 16)
            sp.dma_start(sc[:, :], scale_d.partition_broadcast(P)).then_inc(loaded, 16)
            for t in range(NT):
                sp.wait_ge(x_done, t + 1)
                sp.dma_start(out_d[t * P:(t + 1) * P, :], core.x[:, t, :]).then_inc(stored, 16)
            sp.wait_ge(stored, 16 * NT)

        @block.tensor
        def _(pe):
            pe.wait_ge(made, KC)
            for t in range(NT):
                for c in range(KC):
                    pe.matmul(ps[:, t, :], core.xh[:, c, t * P:(t + 1) * P], w[:, c, :], start=(c == 0), stop=False)
                    last = pe.matmul(ps[:, t, :], core.xl[:, c, t * P:(t + 1) * P], w[:, c, :],
                                     start=False, stop=(c == KC - 1))
                last.then_inc(done, 1)

        @block.scalar
        def _(act):
            act.wait_ge(loaded, 48)
            for t in range(NT):
                act.wait_ge(done, t + 1)
                if t >= 2:
                    act.wait_ge(x_done, t - 1)
                act.activation(f[:, t % 2, :], ps[:, t, :], ACT.Copy, scale=sc[:, 0:1]).then_inc(f_done, 1)
                act.wait_ge(f_done, t + 1)
                act.activation(th[:, t % 2, :], f[:, t % 2, :], ACT.Tanh, scale=0.5).then_inc(tanh_done, 1)

        @block.vector
        def _(dve):
            chain = Chain(dve, step)
            dve.wait_ge(loaded, 48)
            for c in range(KC):
                dve.tensor_scalar(w[:, c, :], k8[:, c, :], ei[:, c:c + 1], None, ALU.mult).then_inc(made, 1)
            for t in range(NT):
                dve.wait_ge(tanh_done, t + 1)
                gate_steps(core, None, dve, t, f[:, t % 2, :], th[:, t % 2, :], gated[:, :], chain, x_done)
                dve.wait_ge(x_done, t + 1)


def laid_out(inputs):
    import numpy as np

    a = {k: np.asarray(v) for k, v in inputs.items()}
    f32 = np.float32

    def chunks(w):
        return np.ascontiguousarray(w.reshape(-1, P, w.shape[1]).transpose(1, 0, 2))

    def groups(w, n):
        k, m = w.shape
        return np.ascontiguousarray(w.reshape(k // P, P, m // n, n).transpose(2, 1, 0, 3))

    d = {"x": a["L0_attn_x"].reshape(N, D)}
    d["l0_wqkv"] = groups(a["L0_attn_wq"], P)[:, :, None]
    d["l0_wkv"] = chunks(np.concatenate([np.tile(a["L0_attn_wk"], (1, U)), a["L0_attn_wv"]], 1))
    d["l0_wo"] = chunks(a["L0_attn_wo"])
    d["l0_wgate"] = chunks(a["L0_ffn_W_gate"])
    d["l0_bgate"] = a["L0_ffn_b_gate"]
    d["l0_we"] = np.ascontiguousarray(a["L0_ffn_W_e"].reshape(8, KC, P, D).transpose(0, 2, 1, 3))
    d["l0_be"] = a["L0_ffn_b_e"]
    wq, wg = (groups(a["L1_attn_" + k].T, P).reshape(8, 4, P, D) for k in ("Wq", "Wg"))
    wk, wv = (groups(a["L1_attn_" + k].T, P).reshape(8, 1, P, D) for k in ("Wk", "Wv"))
    wo = a["L1_attn_Wo"].T.reshape(8, 4, P, D)
    d["l1_w"] = np.stack([wk[:, 0], wv[:, 0]] + [m for h in range(3) for m in (wq[:, h], wg[:, h], wo[:, h])]
                         + [wo[:, 3], wq[:, 3], wg[:, 3]], 1)
    d["l1_win"] = chunks(a["L1_attn_Win"].T)
    d["l1_dtb"] = a["L1_attn_dt_bias"]
    d["l1_ab"] = a["L1_attn_A_log_bias"]
    d["l1_gw"] = a["L1_attn_gnorm_w"].reshape(P, 1)
    d["l1_wup"] = chunks(a["L1_ffn_W_up"].T)
    d["l1_wz"] = chunks(np.concatenate([a["L1_ffn_gate_w"], a["L1_ffn_lora_A"].reshape(32, D)], 0).T)
    d["l1_bz"] = a["L1_ffn_expert_bias"]
    d["l1_zw"] = np.concatenate([a["L1_ffn_lora_B"].transpose(0, 2, 1).reshape(32, D), np.zeros((P - 32, D), f32)], 0)
    d["l2_wqkv"] = np.stack([groups(a["L2_attn_" + k].T, P) for k in ("Wq", "Wk", "Wv")], 2)
    d["l2_qkb"] = np.ascontiguousarray(np.stack([a["L2_attn_bq"].reshape(4, P), a["L2_attn_bk"].reshape(4, P)], 2))
    d["l2_vb"] = a["L2_attn_bv"].reshape(4, P)
    d["l2_wo"] = chunks(a["L2_attn_Wo"].T)
    d["l2_bo"] = a["L2_attn_bo"]
    d["l2_w"] = chunks(a["L2_ffn_weight"].T)
    d["l2_wz"] = chunks(np.concatenate([a["L2_ffn_lora_A"].reshape(48, D), np.zeros((P - 48, D), f32)], 0).T)
    d["l2_zw"] = np.concatenate([a["L2_ffn_lora_B"].transpose(0, 2, 1).reshape(48, D), a["L2_ffn_bias"][None],
                                 np.zeros((P - 49, D), f32)], 0)
    d["l2_starts"] = a["L2_ffn_lora_start_indices"]
    qk = a["L3_attn_Wqk_w"].reshape(64, 2, D)
    qkb = a["L3_attn_Wqk_b"].reshape(64, 2)
    pad = np.zeros((64, D), f32)
    d["l3_wqkv"] = np.stack([groups(np.concatenate([m, pad], 0).T, P)
                             for m in (qk[:, 0], qk[:, 1], a["L3_attn_Wv_w"])], 2)
    d["l3_qkb"] = np.concatenate([qkb, np.zeros((64, 2), f32)], 0)[None]
    d["l3_vb"] = a["L3_attn_Wv_b"].reshape(1, 64)
    d["l3_wo"] = np.ascontiguousarray(a["L3_attn_Wo_w"].T).reshape(64, 1, D)
    d["l3_bo"] = a["L3_attn_Wo_b"]
    d["l3_k"] = np.ascontiguousarray(a["L3_ffn_kernel"].reshape(KC, P, D).transpose(1, 0, 2))
    d["l3_scale"] = a["L3_ffn_scale"].reshape(1)
    i, j = np.arange(P)[:, None], np.arange(P)[None, :]
    d["ident"] = np.eye(P, dtype=f32)
    d["masks"] = np.ascontiguousarray(np.stack([np.where(j > i, NEG, 0), np.where(i > j, NEG, 0)], 1).astype(f32))
    d["minus1"] = np.ascontiguousarray(
        np.broadcast_to(-np.eye(P, U, dtype=f32)[:, :, None], (P, U, P)))
    for E in (16, 8):
        d[f"headmask{E}"] = (np.arange(P)[:, None] // E == np.arange(U)[None]).astype(f32)
    d["tri"] = (i <= j).astype(f32)
    d["limit"] = np.where(j >= i, 80.0, NEG).astype(f32)
    d["iota8"] = np.arange(8, dtype=f32)
    d["adapter_of_row"] = np.stack([np.arange(P) // 16, np.arange(P) == 48], 1).astype(f32)
    inv = 1.0 / 10000.0 ** (np.arange(0, P, 2, dtype=f32) / f32(P))
    ang = np.arange(T, dtype=f32)[None, :] * inv.astype(f32)[:, None]
    d["cos"] = np.concatenate([np.cos(ang), np.cos(ang)], 0).astype(f32)
    d["sin"] = np.concatenate([-np.sin(ang), np.sin(ang)], 0).astype(f32)
    ex = round(D * 0.8)
    d["ei"] = np.where(np.arange(D) < ex, 1.0, -0.8 / (1.0 - 0.8)).astype(f32).reshape(KC, P).T.copy()
    return d


def kernel(**inputs):
    import numpy as np
    import concourse.bacc as bacc
    from concourse.bass_utils import run_bass_kernel_spmd

    nc = bacc.Bacc("TRN2", target_bir_lowering=False, num_devices=1)
    arrays, ins = {}, {}
    for name, array in laid_out(inputs).items():
        arrays[f"in_{name}"] = array = np.ascontiguousarray(array)
        ins[name] = nc.dram_tensor(f"in_{name}", array.shape, mybir.dt.from_np(array.dtype), kind="ExternalInput").ap()
    out = nc.dram_tensor("out_x", (N, D), F32, kind="ExternalOutput").ap()
    build(nc, ins, out)
    result = run_bass_kernel_spmd(nc, [arrays], core_ids=[0])
    return result.results[0]["out_x"].reshape(B, T, D)
```

```python
from contextlib import ExitStack

import concourse.bass as bass
from concourse import mybir

F32 = mybir.dt.float32
F32R = mybir.dt.float32r
BF16 = mybir.dt.bfloat16
I32 = mybir.dt.int32
U32 = mybir.dt.uint32
ALU = mybir.AluOpType
ACT = mybir.ActivationFunctionType
AX = mybir.AxisListType

P = 128
B = 2
T = 512
N = B * T
NT = N // P
QT = T // P
D = 512
KC = D // P
EPS = 1e-5
NEG = -1e30
U = 8


class Core:

    def __init__(self, nc, ctx, ins):
        self.nc = nc
        self.ins = ins
        self.x = ctx.enter_context(nc.sbuf_tensor("x_sb", [P, NT, D], F32))
        self.xh = ctx.enter_context(nc.sbuf_tensor("xnT_high", [P, KC, N], F32R))
        self.xl = ctx.enter_context(nc.sbuf_tensor("xnT_low", [P, KC, N], F32R))
        self.mixed = ctx.enter_context(nc.sbuf_tensor("mixed", [P, NT, D], F32))
        self.stats = ctx.enter_context(nc.sbuf_tensor("stats", [P, NT, 6], F32))
        self.logits0 = ctx.enter_context(nc.sbuf_tensor("logits0", [P, NT, 8], F32))
        self.ident = ctx.enter_context(nc.sbuf_tensor("ident", [P, P], F32))
        self.identb = ctx.enter_context(nc.sbuf_tensor("identb", [P, P], BF16))
        self.ps = ctx.enter_context(nc.psum_tensor("banks", [P, 8, 512], F32))


class Stage:

    def __init__(self, core, name):
        self.core, self.nc, self.name = core, core.nc, name
        self.ctx, self.sems = ExitStack(), []

    def __enter__(self):
        return self

    def __exit__(self, *a):
        self.ctx.close()
        if self.sems:
            self.nc.clear_and_free_semaphores(self.sems)
            self.nc.all_engine_barrier()

    def sb(self, name, shape, dt=F32):
        return self.ctx.enter_context(self.nc.sbuf_tensor(f"{self.name}_{name}", shape, dt))

    def sem(self, name):
        self.sems.append(self.nc.alloc_semaphore(f"{self.name}_{name}"))
        return self.sems[-1]

    def block(self):
        return self.ctx.enter_context(self.nc.Block())


def f32(ap):
    return ap.bitcast(F32)


def product(pe, out, lhs, rhs, start=True, stop=True):
    n = len(lhs)
    for c in range(n):
        (lh, ll), (rh, rl) = lhs[c], rhs[c]
        pe.matmul(out, lh, rh, start=(start and c == 0), stop=False)
        pe.matmul(out, lh, rl, start=False, stop=False)
        last = pe.matmul(out, ll, rh, start=False, stop=(stop and c == n - 1))
    return last


def xrows(core, t0, n):
    return [(core.xh[:, c, t0:t0 + n], core.xl[:, c, t0:t0 + n]) for c in range(KC)]


class Chain:

    def __init__(self, eng, sem):
        self.eng, self.sem, self.n = eng, sem, 0

    def __call__(self, ins):
        self.n += 1
        ins.then_inc(self.sem, 1)
        self.eng.wait_ge(self.sem, self.n)


def load_inputs(core):
    with Stage(core, "load") as st:
        loaded, made = st.sem("loaded"), st.sem("ident_made")
        x_in = [st.sem(f"x_in{t}") for t in range(NT)]
        block = st.block()

        @block.sync
        def _(sp):
            for t in range(NT):
                sp.dma_start(core.x[:, t, :], core.ins["x"][t * P:(t + 1) * P, :]).then_inc(x_in[t], 16)
            sp.dma_start(core.ident[:, :], core.ins["ident"]).then_inc(loaded, 16)

        @block.vector
        def _(dve):
            for t in range(NT):
                dve.wait_ge(x_in[t], 16)
                dve.bn_stats(core.stats[:, t, :], core.x[:, t, :])
            dve.wait_ge(loaded, 16)
            dve.tensor_copy(core.identb[:, :], core.ident[:, :]).then_inc(made, 1)
            dve.wait_ge(made, 1)


def layernorm(core, name, load_ahead):
    x, ps = core.x, core.ps
    with Stage(core, name) as st:
        xn = st.sb("xn", [P, NT, D])
        mv = st.sb("mean_var", [P, NT, 2])
        var = st.sb("var", [P, NT])
        std = st.sb("std", [P, NT])
        rstd = st.sb("rstd", [P, NT])
        step, var_ready, std_ready = st.sem("step"), st.sem("var_ready"), st.sem("std_ready")
        xn_ready, turned, high_kept, low_kept = (st.sem("xn_ready"), st.sem("turned"), st.sem("high_kept"),
                                                 st.sem("low_kept"))
        block = st.block()

        @block.sync
        def _(sp):
            load_ahead(sp)

        def turned_tile(t):
            return ps[:, t, :].rearrange("p (c n) -> p c n", c=KC)

        @block.vector
        def _(dve):
            chain = Chain(dve, step)
            for t in range(NT):
                last = dve.bn_aggr(mv[:, t, :], core.stats[:, t, :])
            chain(last)
            dve.tensor_scalar(var[:, :], mv[:, :, 1], EPS, None, ALU.add).then_inc(var_ready, 1)
            dve.wait_ge(std_ready, 1)
            chain(dve.reciprocal(rstd[:, :], std[:, :]))
            for t in range(NT):
                dve.tensor_scalar(xn[:, t, :], x[:, t, :], mv[:, t, 0:1], rstd[:, t:t + 1],
                                  ALU.subtract, ALU.mult).then_inc(xn_ready, 1)
            for t in range(NT):
                dve.wait_ge(high_kept, t + 1)
                dve.tensor_tensor(core.xl[:, :, t * P:(t + 1) * P], turned_tile(t),
                                  f32(core.xh[:, :, t * P:(t + 1) * P]), ALU.subtract).then_inc(low_kept, 1)

        @block.scalar
        def _(act):
            act.wait_ge(var_ready, 1)
            act.activation(std[:, :], var[:, :], ACT.Sqrt).then_inc(std_ready, 1)
            for t in range(NT):
                act.wait_ge(turned, t + 1)
                act.activation(core.xh[:, :, t * P:(t + 1) * P], turned_tile(t), ACT.Copy).then_inc(high_kept, 1)

        @block.tensor
        def _(pe):
            for t in range(NT):
                pe.wait_ge(xn_ready, t + 1)
                for c in range(KC):
                    last = pe.transpose(ps[:, t, c * P:(c + 1) * P], xn[:, t, c * P:(c + 1) * P], core.ident[:, :])
                last.then_inc(turned, 1)


class FirstWeights:

    def __init__(self, core, stage, name, shared_kv=False):
        self.ins, self.name, self.shared_kv = core.ins, name, shared_kv
        self.w, self.w_in = stage.sb("w", [P, 1 if shared_kv else 3, KC, P]), stage.sem("w_in")
        if shared_kv:
            self.wkv, self.wkv_in = stage.sb("wkv", [P, KC, P]), stage.sem("wkv_in")

    def load(self, sp):
        if self.shared_kv:
            sp.dma_start(self.wkv[:, :, :], self.ins[self.name + "_wkv"]).then_inc(self.wkv_in, 16)
        sp.dma_start(self.w[:, :, :, :], self.ins[self.name + "_wqkv"][0]).then_inc(self.w_in, 16)


def attention(core, name, first, oh, ol, wo_in, G, E, scale, denominator, causal, shared_kv, qk_bias=None, v_bias=None,
              load_ahead=None):
    ins, ps = core.ins, core.ps
    CH = 32 // E
    NC = U // CH
    M = U * E
    parts = 1 if causal else 2
    if causal:
        qside = [[(3, 0, 512), (2, 512, 384), (0, 896, 128), (1, 1024, 256)]]
        kside = [[(0, 0, 512), (1, 512, 384), (3, 896, 128), (2, 1024, 256)]]
    else:
        qside = kside = [[(0, 0, 512), (1, 512, 512)], [(2, 0, 512), (3, 512, 512)]]
    SIZE = 1280 if causal else 1024
    NPR = U // 2
    LEAD = NPR - 1
    NU = U * parts
    MROW = 48
    NW = 1 if shared_kv else 3
    NB = (qk_bias is not None) + (v_bias is not None)
    KS = B if shared_kv else 1
    with Stage(core, name) as st:
        w, w_in = first.w, first.w_in
        wh = st.sb("wh", [P, NW, KC, P], F32R)
        wl = st.sb("wl", [P, NW, KC, P], F32R)
        qf = st.sb("qf", [P, T])
        kf = st.sb("kf", [P, T])
        vf = st.sb("vf", [M, T])
        qh = st.sb("qh", [P, T], F32R)
        ql = st.sb("ql", [P, T], F32R)
        kh = st.sb("kh", [P, KS, T], F32R)
        kl = st.sb("kl", [P, KS, T], F32R)
        spread = st.sb("spread", [P, 4, NPR, P], F32R)
        qpair = st.sb("qpair", [P, NPR, T], F32R)
        qmax = st.sb("qmax", [P, T], F32R)
        khead = st.sb("khead", [P, B if shared_kv else NPR, 2, T], F32R)
        halves = st.sb("halves", [P, 2, 2])
        vaug = st.sb("vaug", [P, B, QT, CH if shared_kv else U, 64])
        mcol = st.sb("mcol", [P, NPR, QT, P])
        probs = st.sb("probs", [P, 2, 1280 if causal else 2048])
        num = st.sb("numerators", [M, T])
        den = st.sb("denominators", [M, T])
        o = st.sb("o", [M, T])
        mask = st.sb("mask", [P, P])
        maskb = st.sb("maskb", [P, P], BF16)
        cutoff = st.sb("cutoff", [P, P])
        qkb = st.sb("qkb", [P, 2])
        vb = st.sb("vb", [P, M])

        consts_in, cleared, consts_made = st.sem("consts_in"), st.sem("cleared"), st.sem("consts_made")
        mcol_cleared = st.sem("mcol_cleared")
        bias_in = st.sem("bias_in")
        w_high, w_low, freed = st.sem("w_high"), st.sem("w_low"), st.sem("freed")
        projected = st.sem("projected")
        q_full, q_high, q_low = st.sem("q_full"), st.sem("q_high"), st.sem("q_low")
        k_full, k_high, k_low, v_kept = st.sem("k_full"), st.sem("k_high"), st.sem("k_low"), st.sem("v_kept")
        v_full, v_turned = st.sem("v_full"), st.sem("v_turned")
        spread_done, spread_kept = st.sem("spread_done"), st.sem("spread_kept")
        rows_scored, max_taken, banks_left = st.sem("rows_scored"), st.sem("max_taken"), st.sem("banks_left")
        max_turned, max_added = st.sem("max_turned"), st.sem("max_added")
        cols_scored, exp_done, cut_done = st.sem("cols_scored"), st.sem("exp_done"), st.sem("cut_done")
        pv_done = st.sem("pv_done")
        num_kept, den_kept = st.sem("num_kept"), st.sem("den_kept")
        rec_done, normed, o_high, o_kept = st.sem("rec_done"), st.sem("normed"), st.sem("o_high"), st.sem("o_kept")
        kv_split, kv_projected, kv_high, kv_low = (st.sem("kv_split"), st.sem("kv_projected"), st.sem("kv_high"),
                                                   st.sem("kv_low"))
        side_kept, side_turned, values_kept, kv_spread, khead_kept = (
            st.sem("side_kept"), st.sem("side_turned"), st.sem("values_kept"), st.sem("kv_spread"), st.sem("khead_kept"))
        if shared_kv:
            wkv, wkv_in = first.wkv, first.wkv_in
            wkvh = st.sb("wkvh", [P, KC, P], F32R)
            wkvl = st.sb("wkvl", [P, KC, P], F32R)
            side = st.sb("side", [P, N])
        block = st.block()

        X = ps[:, 0:3, :].rearrange("p b n -> p (b n)")
        Y = ps[:, 3:6, :].rearrange("p b n -> p (b n)")
        Z = ps[:, 6:8, :].rearrange("p b n -> p (b n)")

        def startup_banks(p, n):
            return (Y, X)[(p * 2 * parts + n) % 2]

        def ahead(r, p, nxt):
            if p == 0:
                return r[0], r[1], LEAD
            return nxt and (nxt[0], nxt[1], p - 1)

        def follows(g, b, last):
            return None if last else (g, 1) if b == 0 else (g + 1, 0)

        def before(g, b):
            return (g - 1, 1) if b == 0 else (g, 0)

        def more(g, b):
            return b == 0 and not (isinstance(g, int) and g == G - 1)

        def finished(g, b, p, first):
            if p == 0:
                return None if first else (*before(g, b), NC - 1)
            return (g, b, 2 * p // CH - 1) if 2 * p % CH == 0 else None

        def before_is_first(g, b):
            return isinstance(g, int) and before(g, b) == (0, 0)

        def rounds(eng, turn):
            turn(0, 0, False, True)
            turn(0, 1, G == 1, False)
            if G > 2:
                with eng.Fori(1, G - 1) as g:
                    for b in range(B):
                        turn(g, b, False, False)
            if G > 1:
                turn(G - 1, 0, False, False)
                turn(G - 1, 1, True, False)

        @block.sync
        def _(sp):
            if NB:
                sp.dma_start(qkb[:, :], qk_bias[0]).then_inc(bias_in, 16)
                sp.dma_start(vb[:, :], v_bias[0].partition_broadcast(P)).then_inc(bias_in, 16)
            sp.dma_start(probs[:, :, 0:2 * NPR * P], ins[f"spread{E}"]).then_inc(consts_in, 16)
            sp.dma_start(halves[:, :, :], ins["halves"]).then_inc(consts_in, 16)
            sp.dma_start(mask[:, :], ins["mask"]).then_inc(consts_in, 16)
            sp.dma_start(cutoff[:, :], ins["cutoff"]).then_inc(consts_in, 16)
            for g, w_piece_in in enumerate(wo_in):
                w_o = ins[f"{name}_wo"]
                sp.dma_start(core.mixed[0:w_o.shape[0], g, :], w_o[:, g, :]).then_inc(w_piece_in, 16)
            if load_ahead:
                load_ahead(sp)
            if G > 1:
                with sp.Fori(0, G - 1) as g:
                    sp.wait_ge(w_low, (g + 1) * NW)
                    sp.sem_inc(freed, 1)
                    sp.dma_start(w[:, :, :, :], ins[name + "_wqkv"][g + 1]).then_inc(w_in, 16)
                    if NB:
                        sp.wait_ge(v_kept, (g + 1) * B)
                        sp.sem_inc(freed, 1)
                        sp.dma_start(qkb[:, :], qk_bias[g + 1]).then_inc(bias_in, 16)
                        sp.dma_start(vb[:, :], v_bias[g + 1].partition_broadcast(P)).then_inc(bias_in, 16)

        @block.gpsimd
        def _(pool):
            def split_low(g):
                for i in range(NW):
                    pool.wait_ge(w_high, g * NW + i + 1)
                    pool.tensor_tensor(wl[:, i, :, :], w[:, i, :, :], f32(wh[:, i, :, :]), ALU.subtract).then_inc(w_low, 1)

            def low_out(g, b):
                pool.wait_ge(o_high, g * B + b + 1)
                pool.tensor_tensor(ol[0:M, g, b * T:(b + 1) * T], o[:, :],
                                   f32(oh[0:M, g, b * T:(b + 1) * T]), ALU.subtract).then_inc(o_kept, 1)

            def turn(g, b, last_round, first):
                if more(g, b):
                    split_low(g + 1)
                if not first:
                    low_out(*before(g, b))

            pool.memset(mcol[:, :, :, :], 0.0).then_inc(mcol_cleared, 1)
            split_low(0)
            rounds(pool, turn)
            low_out(G - 1, 1)

        @block.tensor
        def _(pe):
            def w_piece(i):
                return [(wh[:, i, c, :], wl[:, i, c, :]) for c in range(KC)]

            def project(g, b, first=False):
                r = g * B + b
                pe.wait_ge(w_low, g * NW + NW)
                if not first:
                    pe.wait_ge(max_taken, r * NU)
                last = product(pe, ps[:, 3, :], w_piece(0), xrows(core, b * T, T))
                if not shared_kv:
                    product(pe, ps[:, 4, :], w_piece(1), xrows(core, b * T, T))
                    last = product(pe, ps[0:M, 5, :], [(wh[:, 2, c, 0:M], wl[:, 2, c, 0:M]) for c in range(KC)],
                                   xrows(core, b * T, T))
                last.then_inc(projected, 1)

            def turn_values(g, b):
                pe.wait_ge(v_full, g * B + b + 1)
                for i in range(QT):
                    last = pe.transpose(ps[:, 5, i * M:(i + 1) * M], vf[:, i * P:(i + 1) * P], core.ident[0:M, 0:M])
                last.then_inc(v_turned, 1)

            def spread_pair(g, b, p, out, first=False):
                r = g * B + b
                if p == 0:
                    pe.wait_ge(q_low, r + 1)
                    if not shared_kv:
                        pe.wait_ge(k_low, r + 1)
                        pe.wait_ge(v_kept, r + 1)
                if first and p > 0:
                    pe.wait_ge(spread_kept, p)
                elif not first:
                    pe.wait_ge(banks_left if causal else max_taken, r * NU + p * 2 * parts)
                pe.matmul(out[:, 0:T], spread[:, 0, p, :], qh[:, :], start=True, stop=False)
                last = pe.matmul(out[:, 0:T], spread[:, 1, p, :], ql[:, :], start=False, stop=True)
                if not shared_kv:
                    pe.matmul(out[:, T:2 * T], spread[:, 2, p, :], kh[:, 0, :], start=True, stop=False)
                    last = pe.matmul(out[:, T:2 * T], spread[:, 3, p, :], kl[:, 0, :], start=False, stop=True)
                last.then_inc(spread_done, 1)

            def rows(g, b, p, n, S=Y, sets=1):
                r = g * B + b
                if n == 0:
                    pe.wait_ge(spread_kept, r * NPR + p + 1)
                if sets == 1 or p * 2 * parts + n >= sets:
                    pe.wait_ge(max_taken, r * NU + p * 2 * parts + n + 1 - sets)
                keys = khead[:, b if shared_kv else p, n // parts, :]
                for i, off, size in qside[n % parts]:
                    last = pe.matmul(S[:, off:off + size], qpair[:, p, i * P:(i + 1) * P], keys[:, 0:size],
                                     start=True, stop=not causal)
                    if causal:
                        last = pe.matmul(S[:, off + size - P:off + size], core.identb[:, :], maskb[:, :],
                                         start=False, stop=True)
                last.then_inc(rows_scored, 1)

            def turn_maxima(g, b, p):
                r = g * B + b
                pe.wait_ge(max_taken, r * NU + (p + 1) * 2 * parts)
                for i in range(QT):
                    last = pe.transpose(X[:, i * P:(i + 1) * P], mcol[:, p, i, :], core.ident[:, :])
                last.then_inc(max_turned, 1)

            def cols(g, b, p, n, first):
                r = g * B + b
                done = r * NU + p * 2 * parts + n
                if n == 0:
                    pe.wait_ge(max_added, r * NPR + p + 1)
                else:
                    pe.wait_ge(exp_done, done)
                for k, off, size in kside[n % parts]:
                    q0 = T - size
                    last = pe.matmul(X[:, off:off + size], khead[:, b if shared_kv else p, n // parts, k * P:(k + 1) * P],
                                     qmax[:, q0:T], start=True, stop=True)
                last.then_inc(cols_scored, 1)

            def weigh(g, b, u, first, blocks=(0, QT)):
                r = g * B + b
                pe.wait_ge(cut_done if causal else exp_done, r * NU + (u + 1) * parts)
                c, h = u // CH, u % CH
                if h == 0 and blocks[0] == 0 and not (first and c < 2):
                    pe.wait_ge(num_kept, r * NC + c - 1)
                    pe.wait_ge(den_kept, r * NC + c - 1)
                tiles = [(k, part * 1024 + off, size) for part in range(parts) for k, off, size in kside[part]]
                for k, off, size in tiles[blocks[0]:blocks[1]]:
                    last_block = h == CH - 1 and k == tiles[-1][0]
                    last = pe.matmul(ps[0:64, 6 + c % 2, T - size:T], vaug[:, b, k, h if shared_kv else u, :],
                                     probs[:, u % 2, off:off + size], start=(h == 0 and k == 0), stop=last_block,
                                     skip_group_check=True)
                if blocks[1] == QT:
                    last.then_inc(pv_done, 1)

            def turn(g, b, last_round, first):
                nxt = follows(g, b, last_round)
                for p in range(NPR):
                    lead = ahead((g, b), p, nxt)
                    cols(g, b, p, 0, first)
                    if p == 1 and nxt:
                        project(*nxt)
                    if lead and p != 1:
                        spread_pair(*lead, Y)
                    if p > 0:
                        weigh(g, b, 2 * p - 1, first)
                    elif not first:
                        weigh(*before(g, b), U - 1, False)
                    if lead and p == 1:
                        if not shared_kv:
                            turn_values(*nxt)
                        spread_pair(*lead, Y)
                    if parts == 2:
                        cols(g, b, p, 1, first)
                    if lead and p != 1:
                        rows(*lead, 0)
                    cols(g, b, p, parts, first)
                    if lead and p == 1:
                        rows(*lead, 0)
                    if parts == 2 and lead:
                        rows(*lead, 1)
                    weigh(g, b, 2 * p, first, (0, 2))
                    if parts == 2:
                        cols(g, b, p, 3, first)
                        if lead:
                            rows(*lead, 2)
                        weigh(g, b, 2 * p, first, (2, QT))
                    pe.wait_ge(exp_done, (g * B + b) * NU + (p + 1) * 2 * parts)
                    if p < NPR - 1:
                        turn_maxima(g, b, p + 1)
                    elif nxt:
                        turn_maxima(*nxt, 0)
                    if lead:
                        rows(*lead, 2 * parts - 1)
                    if parts == 1:
                        weigh(g, b, 2 * p, first, (2, QT))

            if shared_kv:
                pe.wait_ge(kv_split, 2)
                for b in range(B):
                    last = product(pe, ps[:, b, :], [(wkvh[:, c, :], wkvl[:, c, :]) for c in range(KC)],
                                   xrows(core, b * T, T))
                last.then_inc(kv_projected, 1)
            project(0, 0, first=True)
            pe.wait_ge(consts_made, 4)
            if not shared_kv:
                turn_values(0, 0)
            if shared_kv:
                pe.wait_ge(kv_low, B)
                for b in range(B):
                    pe.matmul(ps[:, 4 + b, :], spread[:, 2, 0, :], kh[:, b, :], start=True, stop=False)
                    last = pe.matmul(ps[:, 4 + b, :], spread[:, 3, 0, :], kl[:, b, :], start=False, stop=True)
                last.then_inc(kv_spread, 1)
                pe.wait_ge(side_kept, B)
                for t in range(NT):
                    last = pe.transpose(ps[:, 6 + t // QT, (t % QT) * P:(t % QT + 1) * P],
                                        side[:, t * P:(t + 1) * P], core.ident[:, :])
                last.then_inc(side_turned, 1)
                pe.wait_ge(khead_kept, B)
                pe.wait_ge(values_kept, 1)
            spread_pair(0, 0, 0, Z, True)
            for p in range(LEAD):
                for n in range(2 * parts):
                    rows(0, 0, p, n, startup_banks(p, n), 2)
                    if n == 0 and p + 1 < LEAD:
                        spread_pair(0, 0, p + 1, Z, True)
            pe.wait_ge(max_taken, LEAD * 2 * parts)
            turn_maxima(0, 0, 0)
            rounds(pe, turn)
            weigh(G - 1, 1, U - 1, False)

        @block.scalar
        def _(act):
            def split_high(g):
                act.wait_ge(w_in, g * 16 + 16)
                for i in range(NW):
                    act.activation(wh[:, i, :, :], w[:, i, :, :], ACT.Copy).then_inc(w_high, 1)

            def keep_keys(slot, source):
                for h in range(2):
                    last = act.activation(khead[:, slot, h, :], source, ACT.Identity, scale=halves[:, h, 0:1],
                                          bias=halves[:, h, 1:2])
                return last

            if shared_kv:
                act.wait_ge(wkv_in, 16)
                act.activation(wkvh[:, :, :], wkv[:, :, :], ACT.Copy).then_inc(kv_split, 1)
            split_high(0)
            act.wait_ge(consts_in, 64)
            act.activation(spread[:, 0:2, :, :], probs[:, 0, 0:2 * NPR * P].rearrange("p (a b n) -> p a b n", a=2, n=P),
                           ACT.Copy).then_inc(consts_made, 1)
            if shared_kv:
                act.wait_ge(kv_projected, 1)
                for b in range(B):
                    act.activation(side[:, b * T:(b + 1) * T], ps[:, b, :], ACT.Copy).then_inc(side_kept, 1)
                for b in range(B):
                    act.wait_ge(side_kept, b + 1)
                    act.activation(kh[:, b, :], side[:, b * T:(b + 1) * T], ACT.Copy).then_inc(kv_high, 1)

            def queries(g, b):
                r = g * B + b
                act.wait_ge(projected, r + 1)
                if not shared_kv:
                    act.activation(vf[:, :], ps[0:M, 5, :], ACT.Copy).then_inc(v_full, 1)
                if qk_bias is not None:
                    act.wait_ge(bias_in, g * 32 + 32)
                    act.activation(qf[:, :], Y[:, 0:T], ACT.Identity, bias=qkb[:, 0:1]).then_inc(q_full, 1)
                    act.wait_ge(q_full, r + 1)
                    act.activation(qh[:, :], qf[:, :], ACT.Copy).then_inc(q_high, 1)
                else:
                    act.activation(qh[:, :], Y[:, 0:T], ACT.Copy).then_inc(q_high, 1)
                if not shared_kv:
                    act.wait_ge(k_full, r + 1)
                    act.activation(kh[:, 0, :], kf[:, :], ACT.Copy).then_inc(k_high, 1)

            def keep_spread(g, b, p, source):
                act.wait_ge(spread_done, (g * B + b) * NPR + p + 1)
                last = act.activation(qpair[:, p, :], source[:, 0:T], ACT.Copy)
                if not shared_kv:
                    last = keep_keys(p, source[:, T:2 * T])
                last.then_inc(spread_kept, 1)

            def keep_out(g, b):
                act.wait_ge(normed, g * B + b + 1)
                act.activation(oh[0:M, g, b * T:(b + 1) * T], o[:, :], ACT.Copy).then_inc(o_high, 1)

            def keep_denominators(g, b, c, first):
                if c == 0 and not first:
                    act.wait_ge(normed, g * B + b)
                act.wait_ge(pv_done, (g * B + b) * U + (c + 1) * CH)
                act.activation(den[c * 32:(c + 1) * 32, :], ps[32:64, 6 + c % 2, :], ACT.Copy).then_inc(den_kept, 1)

            def exponentials(g, b, p, n):
                r = g * B + b
                act.wait_ge(cols_scored, r * NU + p * 2 * parts + n + 1)
                h, part = n // parts, n % parts
                if part == 0 and p > 0:
                    act.wait_ge(pv_done, r * U + 2 * p + h - 1)
                act.activation(probs[:, h, part * 1024:part * 1024 + SIZE], X[:, 0:SIZE], ACT.Exp,
                               scale=scale).then_inc(exp_done, 1)

            def turn(g, b, last_round, first):
                nxt = follows(g, b, last_round)
                for p in range(NPR):
                    lead = ahead((g, b), p, nxt)
                    exponentials(g, b, p, 0)
                    if p == 1 and nxt:
                        queries(*nxt)
                    if lead:
                        keep_spread(*lead, Y)
                    if p == 1 and not first:
                        keep_out(*before(g, b))
                    for n in range(1, parts):
                        exponentials(g, b, p, n)
                    if finished(g, b, p, first):
                        keep_denominators(*finished(g, b, p, first), first)
                    for n in range(parts, 2 * parts):
                        exponentials(g, b, p, n)
                    if p == 1 and more(g, b):
                        split_high(g + 1)

            queries(0, 0)
            if shared_kv:
                act.wait_ge(kv_spread, 1)
                for b in range(B):
                    keep_keys(b, ps[:, 4 + b, :]).then_inc(khead_kept, 1)
            for p in range(LEAD):
                keep_spread(0, 0, p, Z)
            rounds(act, turn)
            keep_denominators(G - 1, 1, NC - 1, False)
            keep_out(G - 1, 1)

        @block.vector
        def _(dve):
            if shared_kv:
                dve.wait_ge(kv_split, 1)
                dve.tensor_tensor(wkvl[:, :, :], wkv[:, :, :], f32(wkvh[:, :, :]), ALU.subtract).then_inc(kv_split, 1)
            dve.memset(vaug[:, :, :, :, :], 0.0).then_inc(cleared, 1)
            clusters = vaug[:, :, :, :, :].rearrange("p b i (c h) e -> p (b i) c h e", h=CH)
            dve.wait_ge(cleared, 1)
            for h in range(CH):
                last = dve.memset(clusters[:, :, :, h, 32 + h * E:32 + (h + 1) * E], denominator)
            last.then_inc(consts_made, 1)
            dve.wait_ge(consts_in, 64)
            dve.tensor_copy(spread[:, 2:4, :, :], probs[:, 1, 0:2 * NPR * P].rearrange("p (a b n) -> p a b n", a=2, n=P)).then_inc(consts_made, 1)
            dve.tensor_copy(maskb[:, :], mask[:, :]).then_inc(consts_made, 1)
            if shared_kv:
                for b in range(B):
                    dve.wait_ge(kv_high, b + 1)
                    dve.tensor_tensor(kl[:, b, :], side[:, b * T:(b + 1) * T], f32(kh[:, b, :]), ALU.subtract).then_inc(kv_low, 1)

            def keep_values():
                dve.wait_ge(side_turned, 1)
                for b in range(B):
                    turned = ps[:, 6 + b, :].rearrange("p (i n) -> p i n", n=P)
                    for h in range(CH):
                        last = dve.tensor_copy(clusters[:, b * QT:(b + 1) * QT, 0, h, h * E:(h + 1) * E],
                                               turned[:, :, 2 * E:3 * E])
                    last = dve.tensor_copy(core.logits0[:, b * QT:(b + 1) * QT, :], turned[:, :, 3 * E:3 * E + 8])
                last.then_inc(values_kept, 1)

            def projections(g, b):
                r = g * B + b
                if not shared_kv:
                    dve.wait_ge(projected, r + 1)
                    if qk_bias is not None:
                        dve.wait_ge(bias_in, g * 32 + 32)
                    dve.tensor_scalar(kf[:, :], Y[:, T:2 * T], qkb[:, 1:2], None, ALU.add).then_inc(k_full, 1)
                    dve.wait_ge(k_full, r + 1)
                dve.wait_ge(q_high, r + 1)
                dve.tensor_tensor(ql[:, :], qf[:, :] if qk_bias is not None else Y[:, 0:T], f32(qh[:, :]),
                                  ALU.subtract).then_inc(q_low, 1)
                if not shared_kv:
                    dve.wait_ge(k_high, r + 1)
                    dve.tensor_tensor(kl[:, 0, :], kf[:, :], f32(kh[:, 0, :]), ALU.subtract).then_inc(k_low, 1)
                    dve.wait_ge(v_turned, r + 1)
                    for h in range(CH):
                        last = dve.tensor_tensor(
                            clusters[:, b * QT:(b + 1) * QT, :, h, h * E:(h + 1) * E],
                            Y[:, 2 * T:2 * T + QT * M].rearrange("p (i c h e) -> p i c h e", i=QT, h=CH, e=E)[:, :, :, h, :],
                            vb[:, :].rearrange("p (c h e) -> p c h e", h=CH, e=E)[:, :, h, :].unsqueeze(1)
                            .broadcast_to([P, QT, NC, E]), ALU.add)
                    last.then_inc(v_kept, 1)

            def maxima(g, b, p, n, S=Y):
                dve.wait_ge(rows_scored, (g * B + b) * NU + p * 2 * parts + n + 1)
                row = 64 * (n // parts) + MROW
                for k, (i, off, size) in enumerate(qside[n % parts]):
                    last = dve.reduce_max(mcol[:, p, i, row:row + 1], S[:, off:off + size], AX.X)
                    if causal and k == (0 if shared_kv else 2):
                        last.then_inc(banks_left, 1)
                last.then_inc(max_taken, 1)

            def cut(g, b, p, h):
                if causal:
                    dve.wait_ge(exp_done, (g * B + b) * NU + 2 * p + h + 1)
                    e = probs[:, h, :]
                    thirds = e[:, 0:1280].rearrange("p (c n) -> p c n", n=P)[:, 0:9:4, :]
                    dve.tensor_tensor(thirds, thirds, cutoff[:, :].unsqueeze(1).broadcast_to([P, 3, P]), ALU.min)
                    dve.tensor_tensor(e[:, 896:1024], e[:, 896:1024], cutoff[:, :], ALU.min).then_inc(cut_done, 1)

            def add_maxima(g, b, p):
                dve.wait_ge(max_turned, (g * B + b) * NPR + p + 1)
                dve.tensor_tensor(qmax[:, :], X[:, 0:T], f32(qpair[:, p, :]), ALU.add).then_inc(max_added, 1)

            def keep_numerators(g, b, c, first):
                if c == 0 and not first:
                    dve.wait_ge(normed, g * B + b)
                dve.wait_ge(pv_done, (g * B + b) * U + (c + 1) * CH)
                dve.tensor_copy(num[c * 32:(c + 1) * 32, :], ps[0:32, 6 + c % 2, :]).then_inc(num_kept, 1)

            def norm(g, b, first):
                r = g * B + b
                dve.wait_ge(den_kept, (r + 1) * NC)
                dve.reciprocal(den[:, :], den[:, :]).then_inc(rec_done, 1)
                dve.wait_ge(rec_done, r + 1)
                dve.wait_ge(num_kept, (r + 1) * NC)
                if not first:
                    dve.wait_ge(o_kept, r)
                dve.tensor_tensor(o[:, :], num[:, :], den[:, :], ALU.mult).then_inc(normed, 1)

            def turn(g, b, last_round, first):
                nxt = follows(g, b, last_round)
                for p in range(NPR):
                    lead = ahead((g, b), p, nxt)
                    if p == 1 and nxt:
                        projections(*nxt)
                    cut(g, b, p, 0)
                    if lead:
                        maxima(*lead, 0)
                    if finished(g, b, p, first):
                        keep_numerators(*finished(g, b, p, first), first)
                    if lead:
                        for n in range(1, 2 * parts - 1):
                            maxima(*lead, n)
                    if p < NPR - 1:
                        add_maxima(g, b, p + 1)
                    elif nxt:
                        add_maxima(*nxt, 0)
                    if lead:
                        maxima(*lead, 2 * parts - 1)
                    cut(g, b, p, 1)
                    if p == 0 and not first:
                        norm(*before(g, b), before_is_first(g, b))

            projections(0, 0)
            if shared_kv:
                keep_values()
            dve.wait_ge(mcol_cleared, 1)
            for p in range(LEAD):
                for n in range(2 * parts):
                    maxima(0, 0, p, n, startup_banks(p, n))
            add_maxima(0, 0, 0)
            rounds(dve, turn)
            keep_numerators(G - 1, 1, NC - 1, False)
            norm(G - 1, 1, False)


def project_out(core, name, oh, ol, w_in, G, M, bias_d=None):
    ps, mixed = core.ps, core.mixed
    with Stage(core, name) as st:
        w = mixed[0:M, 0:G, :]
        wh = st.sb("wh", [M, G, D], F32R)
        wl = st.sb("wl", [M, G, D], F32R)
        bias = st.sb("bias", [P, D])
        bias_in = st.sem("bias_in")
        done, w_high, w_low = st.sem("done"), st.sem("w_high"), st.sem("w_low")
        kept = st.sem("kept_v"), st.sem("kept_s")
        block = st.block()

        @block.sync
        def _(sp):
            if bias_d is not None:
                sp.dma_start(bias[:, :], bias_d.partition_broadcast(P)).then_inc(bias_in, 16)

        @block.tensor
        def _(pe):
            pe.wait_ge(w_low, G)
            for t in range(NT):
                product(pe, ps[:, t, :], [(oh[0:M, g, t * P:(t + 1) * P], ol[0:M, g, t * P:(t + 1) * P]) for g in range(G)],
                        [(wh[:, g, :], wl[:, g, :]) for g in range(G)]).then_inc(done, 1)

        @block.vector
        def _(dve):
            for g in range(G):
                dve.wait_ge(w_high, g + 1)
                dve.tensor_tensor(wl[:, g, :], w[:, g, :], f32(wh[:, g, :]), ALU.subtract).then_inc(w_low, 1)
            if bias_d is not None:
                dve.wait_ge(bias_in, 16)
            for t in range(NT) if bias_d is not None else range(0, NT, 2):
                dve.wait_ge(done, t + 1)
                if bias_d is not None:
                    dve.tensor_tensor(mixed[:, t, :], ps[:, t, :], bias[:, :], ALU.add).then_inc(kept[0], 1)
                else:
                    dve.tensor_copy(mixed[:, t, :], ps[:, t, :]).then_inc(kept[0], 1)

        @block.scalar
        def _(act):
            for g in range(G):
                act.wait_ge(w_in[g], 16)
                act.activation(wh[:, g, :], w[:, g, :], ACT.Copy).then_inc(w_high, 1)
            if bias_d is None:
                for t in range(1, NT, 2):
                    act.wait_ge(done, t + 1)
                    act.activation(mixed[:, t, :], ps[:, t, :], ACT.Copy).then_inc(kept[1], 1)


def gate_steps(core, dve, t, f, th, gated, chain, x_done):
    chain(dve.scalar_tensor_tensor(out=gated, in0=th, scalar=1.0, in1=f, op0=ALU.add, op1=ALU.mult))
    chain(dve.scalar_tensor_tensor(out=gated, in0=gated, scalar=0.5, in1=core.mixed[:, t, :],
                                   op0=ALU.mult, op1=ALU.mult))
    dve.tensor_tensor(core.x[:, t, :], core.x[:, t, :], gated, ALU.add).then_inc(x_done, 1)


def experts(core, name, we, be, w_in):
    ins, ps = core.ins, core.ps
    NE = 8
    with Stage(core, name) as st:
        bg = st.sb("bg", [P, NE])
        weh = st.sb("weh", [P, 2, KC, D], F32R)
        wel = st.sb("wel", [P, 2, KC, D], F32R)
        logits = st.sb("logits", [P, NT, NE])
        best = st.sb("best", [P, NT, 8])
        where = st.sb("where", [P, NT, 8], U32)
        wheref = st.sb("wheref", [P, NT, 8])
        iota = st.sb("iota", [P, NE])
        pick = st.sb("pick", [P, 2, NT, NE])
        share = st.sb("share", [P, NT, NE])
        now = st.sb("now", [P, 2, NT])
        biased = st.sb("biased", [P, 2, D])
        acted = st.sb("acted", [P, 2, D])
        f = st.sb("f", [P, NT, D])
        th = st.sb("th", [P, 2, D])
        gated = st.sb("gated", [P, D])
        step, consts_in = st.sem("step"), st.sem("consts_in")
        w_high, w_low = st.sem("w_high"), st.sem("w_low")
        b_used, freed = st.sem("b_used"), st.sem("freed")
        mm_done, biased_done, acted_done, summed = (
            st.sem("mm_done"), st.sem("biased_done"), st.sem("acted_done"), st.sem("summed"))
        cleared, now_done = st.sem("cleared"), st.sem("now_done")
        tanh_done, x_done = st.sem("tanh_done"), st.sem("x_done")
        block = st.block()

        def each(eng, one):
            one(0, 0, True, False)
            one(0, 1, True, False)
            with eng.Fori(1, NE // 2 - 1) as j:
                for s in range(2):
                    one(j, s, False, False)
            one(NE // 2 - 1, 0, False, False)
            one(NE // 2 - 1, 1, False, True)

        @block.sync
        def _(sp):
            sp.dma_start(bg[:, :], ins["l0_bgate"].partition_broadcast(P)).then_inc(consts_in, 16)
            sp.dma_start(iota[:, :], ins["iota8"].partition_broadcast(P)).then_inc(consts_in, 16)

            def load(j, s, first, last):
                e = j * 2 + s
                if first:
                    return
                sp.wait_ge(w_low, (e - 1) * KC)
                sp.sem_inc(freed, 1)
                sp.wait_ge(b_used, e - 1)
                sp.sem_inc(freed, 1)
                sp.dma_start(we[:, s, :, :], ins["l0_we"][e]).then_inc(w_in[s], 16)
                sp.dma_start(be[:, s, :], ins["l0_be"][e].partition_broadcast(P)).then_inc(w_in[s], 16)

            each(sp, load)

        @block.tensor
        def _(pe):
            def compute(j, s, first, last):
                e = j * 2 + s
                pe.wait_ge(w_low, e * KC + KC)
                for t in range(NT):
                    n = s * NT + t
                    if not first or n >= 4:
                        pe.wait_ge(biased_done, e * NT + t - 3)
                    product(pe, ps[:, n % 4, :], xrows(core, t * P, P),
                            [(weh[:, s, c, :], wel[:, s, c, :]) for c in range(KC)]).then_inc(mm_done, 1)

            each(pe, compute)

        @block.vector
        def _(dve):
            chain = Chain(dve, step)
            for c in range(KC // 2):
                dve.wait_ge(w_high, c + 1)
                dve.tensor_tensor(wel[:, 0, c, :], we[:, 0, c, :], f32(weh[:, 0, c, :]), ALU.subtract).then_inc(w_low, 1)
            dve.wait_ge(consts_in, 32)
            chain(dve.tensor_tensor(logits[:, :, :], core.logits0[:, :, :],
                                    bg[:, :].unsqueeze(1).broadcast_to([P, NT, NE]), ALU.add))
            for t in range(NT):
                last = dve.max(best[:, t, :], logits[:, t, :])
            chain(last)
            for t in range(NT):
                last = dve.max_index(where[:, t, :], best[:, t, :], logits[:, t, :])
            chain(last)
            chain(dve.tensor_copy(wheref[:, :, :], where[:, :, :]))
            for k in range(2):
                last = dve.tensor_tensor(pick[:, k, :, :], iota[:, :].unsqueeze(1).broadcast_to([P, NT, NE]),
                                         wheref[:, :, k:k + 1].broadcast_to([P, NT, NE]), ALU.is_equal)
            chain(last)
            chain(dve.tensor_tensor(share[:, :, :], pick[:, 0, :, :], pick[:, 1, :, :], ALU.add))
            chain(dve.tensor_scalar(share[:, :, :], share[:, :, :], 0.5, None, ALU.mult))

            def gate(t):
                dve.wait_ge(tanh_done, t + 1)
                gate_steps(core, dve, t, f[:, t, :], th[:, t % 2, :], gated[:, :], chain, x_done)
                dve.wait_ge(x_done, t + 1)
                dve.bn_stats(core.stats[:, t, :], core.x[:, t, :])

            def add_bias(j, s, first, last):
                e = j * 2 + s
                if not first:
                    dve.wait_ge(acted_done, (e - 1) * NT)
                dve.tensor_copy(now[:, s, :].unsqueeze(2), share[:, :, bass.ds(e, 1)]).then_inc(now_done, 1)
                dve.wait_ge(w_in[s], j * 32 + 32)
                for t in range(NT):
                    n = s * NT + t
                    dve.wait_ge(mm_done, e * NT + t + 1)
                    if not first or n >= 2:
                        dve.wait_ge(acted_done, e * NT + t - 1)
                    dve.tensor_tensor(biased[:, t % 2, :], ps[:, n % 4, :], be[:, s, :], ALU.add).then_inc(biased_done, 1)
                    if last and t >= 3:
                        gate(t - 3)
                dve.wait_ge(biased_done, e * NT + NT)
                dve.sem_inc(b_used, 1)

            each(dve, add_bias)
            for t in range(NT - 3, NT):
                gate(t)

        @block.scalar
        def _(act):
            def split(e1, s1, c):
                act.activation(weh[:, s1, c, :], we[:, s1, c, :], ACT.Copy).then_inc(w_high, 1)

            act.wait_ge(w_in[0], 32)
            for c in range(KC):
                split(0, 0, c)

            def activate(j, s, first, last):
                e = j * 2 + s
                if not last:
                    act.wait_ge(w_in[1 - s], j * 32 + 32 + 32 * s)
                    if not (first and s == 0):
                        act.wait_ge(mm_done, e * NT)
                act_now = now[:, s, :]
                act.wait_ge(now_done, e + 1)
                for t in range(NT):
                    n = s * NT + t
                    if not last and t % 2 == 0:
                        split(None, 1 - s, t // 2)
                    act.wait_ge(biased_done, e * NT + t + 1)
                    if not first or n >= 2:
                        act.wait_ge(summed, e * NT + t - 1)
                    act.activation(acted[:, t % 2, :], biased[:, t % 2, :], ACT.Relu,
                                   scale=act_now[:, t:t + 1]).then_inc(acted_done, 1)
                    if last and t >= 2:
                        tanh(t - 2)

            def tanh(t):
                act.wait_ge(summed, (NE - 1) * NT + t + 1)
                if t >= 2:
                    act.wait_ge(x_done, t - 1)
                act.activation(th[:, t % 2, :], f[:, t, :], ACT.Tanh, scale=0.5).then_inc(tanh_done, 1)

            each(act, activate)
            for t in range(NT - 2, NT):
                tanh(t)

        @block.gpsimd
        def _(pool):
            def low(e1, s1, c):
                pool.wait_ge(w_high, e1 * KC + c + 1)
                pool.tensor_tensor(wel[:, s1, c, :], we[:, s1, c, :], f32(weh[:, s1, c, :]),
                                   ALU.subtract).then_inc(w_low, 1)

            for c in range(KC // 2, KC):
                low(0, 0, c)
            pool.memset(f[:, :, :], 0.0).then_inc(cleared, 1)
            pool.wait_ge(cleared, 1)

            def add(j, s, first, last):
                e = j * 2 + s
                for t in range(NT):
                    if not last and t % 2 == 0:
                        low(e + 1, 1 - s, t // 2)
                    pool.wait_ge(acted_done, e * NT + t + 1)
                    if not first or s == 1:
                        pool.wait_ge(summed, e * NT + t - NT + 1)
                    pool.tensor_tensor(f[:, t, :], f[:, t, :], acted[:, t % 2, :], ALU.add).then_inc(summed, 1)

            each(pool, add)


def dense_gate(core, name, w_d, zT, zw_d, z=None, w=None, w_in=None):
    ps = core.ps
    with Stage(core, name) as st:
        w_given = w is not None
        if not w_given:
            w, w_in = st.sb("w", [P, KC, D]), [st.sem(f"w_in{c}") for c in range(KC)]
        wh = st.sb("wh", [P, KC, D], F32R)
        wl = st.sb("wl", [P, KC, D], F32R)
        zw = st.sb("zw", [P, D])
        th = st.sb("th", [P, 2, D])
        gated = st.sb("gated", [P, D])
        done, tanh_done, x_done, zw_in = st.sem("done"), st.sem("tanh_done"), st.sem("x_done"), st.sem("zw_in")
        step, w_high, w_low = st.sem("step"), st.sem("w_high"), st.sem("w_low")
        z_turned, z_kept, z_cleared = st.sem("z_turned"), st.sem("z_kept"), st.sem("z_cleared")
        block = st.block()

        @block.sync
        def _(sp):
            if not w_given:
                for c in range(KC):
                    sp.dma_start(w[:, c, :], w_d[:, c, :]).then_inc(w_in[c], 16)
            sp.dma_start(zw[:, :], zw_d).then_inc(zw_in, 16)

        @block.tensor
        def _(pe):
            if z is not None:
                R = z.shape[2]
                for t in range(NT):
                    last = pe.transpose(ps[0:R, 6 + t // QT, (t % QT) * P:(t % QT + 1) * P], z[:, t, :], core.ident[:, :])
                last.then_inc(z_turned, 1)
                pe.wait_ge(z_kept, 1)
            pe.wait_ge(w_low, KC)
            pe.wait_ge(zw_in, 16)
            for t in range(NT):
                product(pe, ps[:, t, :], xrows(core, t * P, P), [(wh[:, c, :], wl[:, c, :]) for c in range(KC)],
                        stop=False)
                pe.matmul(ps[:, t, :], zT[:, t * P:(t + 1) * P], zw[:, :], start=False, stop=True).then_inc(done, 1)

        @block.scalar
        def _(act):
            for c in range(KC):
                act.wait_ge(w_in[c], 16)
                act.activation(wh[:, c, :], w[:, c, :], ACT.Copy).then_inc(w_high, 1)
            for t in range(NT):
                act.wait_ge(done, t + 1)
                if t >= 2:
                    act.wait_ge(x_done, t - 1)
                act.activation(th[:, t % 2, :], ps[:, t, :], ACT.Tanh, scale=0.5).then_inc(tanh_done, 1)

        @block.gpsimd
        def _(pool):
            for c in range(KC // 2, KC):
                pool.wait_ge(w_high, c + 1)
                pool.tensor_tensor(wl[:, c, :], w[:, c, :], f32(wh[:, c, :]), ALU.subtract).then_inc(w_low, 1)

        @block.vector
        def _(dve):
            chain = Chain(dve, step)
            if z is not None:
                dve.memset(zT[:, :], 0.0).then_inc(z_cleared, 1)
                dve.wait_ge(z_turned, 1)
                dve.wait_ge(z_cleared, 1)
                dve.tensor_copy(zT[0:z.shape[2], :].rearrange("p (h n) -> p h n", h=2), ps[0:z.shape[2], 6:8, :]).then_inc(z_kept, 1)
            for c in range(KC // 2):
                dve.wait_ge(w_high, c + 1)
                dve.tensor_tensor(wl[:, c, :], w[:, c, :], f32(wh[:, c, :]), ALU.subtract).then_inc(w_low, 1)
            for t in range(NT):
                dve.wait_ge(tanh_done, t + 1)
                gate_steps(core, dve, t, ps[:, t, :], th[:, t % 2, :], gated[:, :], chain, x_done)
                dve.wait_ge(x_done, t + 1)
                dve.bn_stats(core.stats[:, t, :], core.x[:, t, :])


def lora_by_batch(core, name, zT, gate_w, gate_w_in):
    ins, ps = core.ins, core.ps
    NA, S = 3, 4
    with Stage(core, name) as st:
        w = st.sb("w", [P, KC, P])
        wh = st.sb("wh", [P, KC, P], F32R)
        wl = st.sb("wl", [P, KC, P], F32R)
        w_split = st.sem("w_split")
        starts = st.sb("starts", [P, S], I32)
        startf = st.sb("startf", [P, S])
        row = st.sb("row", [P, 2])
        past = st.sb("past", [P, B, S])
        seg = st.sb("seg", [P, B])
        pick = st.sb("pick", [P, B])
        loaded, done, step, kept = st.sem("loaded"), st.sem("done"), st.sem("step"), st.sem("kept")
        block = st.block()

        @block.sync
        def _(sp):
            sp.dma_start(w[:, :, :], ins["l2_wz"]).then_inc(loaded, 16)
            sp.dma_start(starts[:, :], ins["l2_starts"].partition_broadcast(P)).then_inc(loaded, 16)
            sp.dma_start(row[:, :], ins["adapter_of_row"]).then_inc(loaded, 16)
            for c in range(KC):
                sp.dma_start(gate_w[:, c, :], ins["l2_w"][:, c, :]).then_inc(gate_w_in[c], 16)

        @block.tensor
        def _(pe):
            pe.wait_ge(w_split, 2)
            for b in range(B):
                last = product(pe, ps[:, b, :], [(wh[:, c, :], wl[:, c, :]) for c in range(KC)], xrows(core, b * T, T))
            last.then_inc(done, 1)

        @block.vector
        def _(dve):
            chain = Chain(dve, step)
            dve.wait_ge(loaded, 48)
            dve.tensor_copy(wh[:, :, :], w[:, :, :]).then_inc(w_split, 1)
            dve.wait_ge(w_split, 1)
            dve.tensor_tensor(wl[:, :, :], w[:, :, :], f32(wh[:, :, :]), ALU.subtract).then_inc(w_split, 1)
            chain(dve.tensor_copy(startf[:, :], starts[:, :]))
            for b in range(B):
                last = dve.tensor_scalar(past[:, b, :], startf[:, :], float(b), None, ALU.is_le)
            chain(last)
            chain(dve.tensor_reduce(seg[:, :], past[:, :, :], AX.X, ALU.add))
            chain(dve.tensor_scalar(seg[:, :], seg[:, :], -2.0, float(NA - 1), ALU.add, ALU.min))
            chain(dve.tensor_scalar(pick[:, :], seg[:, :], row[:, 0:1], None, ALU.is_equal))
            dve.wait_ge(done, 1)
            for b in range(B):
                last = dve.tensor_scalar(zT[:, b * T:(b + 1) * T], ps[:, b, :], pick[:, b:b + 1], row[:, 1:2],
                                         ALU.mult, ALU.add)
            last.then_inc(kept, 1)


def decays(core, name, w, w_in, rows_d, lw, wst, adapted):
    ins, ps = core.ins, core.ps
    H = 32
    NE, R = 4, 8
    with Stage(core, name) as st:
        wh = st.sb("wh", [P, KC, P], F32R)
        wl = st.sb("wl", [P, KC, P], F32R)
        w_split = st.sem("w_split")
        side = st.sb("side", [P, N])
        route = st.sb("route", [P, NT, NE + NE * R])
        bias = st.sb("bias", [P, NE])
        iota = st.sb("iota", [P, 8])
        logits = st.sb("logits", [P, NT, 8])
        best = st.sb("best", [P, NT, 8])
        where = st.sb("where", [P, NT, 8], U32)
        wheref = st.sb("wheref", [P, NT, 8])
        pick = st.sb("pick", [P, NT, NE])
        dtb = st.sb("dtb", [P, H])
        ab = st.sb("ab", [P, H])
        ea = st.sb("ea", [P, H])
        tri = st.sb("tri", [P, P])
        ones = st.sb("ones", [P, P])
        z = st.sb("z", [P, NT, H])
        az = st.sb("az", [P, NT, H])
        dt = st.sb("dt", [P, NT, H])
        g = st.sb("g", [P, NT, H])
        G = st.sb("G", [P, NT, H])
        lndt = st.sb("lndt", [P, NT, H])
        GT = st.sb("GT", [H, N])
        loaded, done, step = st.sem("loaded"), st.sem("done"), st.sem("step")
        projected = st.sem("projected")
        z_done, a_done, sp_done, dt_done, ln_done = (st.sem("z_done"), st.sem("a_done"), st.sem("sp_done"),
                                                     st.sem("dt_done"), st.sem("ln_done"))
        g_done, G_done, G_kept, d_done, turned, GT_kept, stored = (
            st.sem("g_done"), st.sem("G_done"), st.sem("G_kept"), st.sem("d_done"), st.sem("turned"),
            st.sem("GT_kept"), st.sem("stored"))
        act_step, side_kept, adapted_done = st.sem("act_step"), st.sem("side_kept"), st.sem("adapted_done")
        block = st.block()
        got = ps[:, 6:8, :].rearrange("p b (i c) -> p (b i) c", c=P)

        @block.sync
        def _(sp):
            sp.dma_start(bias[:, :], ins["l1_bz"].partition_broadcast(P)).then_inc(loaded, 16)
            sp.dma_start(iota[:, :], ins["iota8"].partition_broadcast(P)).then_inc(loaded, 16)
            sp.dma_start(dtb[:, :], ins["l1_dtb"].partition_broadcast(P)).then_inc(loaded, 16)
            sp.dma_start(ab[:, :], ins["l1_ab"].partition_broadcast(P)).then_inc(loaded, 16)
            sp.dma_start(tri[:, :], ins["tri"]).then_inc(loaded, 16)
            sp.wait_ge(GT_kept, 2)
            sp.dma_start(rows_d.rearrange("t h n -> h t n"),
                         GT[:, :].rearrange("h (t n) -> h t n", n=P)).then_inc(stored, 16)
            sp.wait_ge(stored, 16)

        @block.tensor
        def _(pe):
            pe.wait_ge(w_split, 2)
            for b in range(B):
                product(pe, ps[:, b * 5, :], [(wh[:, c, :], wl[:, c, :]) for c in range(KC)],
                        xrows(core, b * T, T)).then_inc(projected, 1)
            for t in range(NT):
                pe.wait_ge(side_kept, t // QT + 1)
                last = pe.transpose(got[:, t, :], side[:, t * P:(t + 1) * P], core.ident[:, :])
            last.then_inc(done, 1)
            pe.wait_ge(g_done, 1)
            pe.matmul(ps[:, 1, 0:NT * H], tri[:, :], g[:, :, :].rearrange("p t h -> p (t h)"), start=True, stop=True)
            pe.matmul(ps[:, 2, 0:NT * H], ones[:, :], g[:, :, :].rearrange("p t h -> p (t h)"),
                      start=True, stop=True).then_inc(G_done, 1)
            pe.wait_ge(G_kept, 1)
            for t in range(NT):
                last = pe.transpose(ps[0:H, 3 + t // 4, (t % 4) * P:(t % 4 + 1) * P], G[:, t, :], core.ident[:, :])
            last.then_inc(turned, 1)

        def flat(a):
            return a[:, :, :].rearrange("p t h -> p (t h)")

        @block.scalar
        def _(act):
            act.wait_ge(w_in, 16)
            act.activation(wh[:, :, :], w[:, :, :], ACT.Copy).then_inc(w_split, 1)
            for b in range(B):
                act.wait_ge(projected, b + 1)
                act.activation(side[:, b * T:(b + 1) * T], ps[:, b * 5, :], ACT.Copy).then_inc(side_kept, 1)
            act.wait_ge(loaded, 80)
            act.activation(ea[:, :], ab[:, :], ACT.Exp).then_inc(a_done, 1)
            act.wait_ge(z_done, 1)
            act.activation(az[:, :, :], az[:, :, :], ACT.Exp, scale=-1.0).then_inc(act_step, 1)
            act.wait_ge(act_step, 1)
            act.activation(az[:, :, :], az[:, :, :], ACT.Ln, bias=1.0).then_inc(sp_done, 1)
            act.wait_ge(dt_done, 1)
            act.activation(lndt[:, :, :], dt[:, :, :], ACT.Ln).then_inc(ln_done, 1)
            act.wait_ge(d_done, 1)
            act.activation(wst[:, :, :], wst[:, :, :], ACT.Exp).then_inc(act_step, 1)

        @block.vector
        def _(dve):
            chain = Chain(dve, step)
            chain(dve.memset(ones[:, :], 1.0))
            chain(dve.memset(logits[:, :, :], -3e38))
            dve.wait_ge(w_split, 1)
            dve.tensor_tensor(wl[:, :, :], w[:, :, :], f32(wh[:, :, :]), ALU.subtract).then_inc(w_split, 1)
            dve.wait_ge(loaded, 80)
            dve.wait_ge(done, 1)
            chain(dve.tensor_tensor(z[:, :, :], got[:, :, 0:H],
                                    dtb[:, :].unsqueeze(1).broadcast_to([P, NT, H]), ALU.add))
            chain(dve.tensor_scalar(az[:, :, :], z[:, :, :], -1.0, None, ALU.mult))
            dve.tensor_tensor(az[:, :, :], az[:, :, :], z[:, :, :], ALU.max).then_inc(z_done, 1)
            dve.wait_ge(sp_done, 1)
            dve.scalar_tensor_tensor(out=dt[:, :, :], in0=z[:, :, :], scalar=0.0, in1=az[:, :, :],
                                     op0=ALU.max, op1=ALU.add).then_inc(dt_done, 1)
            dve.wait_ge(dt_done, 1)
            dve.wait_ge(a_done, 1)
            dve.scalar_tensor_tensor(out=g[:, :, :], in0=dt[:, :, :], scalar=-1.0,
                                     in1=ea[:, :].unsqueeze(1).broadcast_to([P, NT, H]),
                                     op0=ALU.mult, op1=ALU.mult).then_inc(g_done, 1)
            dve.wait_ge(G_done, 1)
            dve.tensor_copy(flat(G), ps[:, 1, 0:NT * H]).then_inc(G_kept, 1)
            dve.wait_ge(G_kept, 1)
            dve.wait_ge(ln_done, 1)
            chain(dve.tensor_tensor(lw[:, :, :], G[:, :, :], lndt[:, :, :], ALU.subtract))
            dve.tensor_tensor(flat(wst), ps[:, 2, 0:NT * H], flat(lw), ALU.subtract).then_inc(d_done, 1)
            dve.wait_ge(turned, 1)
            dve.tensor_copy(GT[:, :].rearrange("p (h n) -> p h n", h=2), ps[0:H, 3:5, :]).then_inc(GT_kept, 2)
            chain(dve.tensor_copy(route[:, :, :], got[:, :, H:H + NE + NE * R]))
            chain(dve.tensor_tensor(logits[:, :, 0:NE], route[:, :, 0:NE],
                                    bias[:, :].unsqueeze(1).broadcast_to([P, NT, NE]), ALU.add))
            for t in range(NT):
                last = dve.max(best[:, t, :], logits[:, t, :])
            chain(last)
            for t in range(NT):
                last = dve.max_index(where[:, t, :], best[:, t, :], logits[:, t, :])
            chain(last)
            chain(dve.tensor_copy(wheref[:, :, :], where[:, :, :]))
            chain(dve.tensor_tensor(pick[:, :, :], iota[:, 0:NE].unsqueeze(1).broadcast_to([P, NT, NE]),
                                    wheref[:, :, 0:1].broadcast_to([P, NT, NE]), ALU.is_equal))
            for t in range(NT):
                last = dve.tensor_tensor(adapted[:, t, :].rearrange("p (e r) -> p e r", e=NE),
                                         route[:, t, NE:NE + NE * R].rearrange("p (e r) -> p e r", e=NE),
                                         pick[:, t, :].unsqueeze(2).broadcast_to([P, NE, R]), ALU.mult)
            last.then_inc(adapted_done, 1)


def retention(core, name, rows_d, lw, wst):
    ins, ps, mixed = core.ins, core.ps, core.mixed
    KV, R = 8, 4
    NP = 2 + 3 * R
    RING = NP // 2
    C1 = QT - 1
    with Stage(core, name) as st:
        w = st.sb("w", [P, RING, D])
        wh = st.sb("wh", [P, 2, KC, P], F32R)
        wl = st.sb("wl", [P, 2, KC, P], F32R)
        woh = st.sb("woh", [P, R, D], F32R)
        wol = st.sb("wol", [P, R, D], F32R)
        cos = st.sb("cos", [P, T])
        sin = st.sb("sin", [P, T])
        gw = st.sb("gw", [P, 1])
        eps = st.sb("eps", [P, 1])
        limit = st.sb("limit", [P, P])
        ones = st.sb("ones", [P, P])
        qT = st.sb("qT", [P, R, N])
        silu = st.sb("silu", [P, R, N])
        kT = st.sb("kT", [P, N])
        ktm = st.sb("ktm", [P, NT, P])
        v = st.sb("v", [P, NT, P])
        rows = st.sb("rows", [P, 4, R, P])
        er = st.sb("er", [P, 3, R, P])
        lws = st.sb("lws", [P, NT, R])
        wsts = st.sb("wsts", [P, NT, R])
        vw = st.sb("vw", [P, 2, D])
        a2 = st.sb("a2", [P, 2, D])
        b2 = st.sb("b2", [P, 2, D])
        c2 = st.sb("c2", [P, 2, D])
        state = st.sb("state", [P, D])
        y2 = st.sb("y2", [P, 2, D])
        rinv = st.sb("rinv", [P, 2, D])
        rn = st.sb("rn", [P, D])
        ryh = st.sb("ryh", [P, 2, D], F32R)
        ryl = st.sb("ryl", [P, 2, D], F32R)

        consts_in, ones_made, cleared = st.sem("consts_in"), st.sem("ones_made"), st.sem("cleared")
        w_in = [st.sem(f"w_in{i}") for i in range(RING)]
        rows_in = [st.sem(f"rows_in{i}") for i in range(4)]
        w_high, w_low, freed = st.sem("w_high"), st.sem("w_low"), st.sem("freed")
        jobs_done, kept_v, kept_s = st.sem("jobs_done"), st.sem("kept_v"), st.sem("kept_s")
        dstep, gate_done, kt_done, ktm_done = st.sem("dstep"), st.sem("gate_done"), st.sem("kt_done"), st.sem("ktm_done")
        vt_done, v_done = st.sem("vt_done"), st.sem("v_done")
        raw_done, dec_done, er_done = st.sem("raw_done"), st.sem("dec_done"), st.sem("er_done")
        s_done, sc_done, qg_done, vw_done = st.sem("s_done"), st.sem("sc_done"), st.sem("qg_done"), st.sem("vw_done")
        y_done, cs_done, st_done, y2_done = st.sem("y_done"), st.sem("cs_done"), st.sem("st_done"), st.sem("y2_done")
        ms_done, ln_done, rinv_done = st.sem("ms_done"), st.sem("ln_done"), st.sem("rinv_done")
        rn_done, ryh_done, ryl_done, wo_done, added = (st.sem("rn_done"), st.sem("ryh_done"), st.sem("ryl_done"),
                                                       st.sem("wo_done"), st.sem("added"))
        block = st.block()

        pieces, places = [("k", 0), ("v", 0)], [0, 1]
        for h in range(R):
            pieces += [("q", h), ("g", h)]
            places += [2 + 3 * h + (h == R - 1), 3 + 3 * h + (h == R - 1)]
        wo_places = [p for p in range(NP) if p not in places]
        jobs = [(kind, h, b) for kind, h in pieces for b in range(B)]
        NJ = len(jobs)
        ROPE = [n for n, j in enumerate(jobs) if j[0] in "kq"]
        SIDE = [n for n, j in enumerate(jobs) if j[0] in "vg"]
        PB = 6

        def reads(t):
            return (t // QT) * C1 + t % QT

        def adds(t):
            return (t // QT) * C1 + min(t % QT + 1, C1)

        def tile(a, t):
            return a[:, :, t * P:(t + 1) * P]

        def heads(a):
            return a.rearrange("p (h n) -> p h n", h=R)

        @block.sync
        def _(sp):
            sp.dma_start(cos[:, :], ins["cos"]).then_inc(consts_in, 16)
            sp.dma_start(sin[:, :], ins["sin"]).then_inc(consts_in, 16)
            sp.dma_start(gw[:, :], ins["l1_gw"]).then_inc(consts_in, 16)
            sp.dma_start(limit[:, :], ins["limit"]).then_inc(consts_in, 16)

            def load_w(kv, p):
                turn = kv + p // NP
                if not (isinstance(kv, int) and kv * NP + p < RING):
                    sp.wait_ge(w_low, kv * NP + p - RING + 1)
                    sp.sem_inc(freed, 1)
                sp.dma_start(w[:, p % RING, :], ins["l1_w"][turn, p % NP]).then_inc(w_in[p % RING], 16)

            def load_rows(kv, t):
                turn = kv + t // NT
                if not (isinstance(kv, int) and kv * NT + t < 4):
                    sp.wait_ge(er_done, kv * NT + t - 3)
                    sp.sem_inc(freed, 1)
                sp.dma_start(rows[:, t % 4, :, :], rows_d[t % NT, bass.ds(turn * R, R), :].partition_broadcast(P)).then_inc(rows_in[t % 4], 16)

            for p in range(RING):
                load_w(0, p)
            for t in range(4):
                load_rows(0, t)
            with sp.Fori(0, KV - 1) as kv:
                for p in range(RING, NP + RING):
                    load_w(kv, p)
                for t in range(4, NT + 4):
                    load_rows(kv, t)
            for p in range(RING, NP):
                load_w(KV - 1, p)
            for t in range(4, NT):
                load_rows(KV - 1, t)

        @block.tensor
        def _(pe):
            pe.wait_ge(ones_made, 1)

            def job(kv, n):
                kind, h, b = jobs[n]
                if n >= PB:
                    m = n - PB
                    if m in ROPE:
                        pe.wait_ge(kept_v, kv * len(ROPE) + ROPE.index(m) + 1)
                    else:
                        pe.wait_ge(kept_s, kv * len(SIDE) + SIDE.index(m) + 1)
                p = n // B
                if b == 0:
                    pe.wait_ge(w_low, kv * NP + places[p] + 1)
                piece = [(wh[:, p % 2, c, :], wl[:, p % 2, c, :]) for c in range(KC)]
                product(pe, ps[:, n % PB, :], piece, xrows(core, b * T, T)).then_inc(jobs_done, 1)

            def turn(kv, last_turn):
                for n in range(2, NJ):
                    job(kv, n)
                    if n == 7:
                        pe.wait_ge(kept_v, kv * len(ROPE) + 2)
                        pe.wait_ge(added, kv * NT + 1)
                        for t in range(NT):
                            last = pe.transpose(ps[:, 6 + t // 4, (t % 4) * P:(t % 4 + 1) * P],
                                                kT[:, t * P:(t + 1) * P], core.ident[:, :])
                        last.then_inc(kt_done, 1)
                    if n == 11:
                        pe.wait_ge(ktm_done, kv + 1)
                        pe.wait_ge(kept_s, kv * len(SIDE) + 2)
                        for t in range(NT):
                            last = pe.transpose(ps[:, 6 + t // 4, (t % 4) * P:(t % 4 + 1) * P],
                                                vw[:, t // 4, (t % 4) * P:(t % 4 + 1) * P], core.ident[:, :])
                        last.then_inc(vt_done, 1)
                pe.wait_ge(kept_v, kv * len(ROPE) + len(ROPE))
                pe.wait_ge(kept_s, kv * len(SIDE) + len(SIDE))
                pe.wait_ge(v_done, kv + 1)
                pe.wait_ge(w_low, kv * NP + NP)

                def scores(t):
                    if t >= 2:
                        pe.wait_ge(sc_done, kv * NT + t - 1)
                    pe.matmul(ps[:, t % 2, :], kT[:, t * P:(t + 1) * P], tile(qT, t),
                              start=True, stop=True).then_inc(s_done, 1)

                def outputs(t):
                    pe.wait_ge(sc_done, kv * NT + t + 1)
                    if t >= 3:
                        pe.wait_ge(rn_done, kv * NT + t - 2)
                    out = ps[:, 2 + t % 3, :]
                    last = pe.matmul(out, v[:, t, :], a2[:, t % 2, :], start=True, stop=True)
                    if t % QT > 0:
                        pe.wait_ge(qg_done, kv * 2 * C1 + reads(t))
                        pe.wait_ge(st_done, kv * 2 * C1 + adds(t - 1))
                        for h in range(R):
                            last = pe.matmul(out[:, h * P:(h + 1) * P], state[:, h * P:(h + 1) * P],
                                             b2[:, t % 2, h * P:(h + 1) * P],
                                             start=False, stop=True, skip_group_check=True)
                    last.then_inc(y_done, 1)

                def adding(t):
                    pe.wait_ge(vw_done, kv * 2 * C1 + adds(t))
                    if adds(t) > 1:
                        pe.wait_ge(st_done, kv * 2 * C1 + adds(t) - 1)
                    pe.matmul(ps[:, 5, :], ktm[:, t, :], vw[:, t % 2, :], start=True, stop=True).then_inc(cs_done, 1)

                def squares(t):
                    pe.wait_ge(y2_done, kv * NT + t + 1)
                    if t >= 1:
                        pe.wait_ge(ln_done, kv * NT + t)
                    pe.matmul(ps[:, 6, :], ones[:, :], y2[:, t % 2, :], start=True, stop=True).then_inc(ms_done, 1)

                def project(t):
                    pe.wait_ge(ryl_done, kv * NT + t + 1)
                    if t >= 1:
                        pe.wait_ge(added, kv * NT + t + 1)
                    product(pe, ps[:, 7, :],
                            [(ryh[:, t % 2, h * P:(h + 1) * P], ryl[:, t % 2, h * P:(h + 1) * P]) for h in range(R)],
                            [(woh[:, h, :], wol[:, h, :]) for h in range(R)]).then_inc(wo_done, 1)

                scores(0)
                for t in range(NT + 2):
                    if t + 1 < NT:
                        scores(t + 1)
                    if t < NT:
                        outputs(t)
                    if t >= NT and not last_turn:
                        job(kv + 1, t - NT)
                    if 1 <= t <= NT:
                        squares(t - 1)
                    if t < NT and t % QT < C1:
                        adding(t)
                    if t >= 2:
                        project(t - 2)

            job(0, 0)
            job(0, 1)
            with pe.Fori(0, KV - 1) as kv:
                turn(kv, False)
            turn(KV - 1, True)

        @block.scalar
        def _(act):
            def high(kv, p):
                act.wait_ge(w_in[p % RING], kv * 32 + (p // RING) * 16 + 16)
                if p in wo_places:
                    out = woh[:, wo_places.index(p), :]
                else:
                    j = places.index(p)
                    if j >= 2:
                        act.wait_ge(jobs_done, kv * NJ + (j - 1) * B)
                    out = wh[:, j % 2, :, :].rearrange("p c n -> p (c n)")
                act.activation(out, w[:, p % RING, :], ACT.Copy).then_inc(w_high, 1)

            def turn(kv, last_turn):
                def decay(t):
                    act.wait_ge(raw_done, kv * NT + t + 1)
                    act.activation(c2[:, t % 2, :], c2[:, t % 2, :], ACT.Exp).then_inc(dec_done, 1)
                    if t >= 3:
                        act.wait_ge(y_done, kv * NT + t - 2)
                        act.wait_ge(st_done, kv * 2 * C1 + adds(t - 3))
                    act.activation(er[:, t % 3, :, :], rows[:, t % 4, :, :], ACT.Exp).then_inc(er_done, 1)

                for n, (kind, h, b) in enumerate(jobs):
                    if n == 17:
                        decay(0)
                        decay(1)
                    if kind == "v":
                        act.wait_ge(jobs_done, kv * NJ + n + 1)
                        act.activation(vw[:, b, :], ps[:, n % PB, :], ACT.Copy).then_inc(kept_s, 1)
                    if kind == "g":
                        act.wait_ge(jobs_done, kv * NJ + n + 1)
                        m = h * B + b
                        if m >= 2:
                            act.wait_ge(gate_done, kv * (R * B) + m - 1)
                        act.activation(y2[:, b, :], ps[:, n % PB, :], ACT.Tanh, scale=0.5)
                        act.activation(silu[:, h, b * T:(b + 1) * T], ps[:, n % PB, :], ACT.Copy,
                                       scale=0.5).then_inc(kept_s, 1)
                    if n % B == 1 and n // B + 2 < len(pieces):
                        for p in range(places[n // B + 1] + 1, places[n // B + 2] + 1):
                            high(kv, p)

                for t in range(NT + 1):
                    if t < NT:
                        act.wait_ge(y_done, kv * NT + t + 1)
                        act.activation(y2[:, t % 2, :], ps[:, 2 + t % 3, :], ACT.Square).then_inc(y2_done, 1)
                    if t >= 1:
                        u = t - 1
                        act.wait_ge(ms_done, kv * NT + u + 1)
                        act.activation(rinv[:, u % 2, :], ps[:, 6, :], ACT.Ln, bias=eps[:, 0:1],
                                       scale=1.0 / P).then_inc(ln_done, 1)
                        act.wait_ge(ln_done, kv * NT + u + 1)
                        act.activation(rinv[:, u % 2, :], rinv[:, u % 2, :], ACT.Exp, scale=-0.5).then_inc(rinv_done, 1)
                    if t + 2 < NT:
                        decay(t + 2)
                    if t in (3, 4) and not last_turn:
                        high(kv + 1, t - 3)
                    if t >= 1:
                        act.wait_ge(rn_done, kv * NT + u + 1)
                        if u >= 2:
                            act.wait_ge(wo_done, kv * NT + u - 1)
                        act.activation(ryh[:, u % 2, :], rn[:, :], ACT.Copy).then_inc(ryh_done, 1)

            high(0, 0)
            high(0, 1)
            with act.Fori(0, KV - 1) as kv:
                turn(kv, False)
            turn(KV - 1, True)

        @block.gpsimd
        def _(pool):
            pool.memset(eps[:, :], EPS).then_inc(cleared, 1)
            pool.memset(mixed[:, :, :], 0.0).then_inc(cleared, 1)

            def low(kv, p):
                pool.wait_ge(w_high, kv * NP + p + 1)
                if p in wo_places:
                    out, hi = (a[:, wo_places.index(p), :] for a in (wol, woh))
                else:
                    out, hi = (a[:, places.index(p) % 2, :, :].rearrange("p c n -> p (c n)") for a in (wl, wh))
                pool.tensor_tensor(out, w[:, p % RING, :], f32(hi), ALU.subtract).then_inc(w_low, 1)

            def turn(kv, last_turn):
                for p in range(2, NP):
                    low(kv, p)
                pool.wait_ge(kept_v, kv * len(ROPE) + len(ROPE))
                pool.wait_ge(kept_s, kv * len(SIDE) + len(SIDE))
                pool.wait_ge(v_done, kv + 1)
                for t in range(NT):
                    if t % QT > 0:
                        pool.wait_ge(er_done, kv * NT + t + 1)
                        if reads(t) > 2:
                            pool.wait_ge(y_done, kv * NT + t - 1)
                        pool.tensor_tensor(heads(b2[:, t % 2, :]), tile(qT, t), er[:, t % 3, :, :],
                                           ALU.mult).then_inc(qg_done, 1)
                    if t % QT < C1:
                        if adds(t) > 2:
                            pool.wait_ge(cs_done, kv * 2 * C1 + adds(t) - (1 if t % QT == 0 else 2))
                        pool.tensor_tensor(heads(vw[:, t % 2, :]), v[:, t, :].unsqueeze(1).broadcast_to([P, R, P]),
                                           wsts[:, t, :].unsqueeze(2).broadcast_to([P, R, P]),
                                           ALU.mult).then_inc(vw_done, 1)
                    if t in (3, 4) and not last_turn:
                        low(kv + 1, t - 3)

            low(0, 0)
            low(0, 1)
            with pool.Fori(0, KV - 1) as kv:
                turn(kv, False)
            turn(KV - 1, True)

        @block.vector
        def _(dve):
            dve.sem_inc(added, 1)
            dve.memset(ones[:, :], 1.0).then_inc(ones_made, 1)
            dve.wait_ge(consts_in, 64)
            dve.wait_ge(cleared, 2)
            with dve.Fori(0, KV) as kv:
                NSTEP = 1 + len(ROPE) + NT
                count = [0]

                def link(ins_):
                    count[0] += 1
                    ins_.then_inc(dstep, 1)
                    dve.wait_ge(dstep, kv * NSTEP + count[0])

                dve.tensor_copy(lws[:, :, :], lw[:, :, bass.ds(kv * R, R)])
                link(dve.tensor_copy(wsts[:, :, :], wst[:, :, bass.ds(kv * R, R)]))
                def exponents(t):
                    dve.wait_ge(rows_in[t % 4], kv * 32 + (t // 4) * 16 + 16)
                    if t >= 2:
                        dve.wait_ge(sc_done, kv * NT + t - 1)
                    for h in range(R):
                        last = dve.scalar_tensor_tensor(
                            out=c2[:, t % 2, h * P:(h + 1) * P], in0=rows[:, t % 4, h, :],
                            scalar=lws[:, t, h:h + 1], in1=limit[:, :], op0=ALU.subtract, op1=ALU.min)
                    last.then_inc(raw_done, 1)

                for n, (kind, h, b) in enumerate(jobs):
                    if n == 15:
                        exponents(0)
                        exponents(1)
                    if kind in "kq":
                        dve.wait_ge(jobs_done, kv * NJ + n + 1)
                        out = kT[:, b * T:(b + 1) * T] if kind == "k" else qT[:, h, b * T:(b + 1) * T]
                        dve.tensor_tensor(a2[:, b, :], ps[:, n % PB, :], cos[:, :], ALU.mult)
                        dve.tensor_tensor(b2[0:64, b, :], ps[64:128, n % PB, :], sin[0:64, :], ALU.mult)
                        link(dve.tensor_tensor(b2[64:128, b, :], ps[0:64, n % PB, :], sin[64:128, :], ALU.mult))
                        dve.tensor_tensor(out, a2[:, b, :], b2[:, b, :], ALU.add).then_inc(kept_v, 1)
                    if kind == "g":
                        dve.wait_ge(kept_s, kv * len(SIDE) + SIDE.index(n) + 1)
                        dve.scalar_tensor_tensor(out=silu[:, h, b * T:(b + 1) * T], in0=y2[:, b, :], scalar=1.0,
                                                 in1=silu[:, h, b * T:(b + 1) * T], op0=ALU.add,
                                                 op1=ALU.mult).then_inc(gate_done, 1)
                    if n == 8:
                        dve.wait_ge(kt_done, kv + 1)
                        for half in range(2):
                            last = dve.tensor_copy(ktm[:, half * 4:(half + 1) * 4, :].rearrange("p i e -> p (i e)"),
                                                   ps[:, 6 + half, :])
                        last.then_inc(ktm_done, 1)
                    if n == 12:
                        dve.wait_ge(vt_done, kv + 1)
                        for half in range(2):
                            last = dve.tensor_copy(v[:, half * 4:(half + 1) * 4, :].rearrange("p i e -> p (i e)"),
                                                   ps[:, 6 + half, :])
                        last.then_inc(v_done, 1)
                dve.wait_ge(gate_done, kv * (R * B) + R * B)

                def decayed(t):
                    dve.wait_ge(s_done, kv * NT + t + 1)
                    dve.wait_ge(dec_done, kv * NT + t + 1)
                    dve.tensor_tensor(a2[:, t % 2, :], ps[:, t % 2, :], c2[:, t % 2, :], ALU.mult).then_inc(sc_done, 1)

                decayed(0)
                for t in range(NT + 3):
                    if t + 1 < NT:
                        decayed(t + 1)
                    if 2 <= t < NT + 2:
                        dve.wait_ge(ryh_done, kv * NT + t - 1)
                        dve.tensor_tensor(ryl[:, t % 2, :], rn[:, :], f32(ryh[:, t % 2, :]), ALU.subtract).then_inc(ryl_done, 1)
                    if t >= 3:
                        dve.wait_ge(wo_done, kv * NT + t - 2)
                        dve.tensor_tensor(mixed[:, t - 3, :], mixed[:, t - 3, :], ps[:, 7, :], ALU.add).then_inc(added, 1)
                    if t + 2 < NT:
                        exponents(t + 2)
                    if t < NT and t % QT < C1:
                        dve.wait_ge(cs_done, kv * 2 * C1 + adds(t))
                        if t % QT == 0:
                            last = dve.tensor_copy(state[:, :], ps[:, 5, :])
                        else:
                            dve.wait_ge(er_done, kv * NT + t + 1)
                            for h in range(R):
                                last = dve.scalar_tensor_tensor(
                                    out=state[:, h * P:(h + 1) * P], in0=state[:, h * P:(h + 1) * P],
                                    scalar=er[:, t % 3, h, P - 1:P], in1=ps[:, 5, h * P:(h + 1) * P],
                                    op0=ALU.mult, op1=ALU.add)
                        last.then_inc(st_done, 1)
                    if 1 <= t <= NT:
                        u = t - 1
                        dve.wait_ge(rinv_done, kv * NT + u + 1)
                        if u >= 1:
                            dve.wait_ge(ryl_done, kv * NT + u)
                        link(dve.scalar_tensor_tensor(out=rn[:, :], in0=ps[:, 2 + u % 3, :], scalar=gw[:, 0:1],
                                                      in1=rinv[:, u % 2, :], op0=ALU.mult, op1=ALU.mult))
                        dve.tensor_tensor(heads(rn[:, :]), heads(rn[:, :]), tile(silu, u), ALU.mult).then_inc(rn_done, 1)
                assert count[0] == NSTEP


def build(nc, ins, out):
    ctx = ExitStack()
    with ctx:
        core = Core(nc, ctx, ins)
        load_inputs(core)

        with Stage(core, "layer0") as layer:
            we, be = layer.sb("we", [P, 2, KC, D]), layer.sb("be", [P, 2, D])
            we_in = layer.sem("we_in0"), layer.sem("we_in1")

            def load_experts(sp):
                for e in range(2):
                    sp.dma_start(we[:, e, :, :], ins["l0_we"][e]).then_inc(we_in[e], 16)
                    sp.dma_start(be[:, e, :], ins["l0_be"][e].partition_broadcast(P)).then_inc(we_in[e], 16)

            with Stage(core, "mix0") as st:
                first = FirstWeights(core, st, "l0", shared_kv=True)
                layernorm(core, "ln0", first.load)
                oh, ol = st.sb("oh", [P, KC, N], F32R), st.sb("ol", [P, KC, N], F32R)
                wo_in = [st.sem(f"wo_in{g}") for g in range(KC)]
                attention(core, "l0", first, oh, ol, wo_in, G=4, E=16, scale=0.25, denominator=1.0, causal=True,
                          shared_kv=True, load_ahead=load_experts)
                project_out(core, "out0", oh, ol, wo_in, KC, P)
            experts(core, "ffn0", we, be, we_in)

        adapted = ctx.enter_context(nc.sbuf_tensor("adapted", [P, NT, 32], F32))
        with Stage(core, "mix1") as st:
            lw = st.sb("lw", [P, NT, 32])
            wst = st.sb("wst", [P, NT, 32])
            rows_d = nc.dram_tensor("decay_rows", [NT, 32, P], F32).ap()
            with Stage(core, "side1") as side:
                w, w_in = side.sb("w", [P, KC, P]), side.sem("w_in")

                def load_side(sp):
                    sp.dma_start(w[:, :, :], ins["l1_side"]).then_inc(w_in, 16)

                layernorm(core, "ln1", load_side)
                decays(core, "dec1", w, w_in, rows_d, lw, wst, adapted)
            retention(core, "ret1", rows_d, lw, wst)
        with Stage(core, "gate1") as st:
            zT = st.sb("zT", [P, N])
            dense_gate(core, "ffn1", ins["l1_wup"], zT, ins["l1_zw"], z=adapted)

        with Stage(core, "mix2") as st:
            first = FirstWeights(core, st, "l2")
            layernorm(core, "ln2", first.load)
            oh, ol = st.sb("oh", [P, KC, N], F32R), st.sb("ol", [P, KC, N], F32R)
            wo_in = [st.sem(f"wo_in{g}") for g in range(KC)]
            attention(core, "l2", first, oh, ol, wo_in, G=4, E=16, scale=0.25, denominator=1.0, causal=True, shared_kv=False,
                      qk_bias=ins["l2_qkb"], v_bias=ins["l2_vb"])
            project_out(core, "out2", oh, ol, wo_in, KC, P, ins["l2_bo"])
        with Stage(core, "gate2") as st:
            zT = st.sb("zT", [P, N])
            w, w_in = st.sb("w", [P, KC, D]), [st.sem(f"w_in{c}") for c in range(KC)]
            lora_by_batch(core, "byb2", zT, w, w_in)
            dense_gate(core, "ffn2", ins["l2_w"], zT, ins["l2_zw"], w=w, w_in=w_in)

        with Stage(core, "mix3") as st:
            first = FirstWeights(core, st, "l3")
            layernorm(core, "ln3", first.load)
            oh, ol = st.sb("oh", [P, 1, N], F32R), st.sb("ol", [P, 1, N], F32R)
            wo_in = [st.sem("wo_in")]
            attention(core, "l3", first, oh, ol, wo_in, G=1, E=8, scale=1.0, denominator=8.0, causal=False, shared_kv=False,
                      qk_bias=ins["l3_qkb"], v_bias=ins["l3_vb"])
            project_out(core, "out3", oh, ol, wo_in, 1, 64, ins["l3_bo"])
        signed_gate(core, "ffn3", ins["l3_k"], ins["ei"], ins["l3_scale"], out)


def signed_gate(core, name, k_d, ei_d, scale_d, out_d):
    ps = core.ps
    with Stage(core, name) as st:
        k8 = st.sb("k8", [P, KC, D], mybir.dt.uint8)
        ei = st.sb("ei", [P, KC])
        w = st.sb("w", [P, KC, D], F32R)
        sc = st.sb("sc", [P, 1])
        f = st.sb("f", [P, 2, D])
        th = st.sb("th", [P, 2, D])
        gated = st.sb("gated", [P, D])
        loaded, made, done, f_done, tanh_done, x_done, step, stored = (
            st.sem("loaded"), st.sem("made"), st.sem("done"), st.sem("f_done"), st.sem("tanh_done"),
            st.sem("x_done"), st.sem("step"), st.sem("stored"))
        block = st.block()

        @block.sync
        def _(sp):
            sp.dma_start(k8[:, :, :], k_d).then_inc(loaded, 16)
            sp.dma_start(ei[:, :], ei_d).then_inc(loaded, 16)
            sp.dma_start(sc[:, :], scale_d.partition_broadcast(P)).then_inc(loaded, 16)
            for t in range(NT):
                sp.wait_ge(x_done, t + 1)
                sp.dma_start(out_d[t * P:(t + 1) * P, :], core.x[:, t, :]).then_inc(stored, 16)
            sp.wait_ge(stored, 16 * NT)

        @block.tensor
        def _(pe):
            pe.wait_ge(made, KC)
            for t in range(NT):
                for c in range(KC):
                    pe.matmul(ps[:, t, :], core.xh[:, c, t * P:(t + 1) * P], w[:, c, :], start=(c == 0), stop=False)
                    last = pe.matmul(ps[:, t, :], core.xl[:, c, t * P:(t + 1) * P], w[:, c, :],
                                     start=False, stop=(c == KC - 1))
                last.then_inc(done, 1)

        @block.scalar
        def _(act):
            act.wait_ge(loaded, 48)
            for t in range(NT):
                act.wait_ge(done, t + 1)
                if t >= 2:
                    act.wait_ge(x_done, t - 1)
                act.activation(f[:, t % 2, :], ps[:, t, :], ACT.Copy, scale=sc[:, 0:1]).then_inc(f_done, 1)
                act.wait_ge(f_done, t + 1)
                act.activation(th[:, t % 2, :], f[:, t % 2, :], ACT.Tanh, scale=0.5).then_inc(tanh_done, 1)

        @block.vector
        def _(dve):
            chain = Chain(dve, step)
            dve.wait_ge(loaded, 48)
            for c in range(KC):
                dve.tensor_scalar(w[:, c, :], k8[:, c, :], ei[:, c:c + 1], None, ALU.mult).then_inc(made, 1)
            for t in range(NT):
                dve.wait_ge(tanh_done, t + 1)
                gate_steps(core, dve, t, f[:, t % 2, :], th[:, t % 2, :], gated[:, :], chain, x_done)
                dve.wait_ge(x_done, t + 1)


def laid_out(inputs):
    import numpy as np

    a = {k: np.asarray(v) for k, v in inputs.items()}
    f32 = np.float32

    def chunks(w):
        return np.ascontiguousarray(w.reshape(-1, P, w.shape[1]).transpose(1, 0, 2))

    def groups(w, n):
        k, m = w.shape
        return np.ascontiguousarray(w.reshape(k // P, P, m // n, n).transpose(2, 1, 0, 3))

    d = {"x": a["L0_attn_x"].reshape(N, D)}
    d["l0_wqkv"] = groups(a["L0_attn_wq"], P)[:, :, None]
    d["l0_wkv"] = chunks(np.concatenate([a["L0_attn_wk"], a["L0_attn_wk"], a["L0_attn_wv"], a["L0_ffn_W_gate"],
                                         np.zeros((D, P - 56), f32)], 1))
    d["l0_wo"] = chunks(a["L0_attn_wo"])
    d["l0_bgate"] = a["L0_ffn_b_gate"]
    d["l0_we"] = np.ascontiguousarray(a["L0_ffn_W_e"].reshape(8, KC, P, D).transpose(0, 2, 1, 3))
    d["l0_be"] = a["L0_ffn_b_e"]
    wq, wg = (groups(a["L1_attn_" + k].T, P).reshape(8, 4, P, D) for k in ("Wq", "Wg"))
    wk, wv = (groups(a["L1_attn_" + k].T, P).reshape(8, 1, P, D) for k in ("Wk", "Wv"))
    wo = a["L1_attn_Wo"].T.reshape(8, 4, P, D)
    d["l1_w"] = np.stack([wk[:, 0], wv[:, 0]] + [m for h in range(3) for m in (wq[:, h], wg[:, h], wo[:, h])]
                         + [wo[:, 3], wq[:, 3], wg[:, 3]], 1)
    d["l1_side"] = chunks(np.concatenate([a["L1_attn_Win"], a["L1_ffn_gate_w"], a["L1_ffn_lora_A"].reshape(32, D),
                                          np.zeros((P - 68, D), f32)], 0).T)
    d["l1_dtb"] = a["L1_attn_dt_bias"]
    d["l1_ab"] = a["L1_attn_A_log_bias"]
    d["l1_gw"] = a["L1_attn_gnorm_w"].reshape(P, 1)
    d["l1_wup"] = chunks(a["L1_ffn_W_up"].T)
    d["l1_bz"] = a["L1_ffn_expert_bias"]
    d["l1_zw"] = np.concatenate([a["L1_ffn_lora_B"].transpose(0, 2, 1).reshape(32, D), np.zeros((P - 32, D), f32)], 0)
    d["l2_wqkv"] = np.stack([groups(a["L2_attn_" + k].T, P) for k in ("Wq", "Wk", "Wv")], 2)
    d["l2_qkb"] = np.ascontiguousarray(np.stack([a["L2_attn_bq"].reshape(4, P), a["L2_attn_bk"].reshape(4, P)], 2))
    d["l2_vb"] = a["L2_attn_bv"].reshape(4, P)
    d["l2_wo"] = chunks(a["L2_attn_Wo"].T)
    d["l2_bo"] = a["L2_attn_bo"]
    d["l2_w"] = chunks(a["L2_ffn_weight"].T)
    d["l2_wz"] = chunks(np.concatenate([a["L2_ffn_lora_A"].reshape(48, D), np.zeros((P - 48, D), f32)], 0).T)
    d["l2_zw"] = np.concatenate([a["L2_ffn_lora_B"].transpose(0, 2, 1).reshape(48, D), a["L2_ffn_bias"][None],
                                 np.zeros((P - 49, D), f32)], 0)
    d["l2_starts"] = a["L2_ffn_lora_start_indices"]
    qk = a["L3_attn_Wqk_w"].reshape(64, 2, D)
    qkb = a["L3_attn_Wqk_b"].reshape(64, 2)
    pad = np.zeros((64, D), f32)
    d["l3_wqkv"] = np.stack([groups(np.concatenate([m, pad], 0).T, P)
                             for m in (qk[:, 0], qk[:, 1], a["L3_attn_Wv_w"])], 2)
    d["l3_qkb"] = np.concatenate([qkb, np.zeros((64, 2), f32)], 0)[None]
    d["l3_vb"] = a["L3_attn_Wv_b"].reshape(1, 64)
    d["l3_wo"] = np.ascontiguousarray(a["L3_attn_Wo_w"].T).reshape(64, 1, D)
    d["l3_bo"] = a["L3_attn_Wo_b"]
    d["l3_k"] = np.ascontiguousarray(a["L3_ffn_kernel"].reshape(KC, P, D).transpose(1, 0, 2))
    d["l3_scale"] = a["L3_ffn_scale"].reshape(1)
    i, j = np.arange(P)[:, None], np.arange(P)[None, :]
    d["ident"] = np.eye(P, dtype=f32)
    d["mask"] = np.where(j > i, NEG, 0).astype(f32)
    d["cutoff"] = np.where(i > j, 0, 3e38).astype(f32)
    for E in (16, 8):
        spread = np.zeros((P, 4, 4, P), f32)
        for matrix, places in enumerate([(0, 2), (1,), (0, 1), (2,)]):
            for p in range(4):
                for h in range(2):
                    for place in places:
                        row = np.arange(E)
                        spread[(2 * p + h) * E + row, matrix, p, 64 * h + 16 * place + row] = 1
        d[f"spread{E}"] = spread.reshape(P, 2, 8 * P)
    halves = np.zeros((P, 2, 2), f32)
    for h in range(2):
        halves[64 * h:64 * h + 64, h, 0] = 1
        halves[64 * h + 48, h, 1] = -1
    d["halves"] = halves
    d["tri"] = (i <= j).astype(f32)
    d["limit"] = np.where(j >= i, 80.0, NEG).astype(f32)
    d["iota8"] = np.arange(8, dtype=f32)
    d["adapter_of_row"] = np.stack([np.arange(P) // 16, np.arange(P) == 48], 1).astype(f32)
    inv = 1.0 / 10000.0 ** (np.arange(0, P, 2, dtype=f32) / f32(P))
    ang = np.arange(T, dtype=f32)[None, :] * inv.astype(f32)[:, None]
    d["cos"] = np.concatenate([np.cos(ang), np.cos(ang)], 0).astype(f32)
    d["sin"] = np.concatenate([-np.sin(ang), np.sin(ang)], 0).astype(f32)
    ex = round(D * 0.8)
    d["ei"] = np.where(np.arange(D) < ex, 1.0, -0.8 / (1.0 - 0.8)).astype(f32).reshape(KC, P).T.copy()
    return d


def kernel(**inputs):
    import numpy as np
    import concourse.bacc as bacc
    from concourse.bass_utils import run_bass_kernel_spmd

    nc = bacc.Bacc("TRN2", target_bir_lowering=False, num_devices=1)
    arrays, ins = {}, {}
    for name, array in laid_out(inputs).items():
        arrays[f"in_{name}"] = array = np.ascontiguousarray(array)
        ins[name] = nc.dram_tensor(f"in_{name}", array.shape, mybir.dt.from_np(array.dtype), kind="ExternalInput").ap()
    out = nc.dram_tensor("out_x", (N, D), F32, kind="ExternalOutput").ap()
    build(nc, ins, out)
    result = run_bass_kernel_spmd(nc, [arrays], core_ids=[0])
    return result.results[0]["out_x"].reshape(B, T, D)
```
